# Optimizing a Trainium2 kernel written in Bass

```python
import numpy as np
import jax
import jax.numpy as jnp

def _softmax(x, axis=-1):
    return jax.nn.softmax(x, axis=axis)

def _gelu(x):
    return jax.nn.gelu(x, approximate=True)

def _silu(x):
    return jax.nn.silu(x)

def _sigmoid(x):
    return jax.nn.sigmoid(x)

def _layernorm(x, axis=-1, eps=1e-05):
    m = jnp.mean(x, axis=axis, keepdims=True)
    v = jnp.var(x, axis=axis, keepdims=True)
    return (x - m) / jnp.sqrt(v + eps)

def _scatter_add(tgt, idx, src, axis=0):
    return tgt.at[idx].add(src)

def _segment_sum(src, seg, n):
    return jax.ops.segment_sum(src, seg, n)
kernel_name = 'mk_adj_ffn_d1_adj_r2_e09bed'

def setup_inputs(seed: int=0):
    np.random.seed(seed)
    _w = jnp.asarray

    def _rec_inputs():
        import jax
        import jax.numpy as jnp
        _gk = jax.random.key(seed)
        x = -0.0002928 + 1 * jax.random.normal(jax.random.fold_in(_gk, 1), (128, 128, 256), jnp.float32)
        _a = jax.random.bernoulli(jax.random.fold_in(_gk, 2), 0.0625, (128, 128))
        _a = jnp.logical_or(_a, jnp.swapaxes(_a, -1, -2))
        _a = jnp.logical_or(_a, jnp.eye(128, dtype=bool))
        _af = _a.astype(jnp.float32)
        adj = _af
        return (x, adj)
    x, adj = _rec_inputs()

    def _L0_gnn_setup():
        import jax, jax.numpy as jnp
        import numpy as np
        B, N, D, H = (4, 1024, 256, 8)
        HD = D // H
        key = jax.random.key(seed)
        ks = jax.random.split(key, 10)
        x = jax.random.normal(ks[0], (B, N, D), dtype=jnp.float32)
        adj = (jax.random.uniform(ks[1], (N, N)) < 0.1).astype(jnp.float32)
        s = 1.0 / np.sqrt(D)
        Wq = jax.random.normal(ks[2], (D, D), dtype=jnp.float32) * s
        Wk = jax.random.normal(ks[3], (D, D), dtype=jnp.float32) * s
        Wv = jax.random.normal(ks[4], (D, D), dtype=jnp.float32) * s
        Wo = jax.random.normal(ks[5], (D, D), dtype=jnp.float32) * s
        bq = jnp.zeros((D,), jnp.float32)
        bk = jnp.zeros((D,), jnp.float32)
        bv = jnp.zeros((D,), jnp.float32)
        bo = jnp.zeros((D,), jnp.float32)
        return {'x': x, 'adj': adj, 'Wq': Wq, 'bq': bq, 'Wk': Wk, 'bk': bk, 'Wv': Wv, 'bv': bv, 'Wo': Wo, 'bo': bo}
    _L0_gnn_all = _L0_gnn_setup()
    _L0_gnn_in = {k: v for k, v in _L0_gnn_all.items() if k in ('Wq', 'bq', 'Wk', 'bk', 'Wv', 'bv', 'Wo', 'bo')}
    del _L0_gnn_all

    def _L0_ffn_setup():
        import jax, jax.numpy as jnp
        import numpy as np
        NUM_EXPERTS = 8
        TOP_K = 2
        key = jax.random.key(seed)
        ks = jax.random.split(key, 5)
        B, N, E, H, X = (8, 1024, 256, 384, NUM_EXPERTS)
        s_in = 0.02
        return {'x': jax.random.normal(ks[0], (B, N, E), dtype=jnp.float32), 'Wg': jax.random.normal(ks[1], (E, X), dtype=jnp.float32) * s_in, 'bg': jnp.zeros((X,), dtype=jnp.float32), 'W1': jax.random.normal(ks[2], (X, E, H), dtype=jnp.float32) * (1.0 / np.sqrt(E)), 'b1': jnp.zeros((X, H), dtype=jnp.float32), 'W2': jax.random.normal(ks[3], (X, H, E), dtype=jnp.float32) * (1.0 / np.sqrt(H)), 'b2': jnp.zeros((X, E), dtype=jnp.float32)}
    _L0_ffn_all = _L0_ffn_setup()
    _L0_ffn_in = {k: v for k, v in _L0_ffn_all.items() if k in ('Wg', 'bg', 'W1', 'b1', 'W2', 'b2')}
    del _L0_ffn_all
    return {'x': x, 'adj': adj, 'L0_gnn_Wq': _L0_gnn_in['Wq'], 'L0_gnn_bq': _L0_gnn_in['bq'], 'L0_gnn_Wk': _L0_gnn_in['Wk'], 'L0_gnn_bk': _L0_gnn_in['bk'], 'L0_gnn_Wv': _L0_gnn_in['Wv'], 'L0_gnn_bv': _L0_gnn_in['bv'], 'L0_gnn_Wo': _L0_gnn_in['Wo'], 'L0_gnn_bo': _L0_gnn_in['bo'], 'L0_ffn_Wg': _L0_ffn_in['Wg'], 'L0_ffn_bg': _L0_ffn_in['bg'], 'L0_ffn_W1': _L0_ffn_in['W1'], 'L0_ffn_b1': _L0_ffn_in['b1'], 'L0_ffn_W2': _L0_ffn_in['W2'], 'L0_ffn_b2': _L0_ffn_in['b2']}

def reference(x, adj, L0_gnn_Wq, L0_gnn_bq, L0_gnn_Wk, L0_gnn_bk, L0_gnn_Wv, L0_gnn_bv, L0_gnn_Wo, L0_gnn_bo, L0_ffn_Wg, L0_ffn_bg, L0_ffn_W1, L0_ffn_b1, L0_ffn_W2, L0_ffn_b2):
    import jax
    import jax.numpy as jnp

    def _L0_gnn_ref(x, adj, Wq, bq, Wk, bk, Wv, bv, Wo, bo):
        import jax, jax.numpy as jnp
        import numpy as np
        B, N, D, H = (4, 1024, 256, 8)
        HD = D // H
        b, n, d = x.shape
        q = (x @ Wq + bq).reshape(b, n, H, HD)
        k = (x @ Wk + bk).reshape(b, n, H, HD)
        v = (x @ Wv + bv).reshape(b, n, H, HD)
        scores = jnp.einsum('bqhd,bkhd->bhqk', q, k) / jnp.sqrt(jnp.float32(HD))
        scores = scores + (1.0 - adj)[None, None, :, :] * -1000000000.0
        attn = jax.nn.softmax(scores, axis=-1)
        out = jnp.einsum('bhqk,bkhd->bqhd', attn, v).reshape(b, n, d)
        return out @ Wo + bo

    def _L0_ffn_ref(x, Wg, bg, W1, b1, W2, b2):
        import jax, jax.numpy as jnp
        import numpy as np
        NUM_EXPERTS = 8
        TOP_K = 2
        scores = jnp.einsum('bne,ex->bnx', x, Wg) + bg
        topk_vals, topk_idx = jax.lax.top_k(scores, TOP_K)
        gates = jax.nn.softmax(topk_vals, axis=-1)
        h = jnp.einsum('bne,xeh->bnxh', x, W1) + b1
        h = jax.nn.gelu(h, approximate=False)
        expert_out = jnp.einsum('bnxh,xhe->bnxe', h, W2) + b2
        onehot = jax.nn.one_hot(topk_idx, NUM_EXPERTS, dtype=x.dtype)
        combine = jnp.einsum('bnk,bnkx->bnx', gates, onehot)
        out = jnp.einsum('bnx,bnxe->bne', combine, expert_out)
        return out
    x = x + _L0_gnn_ref(_layernorm(x, axis=-1), adj, L0_gnn_Wq, L0_gnn_bq, L0_gnn_Wk, L0_gnn_bk, L0_gnn_Wv, L0_gnn_bv, L0_gnn_Wo, L0_gnn_bo)
    x = x + _L0_ffn_ref(_layernorm(x, axis=-1), L0_ffn_Wg, L0_ffn_bg, L0_ffn_W1, L0_ffn_b1, L0_ffn_W2, L0_ffn_b2)
    return x

_drawn_inputs = setup_inputs


def setup_inputs(seed=0):
    import zlib

    import numpy as np

    out = dict(_drawn_inputs(seed))
    spreads = {'L0_gnn_bq': (0.0, 0.1),
     'L0_gnn_bk': (0.0, 0.1),
     'L0_gnn_bv': (0.0, 0.1),
     'L0_gnn_bo': (0.0, 0.1),
     'L0_ffn_bg': (0.0, 0.1),
     'L0_ffn_b1': (0.0, 0.1),
     'L0_ffn_b2': (0.0, 0.1)}
    factors = {}
    for name, (base, spread) in spreads.items():
        noise = np.random.default_rng([zlib.crc32(name.encode()), seed]).standard_normal(out[name].shape)
        drawn = base * np.exp(spread * noise) if base else spread * noise
        out[name] = jnp.asarray(drawn.astype(out[name].dtype))
    for name, factor in factors.items():
        out[name] = (out[name] * factor).astype(out[name].dtype)
    return out
```

```python
from contextlib import ExitStack

import concourse.bass as bass
from concourse import mybir

F32 = mybir.dt.float32
F32R = mybir.dt.float32r
BF16 = mybir.dt.bfloat16
I32 = mybir.dt.int32
U32 = mybir.dt.uint32
ALU = mybir.AluOpType
ACT = mybir.ActivationFunctionType
AX = mybir.AxisListType

P = 128
HEADS = 8
HEAD_DIM = 32
TOP_K = 2
EPS = 1e-5
MASKED = -1000000000.0
RSQRT_MAGIC = float(0x5F3759DF)
PASSES = ((0, 0), (1, 0), (0, 1))
HIGH, LOW = 0, 1


def build(nc, x, adj, Wq, bq, Wk, bk, Wv, bv, Wo, bo, Wg, bg, W1, b1, W2, b2, out, x1_dram, rows_dram, expert_dram):
    GRAPHS, N, D = x.shape
    EXPERTS, _, HID = W1.shape
    TOKENS = GRAPHS * N
    KB = D // P
    HB = HID // P
    RG = P // HEAD_DIM
    HH = HEADS // RG
    CAP = TOKENS + P
    TILES = TOKENS * TOP_K // P + EXPERTS
    assert N == P and KB == 2 and HH == 2

    x_rows = x.rearrange("g n d -> (g n) d")
    out_rows = out.rearrange("g n d -> (g n) d")

    ctx = ExitStack()
    with ctx:
        def keep(name, shape, dt):
            return ctx.enter_context(nc.sbuf_tensor(name, shape, dt))

        w1 = keep("w1", [P, 2, EXPERTS, KB * HID], F32R)
        w2 = keep("w2", [P, 2, EXPERTS, HB * D], F32R)
        ident = keep("ident", [P, P], F32)
        slots = keep("slots", [P, TOP_K, GRAPHS], F32)
        outputs_at = keep("outputs_at", [P, TOP_K, GRAPHS], I32)
        top_scores = keep("top_scores", [P, TOP_K, GRAPHS], F32)
        counts = keep("counts", [P, EXPERTS], F32)
        count_rows = keep("count_rows", [P, EXPERTS], F32)

        setup_weights(nc, W1, W2, w1, w2, ident, EXPERTS, D, HID)
        attention(nc, x_rows, adj, Wq, bq, Wk, bk, Wv, bv, Wo, bo, Wg, bg, ident, slots, top_scores,
                  counts, count_rows, x1_dram, rows_dram, GRAPHS, D, EXPERTS, CAP)
        experts(nc, b1, b2, w1, w2, ident, counts, count_rows, slots, outputs_at, rows_dram, expert_dram, EXPERTS, D, HID, CAP,
                TILES, TOKENS * TOP_K // P)
        combine(nc, outputs_at, top_scores, x1_dram, expert_dram, out_rows, GRAPHS, D)


def setup_weights(nc, W1, W2, w1, w2, ident, EXPERTS, D, HID):
    KB, HB = D // P, HID // P
    with ExitStack() as ctx:
        RING = 4
        raw = ctx.enter_context(nc.sbuf_tensor("raw", [P, RING, KB * HID], F32))
        loaded = [ctx.enter_context(nc.semaphore(f"w_loaded{k}")) for k in range(RING)]
        split_high = ctx.enter_context(nc.semaphore("w_split_high"))
        split_low = ctx.enter_context(nc.semaphore("w_split_low"))
        ident_zero = ctx.enter_context(nc.semaphore("ident_zero"))
        ident_done = ctx.enter_context(nc.semaphore("ident_done"))
        block = ctx.enter_context(nc.Block())
        pieces = [(W1[e].rearrange("(k p) h -> p k h", p=P), w1, KB, e) for e in range(EXPERTS)]
        pieces += [(W2[e].rearrange("(k p) d -> p k d", p=P), w2, HB, e) for e in range(EXPERTS)]

        @block.sync
        def _(sp):
            for n, (src, _, blocks, _) in enumerate(pieces):
                if n >= RING:
                    sp.wait_ge(split_low, n - RING + 1)
                sp.dma_start(raw[:, n % RING, :].rearrange("p (k h) -> p k h", k=blocks), src).then_inc(
                    loaded[n % RING], 16)

        @block.scalar
        def _(act):
            for n, (_, dst, _, e) in enumerate(pieces):
                act.wait_ge(loaded[n % RING], 16 * (n // RING + 1))
                act.activation(dst[:, HIGH, e, :], raw[:, n % RING, :], ACT.Copy).then_inc(split_high, 1)

        @block.vector
        def _(dve):
            for n, (_, dst, _, e) in enumerate(pieces):
                dve.wait_ge(split_high, n + 1)
                dve.tensor_tensor(dst[:, LOW, e, :], raw[:, n % RING, :], dst[:, HIGH, e, :],
                                  ALU.subtract).then_inc(split_low, 1)

        @block.gpsimd
        def _(pool):
            pool.memset(ident[:], 0.0).then_inc(ident_zero, 1)
            pool.wait_ge(ident_zero, 1)
            pool.affine_select(out=ident[:], in_=ident[:], compare_op=ALU.not_equal, fill=1.0, base=0,
                               pattern=[[-1, P]], channel_multiplier=1).then_inc(ident_done, 1)


def attention(nc, x_rows, adj, Wq, bq, Wk, bk, Wv, bv, Wo, bo, Wg, bg, ident, slots, top_scores,
              counts, count_rows, x1_dram, rows_dram, GRAPHS, D, EXPERTS, CAP):
    KB, RG, HH = D // P, P // HEAD_DIM, HEADS * HEAD_DIM // P
    VW = HEAD_DIM + 1
    SCALE = float(HEAD_DIM) ** -0.5
    UNROLL = 8
    CONSTS = 4 + 1 + 1 + 2 * KB + 3
    L_STATS, L_NEWTON, L_NORM, L_XT, L_QK, L_V = 4, 6, 7, 8, 10, 11
    L_S, L_PT, L_PV, L_OT, L_X1 = 13, 14, 15, 16, 17
    L_NEWTON2, L_NORM2, L_GT, L_TOP, L_RANK, L_SLOT = 20, 21, 22, 23, 24, 24
    L_LAST = L_SLOT + 1
    HEAD_STEPS = -(-L_LAST // UNROLL) * UNROLL
    assert GRAPHS % UNROLL == 0

    with ExitStack() as ctx:
        def sb(name, shape, dt=F32):
            return ctx.enter_context(nc.sbuf_tensor(name, shape, dt))

        def pb(name, shape):
            return ctx.enter_context(nc.psum_tensor(name, shape, F32))

        def sem(name):
            return ctx.enter_context(nc.semaphore(name))

        raw = sb("attn_raw", [P, 4, KB * D])
        wall = sb("attn_w", [P, 2, 4, KB, D], F32R)
        wg = sb("wg", [P, KB, EXPERTS])
        bqk = sb("bqk", [P, 2, KB])
        bv_all = sb("bv_all", [P, D])
        bo_all = sb("bo_all", [P, D])
        bg_all = sb("bg_all", [P, EXPERTS])
        mask = sb("mask", [P, P])
        before = sb("before", [P, P], BF16)
        ones = sb("ones", [P, P], BF16)
        expert_id = sb("expert_id", [P, EXPERTS])
        xin = sb("xin", [P, 8, D])
        stats = sb("stats", [P, 4, 6])
        moments = sb("moments", [P, 2, 4, 2])
        rstd = sb("rstd", [P, 2, 4])
        newton = sb("newton", [P, 2, 2, 2])
        xn = sb("xn", [P, 2, D])
        xT = [sb(f"xT{h}", [P, 2, KB, 2 * P], F32R) for h in (HIGH, LOW)]
        qk = [sb(f"qk{h}", [P, 2, 2, KB, 2 * P], F32R) for h in (HIGH, LOW)]
        v1 = sb("v1", [P, 4, HEADS, VW])
        scores = sb("scores", [P, 2, HEADS, P])
        row_max = sb("row_max", [P, 2, HEADS])
        neg_max = sb("neg_max", [P, 2, HEADS])
        probsT = sb("probsT", [P, HEADS, P])
        denom = sb("denom", [P, 2, HEADS])
        o = sb("o", [P, 2, D])
        oT = [sb(f"oT{h}", [P, 2, KB, P], F32R) for h in (HIGH, LOW)]
        xres = sb("xres", [P, 4, D])
        x1 = sb("x1", [P, 8, D])
        stats2 = sb("stats2", [P, 4, 6])
        xn2 = sb("xn2", [P, 8, D])
        gT = sb("gT", [P, 2, KB, P])
        logits = sb("logits", [P, 4, EXPERTS])
        top8 = sb("top8", [P, 4, 8])
        top8_at = sb("top8_at", [P, 4, 8], U32)
        top_at = sb("top_at", [P, 2, 2, TOP_K])
        chosen = sb("chosen", [P, 2, TOP_K, 2, EXPERTS])
        either = sb("either", [P, 2, 2, EXPERTS], BF16)
        place = sb("place", [P, 2, 2, EXPERTS])
        picked = sb("picked", [P, 2, TOP_K, 2, EXPERTS])
        slot_f = sb("slot_f", [P, 2, TOP_K, 2])
        slot_i = sb("slot_i", [P, 4, TOP_K, 2], I32)

        ps_s = pb("ps_s", [P, RG, 512])
        ps_qk = pb("ps_qk", [P, KB, 2 * P])
        ps_vo = pb("ps_vo", [P, 2, D])
        ps_t = pb("ps_t", [P, 512])[:, 0:KB * P]
        ps_o = pb("ps_o", [P, 512])
        o_ps = ps_o[:, 0:HEADS * VW].rearrange("p (h c) -> p h c", c=VW)
        gate_ps = ps_o[:, 272:272 + EXPERTS]
        rank_ps = ps_o[:, 304:304 + 2 * EXPERTS].rearrange("p (g e) -> p g e", e=EXPERTS)
        total_ps = ps_o[:, 336:336 + EXPERTS]

        x_loaded = [sem(f"x_loaded{k}") for k in range(8)]
        xres_loaded = [sem(f"xres_loaded{k}") for k in range(4)]
        x1_stored = [sem(f"x1_stored{k}") for k in range(8)]
        scattered = [sem(f"scattered{k}") for k in range(4)]
        const_loaded, zero_stored = sem("const_loaded"), sem("zero_stored")
        (const_high, const_low, const_ready, consts_pool, chain_pool, chain_dve, held, stats_done, moments_done, normed,
         xT_mm, xT_high, xT_low, qk_mm, qk_high, qk_low, v_mm, v_done, s_mm, max_done, neg_done, exp_done,
         pT_mm, pT_done, pv_mm, denom_done, o_done, oT_mm, oT_high, oT_low, proj_mm, xres_biased,
         x1_done, stats2_done, moments2_done, normed2, gT_mm, gT_done, gate_mm, logits_done, top_done,
         chosen_done, either_done, rank_mm, placed, chain_slot, slot_done, newton_step, newton_done) = (sem(n) for n in (
             "const_high const_low const_ready consts_pool chain_pool chain_dve held stats_done moments_done normed "
             "xT_mm xT_high xT_low qk_mm qk_high qk_low v_mm v_done s_mm max_done neg_done exp_done "
             "pT_mm pT_done pv_mm denom_done o_done oT_mm oT_high oT_low proj_mm xres_biased "
             "x1_done stats2_done moments2_done normed2 gT_mm gT_done gate_mm logits_done top_done "
             "chosen_done either_done rank_mm placed chain_slot slot_done newton_step newton_done").split())

        def hold(eng, semaphore, count):
            eng.wait_ge(semaphore, count)
            eng.sem_inc(held, 1)

        def run(eng, step):
            for t in range(HEAD_STEPS):
                step(t // UNROLL, t % UNROLL, lambda lag: t >= lag)
            with eng.Fori(HEAD_STEPS // UNROLL, GRAPHS // UNROLL) as base:
                for u in range(UNROLL):
                    step(base, u, lambda lag: True)
            for t in range(GRAPHS, GRAPHS + L_LAST):
                step(t // UNROLL, t % UNROLL, lambda lag: t - lag < GRAPHS)

        def graph(base, u, lag):
            return base * UNROLL + (u - lag)

        def turns(base, u, lag, ring):
            return base * (UNROLL // ring) + ((u - lag) // ring + 1)

        def pair_of(base, u, lag):
            return base * (UNROLL // 2) + (u - lag) // 2

        def newton_run(base, u, lag, newton_lag):
            first = (u - lag) // 2 * 2 + newton_lag
            return base * (UNROLL // 2) + ((first - L_NEWTON) // 2 + 1)

        def old(base, u, lag, back):
            return not isinstance(base, int) or graph(base, u, lag) >= back

        block = ctx.enter_context(nc.Block())

        @block.sync
        def _(sp):
            for k, w in enumerate((Wq, Wk, Wv, Wo)):
                sp.dma_start(raw[:, k, :].rearrange("p (k d) -> p k d", k=KB),
                             w.rearrange("(k p) d -> p k d", p=P)).then_inc(const_loaded, 16)
            sp.dma_start(mask[:], adj).then_inc(const_loaded, 16)
            sp.dma_start(wg[:], Wg.rearrange("(k p) e -> p k e", p=P)).then_inc(const_loaded, 16)
            for k, b in enumerate((bq, bk)):
                for blk in range(KB):
                    sp.dma_start(bqk[:, k, blk:blk + 1], b[blk * P:(blk + 1) * P].unsqueeze(1)).then_inc(
                        const_loaded, 16)
            for dst, b in ((bv_all, bv), (bo_all, bo), (bg_all, bg)):
                sp.dma_start(dst[:], b.partition_broadcast(P)).then_inc(const_loaded, 16)

            def step(base, u, live):
                if live(0):
                    i, k = graph(base, u, 0), u % 8
                    if old(base, u, 0, 8):
                        sp.wait_ge(normed, i - 7)
                    sp.dma_start(xin[:, k, :], x_rows[bass.ds(i * P, P), :]).then_inc(x_loaded[k], 16)
                if live(L_S):
                    i, k = graph(base, u, L_S), (u - L_S) % 4
                    if old(base, u, L_S, 4):
                        sp.wait_ge(x1_done, i - 3)
                    sp.dma_start(xres[:, k, :], x_rows[bass.ds(i * P, P), :]).then_inc(xres_loaded[k], 16)
                if live(L_X1 + 1):
                    i, k = graph(base, u, L_X1 + 1), (u - L_X1 - 1) % 8
                    sp.wait_ge(x1_done, i + 1)
                    sp.dma_start(x1_dram[bass.ds(i * P, P), :], x1[:, k, :]).then_inc(x1_stored[k], 16)

            run(sp, step)
            for k in range(8):
                sp.wait_ge(x1_stored[k], 16 * (GRAPHS // 8))

        @block.tensor
        def _(pe):
            def step(base, u, live):
                if live(L_S):
                    i, par, cols = graph(base, u, L_S), (u - L_S) // 2 % 2, (u - L_S) % 2 * P
                    pe.wait_ge(qk_low, i + (2 if (u - L_S) % 2 == 0 else 1))
                    if live(L_PT + 1) and old(base, u, L_PT + 1, 0):
                        pe.wait_ge(pT_done, graph(base, u, L_PT + 1) + 1)
                    if old(base, u, L_S, 1):
                        pe.wait_ge(max_done, i)
                    for hh in range(HH):
                        for n, (a, b) in enumerate(PASSES):
                            for r in range(RG):
                                rows = slice(r * HEAD_DIM, (r + 1) * HEAD_DIM)
                                mm = pe.matmul(ps_s[:, r, hh * P:(hh + 1) * P],
                                               qk[a][rows, par, 0, hh, cols:cols + P],
                                               qk[b][rows, par, 1, hh, cols:cols + P],
                                               start=n == 0, stop=n == len(PASSES) - 1)
                    mm.then_inc(s_mm, 1)
                if live(L_XT):
                    i = graph(base, u, L_XT)
                    pe.wait_ge(normed, i + 1)
                    if old(base, u, L_XT, 1):
                        pe.wait_ge(xT_low, i)
                    if live(L_OT + 1) and old(base, u, L_OT + 1, 0):
                        pe.wait_ge(oT_low, graph(base, u, L_OT + 1) + 1)
                    if live(L_GT + 1) and old(base, u, L_GT + 1, 0):
                        pe.wait_ge(gT_done, graph(base, u, L_GT + 1) + 1)
                    for kb in range(KB):
                        mm = pe.transpose(ps_t[:, kb * P:(kb + 1) * P], xn[:, (u - L_XT) % 2, kb * P:(kb + 1) * P],
                                          ident[:])
                    mm.then_inc(xT_mm, 1)
                if live(L_PV):
                    i = graph(base, u, L_PV)
                    pe.wait_ge(v_done, i + 1)
                    if old(base, u, L_PV, 1):
                        pe.wait_ge(o_done, i)
                    if live(L_TOP + 1):
                        pe.wait_ge(logits_done, graph(base, u, L_TOP + 1) + 1)
                    if live(L_RANK + 1) and (u - L_RANK - 1) % 2 == 1:
                        pe.wait_ge(placed, 2 * pair_of(base, u, L_RANK + 1) + 2)
                    pe.wait_ge(pT_done, i + 1)
                    for h in range(HEADS):
                        mm = pe.matmul(o_ps[:, h, :], probsT[:, h, :], v1[:, (u - L_PV) % 4, h, :],
                                       start=True, stop=True)
                    mm.then_inc(pv_mm, 1)
                if live(L_V):
                    i, par, cols = graph(base, u, L_V), (u - L_V) // 2 % 2, (u - L_V) % 2 * P
                    pe.wait_ge(xT_low, i + 1)
                    if old(base, u, L_V, 1):
                        pe.wait_ge(v_done, i)
                    if live(L_X1 + 1) and old(base, u, L_X1 + 1, 0):
                        pe.wait_ge(x1_done, graph(base, u, L_X1 + 1) + 1)
                    for n, (kb, (a, b)) in enumerate((kb, ab) for kb in range(KB) for ab in PASSES):
                        mm = pe.matmul(ps_vo[:, 0, :], xT[a][:, par, kb, cols:cols + P], wall[:, b, 2, kb, :],
                                       start=n == 0, stop=n == 3 * KB - 1)
                    mm.then_inc(v_mm, 1)
                if live(L_PT):
                    i, buf = graph(base, u, L_PT), (u - L_PT) % 2
                    pe.wait_ge(exp_done, i + 1)
                    if live(L_S):
                        pe.wait_ge(max_done, graph(base, u, L_S) + 1)
                    elif old(base, u, L_PT, 1):
                        pe.wait_ge(pT_done, i)
                    for hh in range(HH):
                        for r in range(RG):
                            mm = pe.transpose(ps_s[:, hh, r * P:(r + 1) * P], scores[:, buf, hh * RG + r, :], ident[:])
                    mm.then_inc(pT_mm, 1)
                if live(L_OT):
                    i, buf = graph(base, u, L_OT), (u - L_OT) % 2
                    pe.wait_ge(o_done, i + 1)
                    if old(base, u, L_OT, 1):
                        pe.wait_ge(oT_low, i)
                    if live(L_XT):
                        pe.wait_ge(xT_low, graph(base, u, L_XT) + 1)
                    if live(L_GT + 1) and old(base, u, L_GT + 1, 0):
                        pe.wait_ge(gT_done, graph(base, u, L_GT + 1) + 1)
                    for kb in range(KB):
                        mm = pe.transpose(ps_t[:, kb * P:(kb + 1) * P], o[:, buf, kb * P:(kb + 1) * P], ident[:])
                    mm.then_inc(oT_mm, 1)
                if live(L_QK):
                    i, which, par = graph(base, u, L_QK), (u - L_QK) % 2, (u - L_QK) // 2 % 2
                    pe.wait_ge(xT_low, i + (2 if which == 0 else 1))
                    if old(base, u, L_QK, 1):
                        pe.wait_ge(qk_low, i)
                    for blk in range(KB):
                        for n, (kb, (a, b)) in enumerate((kb, ab) for kb in range(KB) for ab in PASSES):
                            mm = pe.matmul(ps_qk[:, blk, :], wall[:, a, which, kb, blk * P:(blk + 1) * P],
                                           xT[b][:, par, kb, :], start=n == 0, stop=n == 3 * KB - 1)
                    mm.then_inc(qk_mm, 1)
                if live(L_TOP):
                    i, buf = graph(base, u, L_TOP), (u - L_TOP) % 2
                    pe.wait_ge(gT_done, i + 1)
                    if old(base, u, L_TOP, 1):
                        pe.wait_ge(logits_done, i)
                    if live(L_PV):
                        pe.wait_ge(o_done, graph(base, u, L_PV) + 1)
                    else:
                        pe.wait_ge(placed, graph(base, u, L_RANK) // 2 * 2)
                    for kb in range(KB):
                        mm = pe.matmul(gate_ps, gT[:, buf, kb, :], wg[:, kb, :], start=kb == 0, stop=kb == KB - 1)
                    mm.then_inc(gate_mm, 1)
                if live(L_RANK) and (u - L_RANK) % 2 == 1:
                    pair, pp = pair_of(base, u, L_RANK), (u - L_RANK) // 2 % 2
                    pe.wait_ge(either_done, pair + 1)
                    if not live(L_TOP):
                        pe.wait_ge(logits_done, graph(base, u, L_RANK) + 1)
                        pe.wait_ge(placed, 2 * pair)
                    pe.matmul(rank_ps[:, 0, :], before[:], either[:, pp, 0, :], start=True, stop=True)
                    pe.matmul(rank_ps[:, 1, :], before[:], either[:, pp, 1, :], start=True, stop=False)
                    pe.matmul(rank_ps[:, 1, :], ones[:], either[:, pp, 0, :], start=False, stop=True)
                    pe.matmul(total_ps, ones[:], either[:, pp, 0, :], start=True, stop=False)
                    pe.matmul(total_ps, ones[:], either[:, pp, 1, :], start=False, stop=True).then_inc(rank_mm, 1)
                if live(L_X1):
                    i, buf = graph(base, u, L_X1), (u - L_X1) % 2
                    pe.wait_ge(oT_low, i + 1)
                    if old(base, u, L_X1, 1):
                        pe.wait_ge(x1_done, i)
                    if live(L_V):
                        pe.wait_ge(v_done, graph(base, u, L_V) + 1)
                    for n, (kb, (a, b)) in enumerate((kb, ab) for kb in range(KB) for ab in PASSES):
                        mm = pe.matmul(ps_vo[:, 1, :], oT[a][:, buf, kb, :], wall[:, b, 3, kb, :],
                                       start=n == 0, stop=n == 3 * KB - 1)
                    mm.then_inc(proj_mm, 1)
                if live(L_GT):
                    i = graph(base, u, L_GT)
                    pe.wait_ge(normed2, i + 1)
                    if live(L_OT):
                        pe.wait_ge(oT_low, graph(base, u, L_OT) + 1)
                    if old(base, u, L_GT, 1):
                        pe.wait_ge(gT_done, i)
                    for kb in range(KB):
                        mm = pe.transpose(ps_t[:, kb * P:(kb + 1) * P],
                                          xn2[:, (u - L_GT) % 8, kb * P:(kb + 1) * P], ident[:])
                    mm.then_inc(gT_mm, 1)

            pe.wait_ge(const_ready, 1)
            pe.wait_ge(consts_pool, 2 + EXPERTS)
            run(pe, step)

        @block.scalar
        def _(act):
            act.wait_ge(const_loaded, 16 * CONSTS)
            act.activation(raw[:, 0, :], raw[:, 0, :], ACT.Copy, scale=SCALE).then_inc(const_high, 1)
            act.activation(bqk[:, 0, :], bqk[:, 0, :], ACT.Copy, scale=SCALE).then_inc(const_high, 1)
            act.wait_ge(const_high, 2)
            for k in range(4):
                act.activation(wall[:, HIGH, k], raw[:, k, :].rearrange("p (k d) -> p k d", k=KB),
                               ACT.Copy).then_inc(const_high, 1)

            def step(base, u, live):
                if live(L_XT):
                    i, par, cols = graph(base, u, L_XT), (u - L_XT) // 2 % 2, (u - L_XT) % 2 * P
                    if old(base, u, L_XT, 4):
                        act.wait_ge(v_mm, i - 3)
                        act.wait_ge(qk_mm, i - 2 - (u - L_XT) % 2)
                    act.wait_ge(xT_mm, i + 1)
                    act.activation(xT[HIGH][:, par, :, cols:cols + P],
                                   ps_t[:].rearrange("p (k n) -> p k n", k=KB), ACT.Copy).then_inc(xT_high, 1)
                if live(L_S):
                    i, buf = graph(base, u, L_S), (u - L_S) % 2
                    act.wait_ge(neg_done, i + 1)
                    for h in range(HEADS):
                        e = act.activation(scores[:, buf, h, :], scores[:, buf, h, :], ACT.Exp,
                                           bias=neg_max[:, buf, h:h + 1])
                    e.then_inc(exp_done, 1)
                if live(L_PT):
                    i = graph(base, u, L_PT)
                    if old(base, u, L_PT, 1):
                        act.wait_ge(pv_mm, i)
                    act.wait_ge(pT_mm, i + 1)
                    act.activation(probsT[:], ps_s[:, 0:HH, :].rearrange("p b (r n) -> p (b r) n", r=RG),
                                   ACT.Copy).then_inc(pT_done, 1)
                if live(L_OT):
                    i, buf = graph(base, u, L_OT), (u - L_OT) % 2
                    if old(base, u, L_OT, 2):
                        act.wait_ge(proj_mm, i - 1)
                    act.wait_ge(oT_mm, i + 1)
                    act.activation(oT[HIGH][:, buf], ps_t[:].rearrange("p (k n) -> p k n", k=KB),
                                   ACT.Copy).then_inc(oT_high, 1)
                if live(L_QK):
                    i, which, par = graph(base, u, L_QK), (u - L_QK) % 2, (u - L_QK) // 2 % 2
                    if old(base, u, L_QK, 4):
                        act.wait_ge(s_mm, i - 2 - which)
                    act.wait_ge(qk_mm, i + 1)
                    for blk in range(KB):
                        act.activation(qk[HIGH][:, par, which, blk, :], ps_qk[:, blk, :], ACT.Identity,
                                       bias=bqk[:, which, blk:blk + 1]).then_inc(qk_high, 1)
                if live(L_GT):
                    i, buf = graph(base, u, L_GT), (u - L_GT) % 2
                    if old(base, u, L_GT, 2):
                        act.wait_ge(gate_mm, i - 1)
                    act.wait_ge(gT_mm, i + 1)
                    act.activation(gT[:, buf], ps_t[:].rearrange("p (k n) -> p k n", k=KB),
                                   ACT.Copy).then_inc(gT_done, 1)

            run(act, step)

        @block.vector
        def _(dve):
            dve.wait_ge(const_loaded, 16 * CONSTS)
            dve.wait_ge(const_high, 6)
            for k in range(4):
                dve.tensor_tensor(wall[:, LOW, k], raw[:, k, :].rearrange("p (k d) -> p k d", k=KB),
                                  wall[:, HIGH, k], ALU.subtract)
            dve.tensor_scalar(mask[:], mask[:], -1.0, 1.0, ALU.mult, ALU.add).then_inc(const_low, 1)
            dve.wait_ge(const_low, 1)
            dve.tensor_scalar(mask[:], mask[:], MASKED, None, ALU.mult).then_inc(const_low, 1)
            dve.memset(v1[:], 1.0).then_inc(const_low, 1)
            dve.memset(counts[:], 0.0).then_inc(const_low, 1)
            dve.wait_ge(const_low, 4)
            dve.wait_ge(consts_pool, 2 + EXPERTS)
            dve.tensor_scalar(count_rows[:], expert_id[:], float(CAP), None, ALU.mult).then_inc(const_ready, 1)
            dve.wait_ge(const_ready, 1)

            def step(base, u, live):
                if live(L_S):
                    i, buf = graph(base, u, L_S), (u - L_S) % 2
                    if old(base, u, L_S, 2):
                        hold(dve, pT_mm, i - 1)
                    hold(dve, s_mm, i + 1)
                    for h in range(HEADS):
                        hh, r = h // RG, h % RG
                        m = dve.tensor_tensor_reduce(
                            scores[:, buf, h, :], ps_s[:, r, hh * P:(hh + 1) * P], mask[:], 1.0, -3.0e38,
                            ALU.add, ALU.max, row_max[:, buf, h:h + 1])
                    m.then_inc(max_done, 1)
                    dve.wait_ge(max_done, i + 1)
                    dve.tensor_scalar(neg_max[:, buf, :], row_max[:, buf, :], -1.0, None,
                                      ALU.mult).then_inc(neg_done, 1)
                if live(L_XT):
                    i, par, cols = graph(base, u, L_XT), (u - L_XT) // 2 % 2, (u - L_XT) % 2 * P
                    dve.wait_ge(xT_high, i + 1)
                    dve.tensor_tensor(xT[LOW][:, par, :, cols:cols + P],
                                      ps_t[:].rearrange("p (k n) -> p k n", k=KB),
                                      xT[HIGH][:, par, :, cols:cols + P], ALU.subtract).then_inc(xT_low, 1)
                if live(L_PV):
                    i, buf = graph(base, u, L_PV), (u - L_PV) % 2
                    dve.wait_ge(pv_mm, i + 1)
                    dve.reciprocal(denom[:, buf, :], o_ps[:, :, HEAD_DIM]).then_inc(denom_done, 1)
                    if old(base, u, L_PV, 2):
                        dve.wait_ge(oT_mm, i - 1)
                    dve.wait_ge(denom_done, i + 1)
                    dve.tensor_tensor(o[:, buf, :].rearrange("p (h c) -> p h c", c=HEAD_DIM),
                                      o_ps[:, :, 0:HEAD_DIM],
                                      denom[:, buf, :].unsqueeze(2).broadcast_to([P, HEADS, HEAD_DIM]),
                                      ALU.mult).then_inc(o_done, 1)
                if live(L_V):
                    i, buf = graph(base, u, L_V), (u - L_V) % 4
                    if old(base, u, L_V, 4):
                        dve.wait_ge(pv_mm, i - 3)
                    dve.wait_ge(v_mm, i + 1)
                    dve.tensor_tensor(v1[:, buf, :, 0:HEAD_DIM],
                                      ps_vo[:, 0, :].rearrange("p (h c) -> p h c", c=HEAD_DIM),
                                      bv_all[:].rearrange("p (h c) -> p h c", c=HEAD_DIM),
                                      ALU.add).then_inc(v_done, 1)
                if live(L_NORM):
                    i, k = graph(base, u, L_NORM), (u - L_NORM) % 4
                    hold(dve, newton_done, newton_run(base, u, L_NORM, L_NEWTON))
                    if old(base, u, L_NORM, 2):
                        hold(dve, xT_mm, i - 1)
                    dve.tensor_scalar(xn[:, k % 2, :], xin[:, (u - L_NORM) % 8, :], moments[:, 0, k, 0:1],
                                      rstd[:, 0, k:k + 1], ALU.subtract, ALU.mult).then_inc(normed, 1)
                if live(L_NORM2):
                    i, k = graph(base, u, L_NORM2), (u - L_NORM2) % 8
                    m = (k + 2) % 4
                    hold(dve, newton_done, newton_run(base, u, L_NORM2, L_NEWTON2))
                    if old(base, u, L_NORM2, 8):
                        hold(dve, scattered[k // 2], 64 * (turns(base, u, L_NORM2, 8) - 1))
                    dve.tensor_scalar(xn2[:, k, :], x1[:, k, :], moments[:, 1, m, 0:1],
                                      rstd[:, 1, m:m + 1], ALU.subtract, ALU.mult).then_inc(normed2, 1)
                if live(L_OT):
                    i, buf = graph(base, u, L_OT), (u - L_OT) % 2
                    dve.wait_ge(oT_high, i + 1)
                    dve.tensor_tensor(oT[LOW][:, buf], ps_t[:].rearrange("p (k n) -> p k n", k=KB),
                                      oT[HIGH][:, buf], ALU.subtract).then_inc(oT_low, 1)
                if live(L_TOP):
                    i, k = graph(base, u, L_TOP), (u - L_TOP) % 4
                    if live(L_RANK) and (u - L_RANK) % 2 == 1:
                        dve.wait_ge(rank_mm, pair_of(base, u, L_RANK) + 1)
                    dve.wait_ge(gate_mm, i + 1)
                    dve.tensor_tensor(logits[:, k, :], gate_ps, bg_all[:],
                                      ALU.add).then_inc(logits_done, 1)
                if live(L_X1):
                    i, k = graph(base, u, L_X1), (u - L_X1) % 8
                    if old(base, u, L_X1, 8):
                        dve.wait_ge(x1_stored[k], 16 * turns(base, u, L_X1, 8) - 16)
                    dve.wait_ge(xres_biased, i + 1)
                    dve.wait_ge(proj_mm, i + 1)
                    dve.tensor_tensor(x1[:, k, :], ps_vo[:, 1, :], xres[:, k % 4, :], ALU.add).then_inc(x1_done, 1)
                if live(L_QK):
                    i, which, par = graph(base, u, L_QK), (u - L_QK) % 2, (u - L_QK) // 2 % 2
                    dve.wait_ge(qk_high, KB * i + KB)
                    for blk in range(KB):
                        low = dve.scalar_tensor_tensor(
                            out=qk[LOW][:, par, which, blk, :], in0=ps_qk[:, blk, :],
                            scalar=bqk[:, which, blk:blk + 1], in1=qk[HIGH][:, par, which, blk, :],
                            op0=ALU.add, op1=ALU.subtract)
                    low.then_inc(qk_low, 1)
                if live(L_SLOT) and (u - L_SLOT) % 2 == 1:
                    i, pair = graph(base, u, L_SLOT), pair_of(base, u, L_SLOT)
                    pp, k = (u - L_SLOT) // 2 % 2, (u - L_SLOT) // 2 % 4
                    if old(base, u, L_SLOT, 8):
                        dve.wait_ge(scattered[k], 16 * 4 * (turns(base, u - 1, L_SLOT, 8) - 1))
                    dve.wait_ge(rank_mm, pair + 1)
                    dve.tensor_tensor(place[:, pp], rank_ps,
                                      count_rows[:].unsqueeze(1).broadcast_to([P, 2, EXPERTS]),
                                      ALU.add).then_inc(placed, 1)
                    dve.tensor_tensor(counts[:], total_ps, counts[:], ALU.add)
                    dve.wait_ge(placed, 2 * pair + 1)
                    dve.tensor_tensor(count_rows[:], total_ps, count_rows[:], ALU.add).then_inc(placed, 1)
                    for c in range(TOP_K):
                        dve.tensor_tensor(picked[:, pp, c], chosen[:, pp, c], place[:, pp],
                                          ALU.mult).then_inc(chain_slot, 1)
                    dve.wait_ge(chain_slot, 3 * pair + 2)
                    dve.tensor_reduce(slot_f[:, pp], picked[:, pp], AX.X, ALU.add).then_inc(chain_slot, 1)
                    dve.wait_ge(chain_slot, 3 * pair + 3)
                    dve.tensor_copy(slot_i[:, k], slot_f[:, pp]).then_inc(slot_done, 1)
                    dve.tensor_copy(slots[:, :, bass.ds(graph(base, u, L_SLOT + 1), 2)], slot_f[:, pp])
                if live(L_X1):
                    i, k = graph(base, u, L_X1), (u - L_X1) % 8
                    dve.wait_ge(x1_done, i + 1)
                    dve.bn_stats(stats2[:, k % 4, :], x1[:, k, :]).then_inc(stats2_done, 1)
                if live(L_STATS):
                    i, k = graph(base, u, L_STATS), (u - L_STATS) % 8
                    dve.wait_ge(x_loaded[k], 16 * turns(base, u, L_STATS, 8))
                    dve.bn_stats(stats[:, k % 4, :], xin[:, k, :]).then_inc(stats_done, 1)
                if live(L_TOP):
                    i, k = graph(base, u, L_TOP), (u - L_TOP) % 4
                    hold(dve, logits_done, i + 1)
                    dve.max(top8[:, k, :], logits[:, k, :]).then_inc(chain_dve, 1)
                if live(L_X1):
                    i, k = graph(base, u, L_X1), (u - L_X1) % 4
                    hold(dve, stats2_done, i + 1)
                    dve.bn_aggr(moments[:, 1, (k + 2) % 4, :], stats2[:, k, :]).then_inc(moments2_done, 1)
                if live(L_TOP):
                    i, k = graph(base, u, L_TOP), (u - L_TOP) % 4
                    hold(dve, chain_dve, i + 1)
                    dve.max_index(top8_at[:, k, :], top8[:, k, :], logits[:, k, :]).then_inc(top_done, 1)
                    dve.tensor_copy(top_scores[:, :, bass.ds(i, 1)], top8[:, k, 0:TOP_K].unsqueeze(2))
                if live(L_STATS):
                    i, k = graph(base, u, L_STATS), (u - L_STATS) % 4
                    hold(dve, stats_done, i + 1)
                    dve.bn_aggr(moments[:, 0, k, :], stats[:, k, :]).then_inc(moments_done, 1)
                if live(L_TOP) and (u - L_TOP) % 2 == 1:
                    i, pair = graph(base, u, L_TOP), pair_of(base, u, L_TOP)
                    pp, k = (u - L_TOP) // 2 % 2, (u - L_TOP) % 4 - 1
                    dve.wait_ge(top_done, i + 1)
                    dve.tensor_copy(top_at[:, pp], top8_at[:, k:k + 2, 0:TOP_K]).then_inc(chosen_done, 1)
                    dve.wait_ge(chosen_done, 3 * pair + 1)
                    for c in range(TOP_K):
                        dve.tensor_tensor(
                            chosen[:, pp, c], expert_id[:].unsqueeze(1).broadcast_to([P, 2, EXPERTS]),
                            top_at[:, pp, :, c].unsqueeze(2).broadcast_to([P, 2, EXPERTS]),
                            ALU.is_equal).then_inc(chosen_done, 1)
                    dve.wait_ge(chosen_done, 3 * pair + 3)
                    dve.tensor_tensor(either[:, pp], chosen[:, pp, 0], chosen[:, pp, 1],
                                      ALU.add).then_inc(either_done, 1)

            run(dve, step)

        @block.gpsimd
        def _(pool):
            pool.memset(before[:], 1.0).then_inc(chain_pool, 1)
            pool.wait_ge(chain_pool, 1)
            pool.affine_select(out=before[:], in_=before[:], compare_op=ALU.is_gt, fill=0.0, base=0,
                               pattern=[[1, P]], channel_multiplier=-1).then_inc(consts_pool, 1)
            pool.memset(ones[:], 1.0).then_inc(consts_pool, 1)
            for e in range(EXPERTS):
                pool.memset(expert_id[:, e:e + 1], float(e)).then_inc(consts_pool, 1)
            pool.wait_ge(const_loaded, 16 * CONSTS)

            ROUND = 14

            def rsqrt(run_before, var, root, shifted, square):
                n = [0]

                def then(instruction):
                    n[0] += 1
                    if n[0] == ROUND:
                        instruction.then_inc(newton_done, 1)
                    else:
                        instruction.then_inc(newton_step, 1)
                        hold(pool, newton_step, run_before * (ROUND - 1) + n[0])

                then(pool.tensor_scalar(shifted, var, EPS, None, ALU.add))
                then(pool.tensor_scalar(root.bitcast(I32), shifted.bitcast(I32), -0.5, RSQRT_MAGIC,
                                        ALU.mult, ALU.add))
                for _ in range(3):
                    then(pool.tensor_tensor(square, root, root, ALU.mult))
                    then(pool.tensor_tensor(square, square, shifted, ALU.mult))
                    then(pool.tensor_scalar(square, square, -0.5, 1.5, ALU.mult, ALU.add))
                    then(pool.tensor_tensor(root, square, root, ALU.mult))
                assert n[0] == ROUND

            def step(base, u, live):
                if (live(L_NEWTON) or live(L_NEWTON2)) and u % 2 == 0:
                    norms = slice(0 if live(L_NEWTON) else 1, 2 if live(L_NEWTON2) else 1)
                    if live(L_NEWTON):
                        hold(pool, moments_done, graph(base, u, L_NEWTON) + 2)
                    if live(L_NEWTON2):
                        hold(pool, moments2_done, graph(base, u, L_NEWTON2) + 2)
                    k = (u - L_NEWTON) % 4
                    rsqrt(pair_of(base, u, L_NEWTON), moments[:, norms, k:k + 2, 1], rstd[:, norms, k:k + 2],
                          newton[:, 0, norms, :], newton[:, 1, norms, :])
                if live(L_OT):
                    k = (u - L_OT) % 4
                    pool.wait_ge(xres_loaded[k], 16 * turns(base, u, L_OT, 4))
                    pool.tensor_tensor(xres[:, k, :], xres[:, k, :], bo_all[:], ALU.add).then_inc(xres_biased, 1)
                if live(L_SLOT) and (u - L_SLOT) % 2 == 1:
                    i, pair = graph(base, u, L_SLOT), pair_of(base, u, L_SLOT)
                    k = (u - L_SLOT) // 2 % 4
                    hold(pool, slot_done, pair + 1)
                    for g in range(2):
                        for c in range(TOP_K):
                            pool.indirect_dma_start(
                                rows_dram, bass.IndirectOffsetOnAxis(slot_i[:, k, c, g:g + 1], axis=0),
                                xn2[:, (u - L_SLOT - 1 + g) % 8, :], None).then_inc(scattered[k], 16)

            run(pool, step)
            for k in range(4):
                pool.wait_ge(scattered[k], 64 * (GRAPHS // 8))


def experts(nc, b1, b2, w1, w2, ident, counts, count_rows, slots, outputs_at, rows_dram, expert_dram, EXPERTS, D, HID, CAP,
            TILES, FEWEST_TILES):
    KB, HB = D // P, HID // P
    UNROLL = 4
    L_XT, L_F1, L_HT, L_F2, L_STORE = 2, 3, 4, 5, 6
    HEAD_STEPS = -(-L_STORE // UNROLL) * UNROLL
    assert TILES % UNROLL == 0
    with ExitStack() as ctx:
        def sb(name, shape, dt=F32):
            return ctx.enter_context(nc.sbuf_tensor(name, shape, dt))

        def pb(name, shape):
            return ctx.enter_context(nc.psum_tensor(name, shape, F32))

        def sem(name):
            return ctx.enter_context(nc.semaphore(name))

        b1_all = sb("b1_all", [P, EXPERTS, HID])
        b2_all = sb("b2_all", [P, EXPERTS, D])
        zeros = sb("zeros", [P, D])
        tile_i = sb("tile_i", [1, TILES], I32)
        tile_f = sb("tile_f", [1, TILES])
        past = sb("past", [1, TILES])
        tile_expert_f = sb("tile_expert_f", [1, TILES])
        tile_first = sb("tile_first", [1, TILES])
        tile_row_f = sb("tile_row_f", [1, TILES])
        tile_expert = sb("tile_expert", [1, TILES], I32)
        tile_row = sb("tile_row", [1, TILES], I32)
        count_i = sb("count_i", [P, EXPERTS], I32)
        tiles_of = sb("tiles_of", [P, EXPERTS])
        jump = sb("jump", [P, EXPERTS])
        closer = sb("closer", list(slots.shape))
        moved_slots = sb("moved_slots", list(slots.shape))
        tiles_upto = sb("tiles_upto", [1, EXPERTS])
        pad_row = sb("pad_row", [1, EXPERTS], I32)
        rows = sb("rows", [P, 4, D])
        xT = [sb(f"rowsT{h}", [P, 2, KB, P], F32R) for h in (HIGH, LOW)]
        biased = sb("biased", [P, 2, HID])
        hidden = sb("hidden", [P, 2, HID])
        hT = [sb(f"hT{h}", [P, 2, HB, P], F32R) for h in (HIGH, LOW)]
        y = sb("y", [P, 4, D])
        ps_xT = pb("ps_xT", [P, 2, 512])
        ps_h = pb("ps_h", [P, 2, 512])
        ps_hT = pb("ps_hT", [P, 2, 512])
        ps_y = pb("ps_y", [P, 2, 512])

        bias_loaded, padded = sem("bias_loaded"), sem("padded")
        rows_loaded = [sem(f"rows_loaded{k}") for k in range(4)]
        y_stored = [sem(f"y_stored{k}") for k in range(4)]
        (tile_iota, zeros_done, moved, table_step, table_done, xT_mm, xT_high, xT_low, h_mm, h_biased, gelu_done,
         hT_mm, hT_high, hT_low, y_mm, y_done) = (sem("e_" + n) for n in (
             "tile_iota zeros_done moved table_step table_done xT_mm xT_high xT_low h_mm h_biased gelu_done "
             "hT_mm hT_high hT_low y_mm y_done").split())

        def run(eng, step):
            for t in range(HEAD_STEPS):
                step(t // UNROLL, t % UNROLL, lambda lag: t >= lag)
            with eng.Fori(HEAD_STEPS // UNROLL, TILES // UNROLL) as base:
                for u in range(UNROLL):
                    step(base, u, lambda lag: True)
            for t in range(TILES, TILES + L_STORE + 1):
                step(t // UNROLL, t % UNROLL, lambda lag: t - lag < TILES)

        def tile(base, u, lag):
            return base * UNROLL + (u - lag)

        def turns(base, u, lag, ring):
            return base * (UNROLL // ring) + ((u - lag) // ring + 1)

        def old(base, u, lag, back):
            return not isinstance(base, int) or tile(base, u, lag) >= back

        block = ctx.enter_context(nc.Block())

        @block.gpsimd
        def _(pool):
            pool.iota(tile_i[:], pattern=[[1, TILES]], base=0, channel_multiplier=0).then_inc(tile_iota, 1)
            pool.memset(zeros[:], 0.0).then_inc(zeros_done, 1)
            pool.wait_ge(table_done, 1)
            for e in range(1, EXPERTS):
                if e > 1:
                    pool.wait_ge(moved, 2 * e - 2)
                pool.tensor_scalar(closer[:], slots[:], float(e * CAP), jump[:, e - 1:e], ALU.is_ge,
                                   ALU.mult).then_inc(moved, 1)
                pool.wait_ge(moved, 2 * e - 1)
                pool.tensor_tensor(moved_slots[:], (slots if e == 1 else moved_slots)[:], closer[:],
                                   ALU.add).then_inc(moved, 1)
            pool.wait_ge(moved, 2 * EXPERTS - 2)
            pool.tensor_copy(outputs_at[:], moved_slots[:]).then_inc(moved, 1)

        @block.sync
        def _(sp):
            sp.dma_start(b1_all[:], b1.partition_broadcast(P)).then_inc(bias_loaded, 16)
            sp.dma_start(b2_all[:], b2.partition_broadcast(P)).then_inc(bias_loaded, 16)
            sp.wait_ge(zeros_done, 1)
            for n in range(TILES - FEWEST_TILES):
                at = EXPERTS * CAP + n * P
                sp.dma_start(rows_dram[at:at + P, :], zeros[:]).then_inc(padded, 16)
            sp.wait_ge(table_done, 1)
            for e in range(EXPERTS):
                at = sp.value_load(pad_row[0:1, e:e + 1], min_val=e * CAP, max_val=(e + 1) * CAP - P)
                sp.dma_start(rows_dram[bass.ds(at, P), :], zeros[:]).then_inc(padded, 16)
            sp.wait_ge(padded, 16 * (TILES - FEWEST_TILES + EXPERTS))

            def tile_rows(base, u, lag):
                at = sp.value_load(tile_row[0:1, bass.ds(tile(base, u, lag), 1)], min_val=0,
                                   max_val=EXPERTS * CAP + (TILES - FEWEST_TILES - 1) * P)
                return bass.ds(at, P)

            def step(base, u, live):
                if live(L_STORE):
                    j, k = tile(base, u, L_STORE), (u - L_STORE) % 4
                    sp.wait_ge(y_done, j + 1)
                    sp.dma_start(expert_dram[bass.ds(j * P, P), :], y[:, k, :]).then_inc(y_stored[k], 16)
                if live(0):
                    j, k = tile(base, u, 0), u % 4
                    at = tile_rows(base, u, 0)
                    if old(base, u, 0, 4):
                        sp.wait_ge(xT_mm, j - 3)
                    sp.dma_start(rows[:, k, :], rows_dram[at, :]).then_inc(rows_loaded[k], 16)

            run(sp, step)
            for k in range(4):
                sp.wait_ge(y_stored[k], 16 * (TILES // 4))

        def expert_of(eng, base, u, lag):
            return eng.value_load(tile_expert[0:1, bass.ds(tile(base, u, lag), 1)], min_val=0, max_val=EXPERTS - 1)

        @block.tensor
        def _(pe):
            def step(base, u, live):
                if live(L_F2):
                    j, buf = tile(base, u, L_F2), (u - L_F2) % 2
                    e = expert_of(pe, base, u, L_F2)
                    pe.wait_ge(hT_low, j + 1)
                    if old(base, u, L_F2, 2):
                        pe.wait_ge(y_done, j - 1)
                    for n, (hb, (a, b)) in enumerate((hb, ab) for hb in range(HB) for ab in PASSES):
                        mm = pe.matmul(ps_y[:, buf, 0:D], hT[a][:, buf, hb, :],
                                       w2[:, b, bass.ds(e, 1), hb * D:(hb + 1) * D],
                                       start=n == 0, stop=n == 3 * HB - 1)
                    mm.then_inc(y_mm, 1)
                if live(L_F1):
                    j, buf = tile(base, u, L_F1), (u - L_F1) % 2
                    e = expert_of(pe, base, u, L_F1)
                    pe.wait_ge(xT_low, j + 1)
                    if old(base, u, L_F1, 2):
                        pe.wait_ge(h_biased, j - 1)
                    for n, (kb, (a, b)) in enumerate((kb, ab) for kb in range(KB) for ab in PASSES):
                        mm = pe.matmul(ps_h[:, buf, 0:HID], xT[a][:, buf, kb, :],
                                       w1[:, b, bass.ds(e, 1), kb * HID:(kb + 1) * HID],
                                       start=n == 0, stop=n == 3 * KB - 1)
                    mm.then_inc(h_mm, 1)
                if live(L_XT):
                    j, buf, k = tile(base, u, L_XT), (u - L_XT) % 2, (u - L_XT) % 4
                    pe.wait_ge(rows_loaded[k], 16 * turns(base, u, L_XT, 4))
                    if old(base, u, L_XT, 2):
                        pe.wait_ge(xT_low, j - 1)
                    for kb in range(KB):
                        mm = pe.transpose(ps_xT[:, buf, kb * P:(kb + 1) * P], rows[:, k, kb * P:(kb + 1) * P],
                                          ident[:])
                    mm.then_inc(xT_mm, 1)
                if live(L_HT):
                    j, buf = tile(base, u, L_HT), (u - L_HT) % 2
                    pe.wait_ge(gelu_done, j + 1)
                    if old(base, u, L_HT, 2):
                        pe.wait_ge(hT_low, j - 1)
                    for hb in range(HB):
                        mm = pe.transpose(ps_hT[:, buf, hb * P:(hb + 1) * P], hidden[:, buf, hb * P:(hb + 1) * P],
                                          ident[:])
                    mm.then_inc(hT_mm, 1)

            pe.wait_ge(table_done, 1)
            run(pe, step)

        @block.scalar
        def _(act):
            def step(base, u, live):
                if live(L_XT):
                    j, buf = tile(base, u, L_XT), (u - L_XT) % 2
                    if old(base, u, L_XT, 2):
                        act.wait_ge(h_mm, j - 1)
                    act.wait_ge(xT_mm, j + 1)
                    act.activation(xT[HIGH][:, buf], ps_xT[:, buf, 0:KB * P].rearrange("p (k n) -> p k n", k=KB),
                                   ACT.Copy).then_inc(xT_high, 1)
                if live(L_HT):
                    j, buf = tile(base, u, L_HT), (u - L_HT) % 2
                    if old(base, u, L_HT, 2):
                        act.wait_ge(y_mm, j - 1)
                    act.wait_ge(hT_mm, j + 1)
                    act.activation(hT[HIGH][:, buf], ps_hT[:, buf, 0:HID].rearrange("p (k n) -> p k n", k=HB),
                                   ACT.Copy).then_inc(hT_high, 1)
                if live(L_F1):
                    j, buf = tile(base, u, L_F1), (u - L_F1) % 2
                    if old(base, u, L_F1, 2):
                        act.wait_ge(hT_mm, j - 1)
                    act.wait_ge(h_biased, j + 1)
                    act.activation(hidden[:, buf, :], biased[:, buf, :], ACT.Gelu).then_inc(gelu_done, 1)

            run(act, step)

        @block.vector
        def _(dve):
            n = [0]

            def then(instruction):
                instruction.then_inc(table_step, 1)
                n[0] += 1
                dve.wait_ge(table_step, n[0])

            dve.wait_ge(tile_iota, 1)
            then(dve.tensor_copy(tile_f[:], tile_i[:]))
            then(dve.tensor_copy(pad_row[:], count_rows[0:1, :]))
            then(dve.tensor_scalar(tiles_of[:], counts[:], float(P - 1), None, ALU.add))
            then(dve.tensor_copy(count_i[:], tiles_of[:]))
            then(dve.tensor_scalar(count_i[:], count_i[:], 7, None, ALU.logical_shift_right))
            then(dve.tensor_copy(tiles_of[:], count_i[:]))
            then(dve.tensor_scalar(jump[:], tiles_of[:], float(P), -float(CAP), ALU.mult, ALU.add))
            then(dve.tensor_copy(tiles_upto[:], tiles_of[0:1, :]))
            for e in range(1, EXPERTS):
                then(dve.tensor_tensor(tiles_upto[:, e:e + 1], tiles_upto[:, e - 1:e], tiles_of[0:1, e:e + 1], ALU.add))
            then(dve.memset(tile_expert_f[:], 0.0))
            then(dve.memset(tile_first[:], 0.0))
            for e in range(EXPERTS):
                then(dve.tensor_scalar(past[:], tile_f[:], tiles_upto[:, e:e + 1], None, ALU.is_ge))
                then(dve.tensor_tensor(tile_expert_f[:], tile_expert_f[:], past[:], ALU.add))
                then(dve.scalar_tensor_tensor(out=tile_first[:], in0=past[:], scalar=tiles_of[0:1, e:e + 1],
                                              in1=tile_first[:], op0=ALU.mult, op1=ALU.add))
            then(dve.tensor_tensor(tile_f[:], tile_f[:], tile_first[:], ALU.subtract))
            then(dve.tensor_scalar(tile_f[:], tile_f[:], float(P), None, ALU.mult))
            then(dve.scalar_tensor_tensor(out=tile_row_f[:], in0=tile_expert_f[:], scalar=float(CAP),
                                          in1=tile_f[:], op0=ALU.mult, op1=ALU.add))
            then(dve.tensor_copy(tile_row[:], tile_row_f[:]))
            then(dve.tensor_scalar(tile_expert_f[:], tile_expert_f[:], float(EXPERTS - 1), None, ALU.min))
            dve.tensor_copy(tile_expert[:], tile_expert_f[:]).then_inc(table_done, 1)
            dve.wait_ge(table_done, 1)
            dve.wait_ge(bias_loaded, 32)

            def step(base, u, live):
                if live(L_F2):
                    j, buf, k = tile(base, u, L_F2), (u - L_F2) % 2, (u - L_F2) % 4
                    e = expert_of(dve, base, u, L_F2)
                    if old(base, u, L_F2, 4):
                        dve.wait_ge(y_stored[k], 16 * (turns(base, u, L_F2, 4) - 1))
                    dve.wait_ge(y_mm, j + 1)
                    dve.tensor_tensor(y[:, k, :].unsqueeze(1), ps_y[:, buf, 0:D].unsqueeze(1),
                                      b2_all[:, bass.ds(e, 1), :], ALU.add).then_inc(y_done, 1)
                if live(L_F1):
                    j, buf = tile(base, u, L_F1), (u - L_F1) % 2
                    e = expert_of(dve, base, u, L_F1)
                    if old(base, u, L_F1, 2):
                        dve.wait_ge(gelu_done, j - 1)
                    dve.wait_ge(h_mm, j + 1)
                    dve.tensor_tensor(biased[:, buf, :].unsqueeze(1), ps_h[:, buf, 0:HID].unsqueeze(1),
                                      b1_all[:, bass.ds(e, 1), :], ALU.add).then_inc(h_biased, 1)
                if live(L_XT):
                    j, buf = tile(base, u, L_XT), (u - L_XT) % 2
                    dve.wait_ge(xT_high, j + 1)
                    dve.tensor_tensor(xT[LOW][:, buf], ps_xT[:, buf, 0:KB * P].rearrange("p (k n) -> p k n", k=KB),
                                      xT[HIGH][:, buf], ALU.subtract).then_inc(xT_low, 1)
                if live(L_HT):
                    j, buf = tile(base, u, L_HT), (u - L_HT) % 2
                    dve.wait_ge(hT_high, j + 1)
                    dve.tensor_tensor(hT[LOW][:, buf], ps_hT[:, buf, 0:HID].rearrange("p (k n) -> p k n", k=HB),
                                      hT[HIGH][:, buf], ALU.subtract).then_inc(hT_low, 1)

            run(dve, step)


def combine(nc, outputs_at, top_scores, x1_dram, expert_dram, out_rows, GRAPHS, D):
    UNROLL = 4
    with ExitStack() as ctx:
        def sb(name, shape, dt=F32):
            return ctx.enter_context(nc.sbuf_tensor(name, shape, dt))

        def sem(name):
            return ctx.enter_context(nc.semaphore(name))

        gates = sb("gates", [P, TOP_K, GRAPHS])
        gate_sum = sb("gate_sum", [P, GRAPHS])
        index = sb("index", [P, 4, TOP_K], I32)
        x1 = sb("c_x1", [P, 4, D])
        y = sb("c_y", [P, 4, TOP_K, D])
        part = sb("part", [P, 4, D])
        total = sb("total", [P, 4, D])
        x1_loaded = [sem(f"c_x1_loaded{k}") for k in range(4)]
        y_gathered = [sem(f"c_y_gathered{k}") for k in range(4)]
        out_stored = [sem(f"out_stored{k}") for k in range(4)]
        gate_step, gate_exp, gates_done, index_done, part_done, total_done, held = (sem("c_" + n) for n in (
            "gate_step gate_exp gates_done index_done part_done total_done held").split())

        block = ctx.enter_context(nc.Block())

        @block.sync
        def _(sp):
            def load(i, k, again):
                if again:
                    sp.wait_ge(part_done, i - 3)
                sp.dma_start(x1[:, k, :], x1_dram[bass.ds(i * P, P), :]).then_inc(x1_loaded[k], 16)

            def store(i, k):
                sp.wait_ge(total_done, i + 1)
                sp.dma_start(out_rows[bass.ds(i * P, P), :], total[:, k, :]).then_inc(out_stored[k], 16)

            for i in range(4):
                load(i, i, False)
            with sp.Fori(1, GRAPHS // UNROLL) as base:
                for u in range(UNROLL):
                    store(base * UNROLL + (u - UNROLL), u)
                    load(base * UNROLL + u, u, True)
            for i in range(GRAPHS - 4, GRAPHS):
                store(i, i % 4)
            for k in range(4):
                sp.wait_ge(out_stored[k], 16 * (GRAPHS // 4))

        @block.gpsimd
        def _(pool):
            def gather(base, u, again):
                i = base * UNROLL + u
                if again:
                    pool.wait_ge(total_done, i - 3)
                    pool.sem_inc(held, 1)
                pool.tensor_copy(index[:, u, :].unsqueeze(2), outputs_at[:, :, bass.ds(i, 1)]).then_inc(index_done, 1)
                pool.wait_ge(index_done, i + 1)
                pool.sem_inc(held, 1)
                for c in range(TOP_K):
                    pool.indirect_dma_start(y[:, u, c, :], None, expert_dram,
                                            bass.IndirectOffsetOnAxis(index[:, u, c:c + 1], axis=0)).then_inc(
                                                y_gathered[u], 16)

            for u in range(4):
                gather(0, u, False)
            with pool.Fori(1, GRAPHS // UNROLL) as base:
                for u in range(UNROLL):
                    gather(base, u, True)

        @block.scalar
        def _(act):
            act.wait_ge(gate_step, 1)
            act.activation(gates[:, 1, :], gate_sum[:], ACT.Exp).then_inc(gate_exp, 1)

        @block.vector
        def _(dve):
            dve.tensor_tensor(gate_sum[:], top_scores[:, 1, :], top_scores[:, 0, :], ALU.subtract).then_inc(gate_step, 1)
            dve.wait_ge(gate_exp, 1)
            dve.tensor_scalar(gate_sum[:], gates[:, 1, :], 1.0, None, ALU.add).then_inc(gate_step, 1)
            dve.wait_ge(gate_step, 2)
            dve.reciprocal(gates[:, 0, :], gate_sum[:]).then_inc(gate_step, 1)
            dve.wait_ge(gate_step, 3)
            dve.tensor_tensor(gates[:, 1, :], gates[:, 1, :], gates[:, 0, :], ALU.mult).then_inc(gates_done, 1)
            dve.wait_ge(gates_done, 1)

            def add(base, u, again):
                i = base * UNROLL + u
                n = base
                if again:
                    dve.wait_ge(out_stored[u], n * 16)
                dve.wait_ge(x1_loaded[u], n * 16 + 16)
                dve.wait_ge(y_gathered[u], n * 32 + 32)
                dve.scalar_tensor_tensor(out=part[:, u, :], in0=y[:, u, 0, :], scalar=gates[:, 0, bass.ds(i, 1)],
                                         in1=x1[:, u, :], op0=ALU.mult, op1=ALU.add).then_inc(part_done, 1)
                dve.wait_ge(part_done, i + 1)
                dve.scalar_tensor_tensor(out=total[:, u, :], in0=y[:, u, 1, :], scalar=gates[:, 1, bass.ds(i, 1)],
                                         in1=part[:, u, :], op0=ALU.mult, op1=ALU.add).then_inc(total_done, 1)

            for u in range(4):
                add(0, u, False)
            with dve.Fori(1, GRAPHS // UNROLL) as base:
                for u in range(UNROLL):
                    add(base, u, True)


_INS = ["x", "adj", "L0_gnn_Wq", "L0_gnn_bq", "L0_gnn_Wk", "L0_gnn_bk", "L0_gnn_Wv", "L0_gnn_bv", "L0_gnn_Wo",
        "L0_gnn_bo", "L0_ffn_Wg", "L0_ffn_bg", "L0_ffn_W1", "L0_ffn_b1", "L0_ffn_W2", "L0_ffn_b2"]


def kernel(**inputs):
    import numpy as _np
    import concourse.bacc as _bacc
    from concourse.bass_utils import run_bass_kernel_spmd as _run

    nc = _bacc.Bacc("TRN2", target_bir_lowering=False, num_devices=1)
    arrays, args = {}, []
    for name in _INS:
        a = _np.ascontiguousarray(inputs[name])
        arrays[f"in_{name}"] = a
        args.append(nc.dram_tensor(f"in_{name}", a.shape, mybir.dt.from_np(a.dtype), kind="ExternalInput").ap())
    graphs, n, d = inputs["x"].shape
    n_experts = inputs["L0_ffn_W1"].shape[0]
    table = n_experts * (graphs * n + P) + n_experts * P
    args.append(nc.dram_tensor("out_x", (graphs, n, d), F32, kind="ExternalOutput").ap())
    args.append(nc.dram_tensor("x1_dram", (graphs * n, d), F32, kind="Internal").ap())
    args.append(nc.dram_tensor("rows_dram", (table, d), F32, kind="Internal").ap())
    tiles = graphs * n * TOP_K // P + n_experts
    args.append(nc.dram_tensor("expert_dram", (tiles * P, d), F32, kind="Internal").ap())
    build(nc, *args)
    r = _run(nc, [arrays], core_ids=[0])
    return r.results[0]["out_x"]
```

```python
from contextlib import ExitStack

import concourse.bass as bass
from concourse import mybir

F32 = mybir.dt.float32
F32R = mybir.dt.float32r
BF16 = mybir.dt.bfloat16
I32 = mybir.dt.int32
U32 = mybir.dt.uint32
ALU = mybir.AluOpType
ACT = mybir.ActivationFunctionType
AX = mybir.AxisListType

P = 128
HEADS = 8
HEAD_DIM = 32
TOP_K = 2
EPS = 1e-5
MASKED = -1000000000.0
RSQRT_MAGIC = float(0x5F3759DF)
PASSES = ((0, 0), (1, 0), (0, 1))
HIGH, LOW = 0, 1


def build(nc, x, adj, Wq, bq, Wk, bk, Wv, bv, Wo, bo, Wg, bg, W1, b1, W2, b2, out, x1_dram, rows_dram, expert_dram):
    GRAPHS, N, D = x.shape
    EXPERTS, _, HID = W1.shape
    TOKENS = GRAPHS * N
    KB = D // P
    HB = HID // P
    RG = P // HEAD_DIM
    HH = HEADS // RG
    CAP = TOKENS + P
    TILES = TOKENS * TOP_K // P + EXPERTS
    assert N == P and KB == 2 and HH == 2

    x_rows = x.rearrange("g n d -> (g n) d")
    out_rows = out.rearrange("g n d -> (g n) d")

    ctx = ExitStack()
    with ctx:
        def keep(name, shape, dt):
            return ctx.enter_context(nc.sbuf_tensor(name, shape, dt))

        w1 = keep("w1", [P, 2, EXPERTS, KB * HID], F32R)
        w2 = keep("w2", [P, 2, EXPERTS, HB * D], F32R)
        ident = keep("ident", [P, P], F32)
        slots = keep("slots", [P, TOP_K, GRAPHS], F32)
        outputs_at = keep("outputs_at", [P, TOP_K, GRAPHS], I32)
        top_scores = keep("top_scores", [P, TOP_K, GRAPHS], F32)
        counts = keep("counts", [P, EXPERTS], F32)
        count_rows = keep("count_rows", [P, EXPERTS], F32)

        wall = keep("attn_w", [P, 2, 4, KB, D], F32R)

        setup_weights(nc, Wq, Wk, Wv, Wo, W1, W2, wall, w1, w2, ident, EXPERTS, D, HID)
        attention(nc, x_rows, adj, wall, bq, bk, bv, bo, Wg, bg, ident, slots, top_scores,
                  counts, count_rows, x1_dram, rows_dram, GRAPHS, D, EXPERTS, CAP)
        experts(nc, b1, b2, w1, w2, ident, counts, count_rows, slots, outputs_at, rows_dram, expert_dram, EXPERTS, D, HID, CAP,
                TILES, TOKENS * TOP_K // P)
        combine(nc, outputs_at, top_scores, x1_dram, expert_dram, out_rows, GRAPHS, D)


def setup_weights(nc, Wq, Wk, Wv, Wo, W1, W2, wall, w1, w2, ident, EXPERTS, D, HID):
    KB, HB = D // P, HID // P
    with ExitStack() as ctx:
        RING = 4
        raw = ctx.enter_context(nc.sbuf_tensor("raw", [P, RING, KB * HID], F32))
        loaded = [ctx.enter_context(nc.semaphore(f"w_loaded{k}")) for k in range(RING)]
        split_high = ctx.enter_context(nc.semaphore("w_split_high"))
        split_low = ctx.enter_context(nc.semaphore("w_split_low"))
        ident_zero = ctx.enter_context(nc.semaphore("ident_zero"))
        ident_done = ctx.enter_context(nc.semaphore("ident_done"))
        raw_attn = ctx.enter_context(nc.sbuf_tensor("raw_attn", [P, 4, KB * D], F32))
        attn_loaded = [ctx.enter_context(nc.semaphore(f"attn_loaded{k}")) for k in range(4)]
        q_scaled = ctx.enter_context(nc.semaphore("q_scaled"))
        attn_high = ctx.enter_context(nc.semaphore("attn_high"))
        block = ctx.enter_context(nc.Block())
        SCALE = float(HEAD_DIM) ** -0.5
        pieces = [(W1[e].rearrange("(k p) h -> p k h", p=P), w1, KB, e) for e in range(EXPERTS)]
        pieces += [(W2[e].rearrange("(k p) d -> p k d", p=P), w2, HB, e) for e in range(EXPERTS)]

        @block.sync
        def _(sp):
            for k, w in enumerate((Wq, Wk, Wv, Wo)):
                sp.dma_start(raw_attn[:, k, :].rearrange("p (k d) -> p k d", k=KB),
                             w.rearrange("(k p) d -> p k d", p=P)).then_inc(attn_loaded[k], 16)
            for n, (src, _, blocks, _) in enumerate(pieces):
                if n >= RING:
                    sp.wait_ge(split_low, n - RING + 1)
                sp.dma_start(raw[:, n % RING, :].rearrange("p (k h) -> p k h", k=blocks), src).then_inc(
                    loaded[n % RING], 16)

        @block.scalar
        def _(act):
            act.wait_ge(attn_loaded[0], 16)
            act.activation(raw_attn[:, 0, :], raw_attn[:, 0, :], ACT.Copy, scale=SCALE).then_inc(q_scaled, 1)
            act.wait_ge(q_scaled, 1)
            for k in range(4):
                act.wait_ge(attn_loaded[k], 16)
                act.activation(wall[:, HIGH, k], raw_attn[:, k, :].rearrange("p (k d) -> p k d", k=KB),
                               ACT.Copy).then_inc(attn_high, 1)
            for n, (_, dst, _, e) in enumerate(pieces):
                act.wait_ge(loaded[n % RING], 16 * (n // RING + 1))
                act.activation(dst[:, HIGH, e, :], raw[:, n % RING, :], ACT.Copy).then_inc(split_high, 1)

        @block.vector
        def _(dve):
            for k in range(4):
                dve.wait_ge(attn_high, k + 1)
                dve.tensor_tensor(wall[:, LOW, k], raw_attn[:, k, :].rearrange("p (k d) -> p k d", k=KB),
                                  wall[:, HIGH, k], ALU.subtract)
            for n, (_, dst, _, e) in enumerate(pieces):
                dve.wait_ge(split_high, n + 1)
                dve.tensor_tensor(dst[:, LOW, e, :], raw[:, n % RING, :], dst[:, HIGH, e, :],
                                  ALU.subtract).then_inc(split_low, 1)

        @block.gpsimd
        def _(pool):
            pool.memset(ident[:], 0.0).then_inc(ident_zero, 1)
            pool.wait_ge(ident_zero, 1)
            pool.affine_select(out=ident[:], in_=ident[:], compare_op=ALU.not_equal, fill=1.0, base=0,
                               pattern=[[-1, P]], channel_multiplier=1).then_inc(ident_done, 1)


def attention(nc, x_rows, adj, wall, bq, bk, bv, bo, Wg, bg, ident, slots, top_scores,
              counts, count_rows, x1_dram, rows_dram, GRAPHS, D, EXPERTS, CAP):
    KB, RG, HH = D // P, P // HEAD_DIM, HEADS * HEAD_DIM // P
    VW = HEAD_DIM + 1
    SCALE = float(HEAD_DIM) ** -0.5
    UNROLL = 8
    CONSTS = 1 + 1 + 2 * KB + 3
    L_STATS, L_NEWTON, L_NORM, L_XT, L_QK, L_V = 4, 6, 7, 8, 10, 11
    L_SPREAD, L_S, L_PT, L_PV, L_OT, L_RES, L_X1 = 12, 13, 14, 15, 16, 16, 17
    L_STATS2, L_NEWTON2, L_NORM2, L_GT, L_TOP, L_BEST, L_RANK, L_SLOT = 18, 20, 21, 22, 23, 24, 25, 25
    L_LAST = L_SLOT + 1
    HEAD_STEPS = -(-L_LAST // UNROLL) * UNROLL
    assert GRAPHS % UNROLL == 0

    with ExitStack() as ctx:
        def sb(name, shape, dt=F32):
            return ctx.enter_context(nc.sbuf_tensor(name, shape, dt))

        def pb(name, shape):
            return ctx.enter_context(nc.psum_tensor(name, shape, F32))

        def sem(name):
            return ctx.enter_context(nc.semaphore(name))

        wg = sb("wg", [P, KB, EXPERTS])
        bqk = sb("bqk", [P, 2, KB])
        bv_all = sb("bv_all", [P, D])
        bo_all = sb("bo_all", [P, D])
        bg_all = sb("bg_all", [P, EXPERTS])
        mask = sb("mask", [P, P])
        before = sb("before", [P, P], BF16)
        ones = sb("ones", [P, P], BF16)
        expert_id = sb("expert_id", [P, EXPERTS])
        xin = sb("xin", [P, 8, D])
        stats = sb("stats", [P, 4, 6])
        moments = sb("moments", [P, 2, 4, 2])
        rstd = sb("rstd", [P, 2, 4])
        newton = sb("newton", [P, 2, 2, 2])
        xn = sb("xn", [P, D])
        xT = [sb(f"xT{h}", [P, 2, KB, 2 * P], F32R) for h in (HIGH, LOW)]
        q = sb("q", [P, 2, 2, KB, 2 * P], F32R)
        k_all = sb("k_all", [P, 2, KB, 2 * P], F32R)
        k_heads = sb("k_heads", [P, 2, 2, KB, RG, P], F32R)
        v1 = sb("v1", [P, 4, HEADS, VW])
        scores = sb("scores", [P, 2, HEADS, P])
        neg_max = sb("neg_max", [P, 2, HEADS])
        probsT = sb("probsT", [P, HEADS, P])
        denom = sb("denom", [P, 2, HEADS])
        o = sb("o", [P, 2, D])
        oT = [sb(f"oT{h}", [P, 2, KB, P], F32R) for h in (HIGH, LOW)]
        xres = sb("xres", [P, 2, D])
        x1 = sb("x1", [P, 8, D])
        stats2 = sb("stats2", [P, 4, 6])
        xn2 = sb("xn2", [P, 8, D])
        gT = sb("gT", [P, 2, KB, P])
        logits = sb("logits", [P, 4, EXPERTS])
        top8 = sb("top8", [P, 4, 8])
        top8_at = sb("top8_at", [P, 4, 8], U32)
        top_at = sb("top_at", [P, 2, 2, TOP_K])
        chosen = sb("chosen", [P, 2, TOP_K, 2, EXPERTS])
        either = sb("either", [P, 2, 2, EXPERTS], BF16)
        place = sb("place", [P, 2, 2, EXPERTS])
        picked = sb("picked", [P, 2, TOP_K, 2, EXPERTS])
        slot_f = sb("slot_f", [P, 2, TOP_K, 2])
        slot_i = sb("slot_i", [P, 4, TOP_K, 2], I32)

        ps_s = pb("ps_s", [P, HH, RG * P])
        ps_pT = pb("ps_pT", [P, HH, RG * P])
        ps_qk = pb("ps_qk", [P, KB, 2 * P])
        ps_vo = pb("ps_vo", [P, 2, D])
        ps_t = pb("ps_t", [P, 512])[:, 0:KB * P]
        ps_o = pb("ps_o", [P, 512])
        o_ps = ps_o[:, 0:HEADS * VW].rearrange("p (h c) -> p h c", c=VW)
        gate_ps = ps_o[:, 272:272 + EXPERTS]
        rank_ps = ps_o[:, 304:304 + 2 * EXPERTS].rearrange("p (g e) -> p g e", e=EXPERTS)
        total_ps = ps_o[:, 336:336 + EXPERTS]

        x_loaded = [sem(f"x_loaded{k}") for k in range(8)]
        k_spread = [sem(f"k_spread{k}") for k in range(2)]
        xres_loaded = [sem(f"xres_loaded{k}") for k in range(2)]
        x1_stored = [sem(f"x1_stored{k}") for k in range(8)]
        scattered = [sem(f"scattered{k}") for k in range(4)]
        const_loaded, zero_stored = sem("const_loaded"), sem("zero_stored")
        (const_high, const_low, const_ready, consts_pool, chain_pool, chain_dve, held, stats_done, moments_done, normed,
         xT_mm, xT_high, xT_low, qk_mm, qk_high, qk_low, v_mm, v_done, s_mm, max_done, exp_done,
         pT_mm, pT_done, pv_mm, denom_done, o_done, oT_mm, oT_high, oT_low, proj_mm, xres_biased,
         x1_done, stats2_done, moments2_done, normed2, gT_mm, gT_done, gate_mm, logits_done, top_done,
         chosen_done, either_done, rank_mm, placed, chain_slot, slot_done, newton_step, newton_done) = (sem(n) for n in (
             "const_high const_low const_ready consts_pool chain_pool chain_dve held stats_done moments_done normed "
             "xT_mm xT_high xT_low qk_mm qk_high qk_low v_mm v_done s_mm max_done exp_done "
             "pT_mm pT_done pv_mm denom_done o_done oT_mm oT_high oT_low proj_mm xres_biased "
             "x1_done stats2_done moments2_done normed2 gT_mm gT_done gate_mm logits_done top_done "
             "chosen_done either_done rank_mm placed chain_slot slot_done newton_step newton_done").split())

        def hold(eng, semaphore, count):
            eng.wait_ge(semaphore, count)
            eng.sem_inc(held, 1)

        def run(eng, step):
            for t in range(HEAD_STEPS):
                step(t // UNROLL, t % UNROLL, lambda lag: t >= lag)
            with eng.Fori(HEAD_STEPS // UNROLL, GRAPHS // UNROLL) as base:
                for u in range(UNROLL):
                    step(base, u, lambda lag: True)
            for t in range(GRAPHS, GRAPHS + L_LAST):
                step(t // UNROLL, t % UNROLL, lambda lag: t - lag < GRAPHS)

        def graph(base, u, lag):
            return base * UNROLL + (u - lag)

        def turns(base, u, lag, ring):
            return base * (UNROLL // ring) + ((u - lag) // ring + 1)

        def pair_of(base, u, lag):
            return base * (UNROLL // 2) + (u - lag) // 2

        def newton_run(base, u, lag, newton_lag):
            first = (u - lag) // 2 * 2 + newton_lag
            return base * (UNROLL // 2) + ((first - L_NEWTON) // 2 + 1)

        def old(base, u, lag, back):
            return not isinstance(base, int) or graph(base, u, lag) >= back

        block = ctx.enter_context(nc.Block())

        @block.sync
        def _(sp):
            sp.dma_start(mask[:], adj).then_inc(const_loaded, 16)
            sp.dma_start(wg[:], Wg.rearrange("(k p) e -> p k e", p=P)).then_inc(const_loaded, 16)
            for k, b in enumerate((bq, bk)):
                for blk in range(KB):
                    sp.dma_start(bqk[:, k, blk:blk + 1], b[blk * P:(blk + 1) * P].unsqueeze(1)).then_inc(
                        const_loaded, 16)
            for dst, b in ((bv_all, bv), (bo_all, bo), (bg_all, bg)):
                sp.dma_start(dst[:], b.partition_broadcast(P)).then_inc(const_loaded, 16)

            def step(base, u, live):
                if live(0):
                    i, k = graph(base, u, 0), u % 8
                    if old(base, u, 0, 8):
                        sp.wait_ge(normed, i - 7)
                    sp.dma_start(xin[:, k, :], x_rows[bass.ds(i * P, P), :]).then_inc(x_loaded[k], 16)
                if live(L_RES):
                    i, k = graph(base, u, L_RES), (u - L_RES) % 2
                    if old(base, u, L_RES, 2):
                        sp.wait_ge(x1_done, i - 1)
                    sp.dma_start(xres[:, k, :], x_rows[bass.ds(i * P, P), :]).then_inc(xres_loaded[k], 16)
                if live(L_SPREAD):
                    i, buf, cols = graph(base, u, L_SPREAD), (u - L_SPREAD) % 2, (u - L_SPREAD) % 2 * P
                    hold(sp, qk_low, i + (2 if buf == 0 else 1))
                    if old(base, u, L_SPREAD, 2):
                        hold(sp, s_mm, (i - 1) * HH)
                    for r in range(RG):
                        rows = slice(r * HEAD_DIM, (r + 1) * HEAD_DIM)
                        sp.dma_start(k_heads[rows, buf, :, :, r, :].bitcast(F32),
                                     k_all[rows, :, :, cols:cols + P].bitcast(F32)).then_inc(
                            k_spread[buf], 16)
                if live(L_X1 + 1):
                    i, k = graph(base, u, L_X1 + 1), (u - L_X1 - 1) % 8
                    sp.wait_ge(x1_done, i + 1)
                    sp.dma_start(x1_dram[bass.ds(i * P, P), :], x1[:, k, :]).then_inc(x1_stored[k], 16)

            run(sp, step)
            for k in range(8):
                sp.wait_ge(x1_stored[k], 16 * (GRAPHS // 8))

        @block.tensor
        def _(pe):
            def step(base, u, live):
                if live(L_S):
                    i, par, cols = graph(base, u, L_S), (u - L_S) // 2 % 2, (u - L_S) % 2 * P
                    pe.wait_ge(k_spread[(u - L_S) % 2], 16 * RG * turns(base, u, L_S, 2))
                    if old(base, u, L_S, 1):
                        pe.wait_ge(max_done, i)
                    for hh in range(HH):
                        for n, (a, b) in enumerate(PASSES):
                            mm = pe.matmul(ps_s[:, hh, :], q[:, a, par, hh, cols:cols + P],
                                           k_heads[:, (u - L_S) % 2, b, hh], start=n == 0, stop=n == len(PASSES) - 1)
                        mm.then_inc(s_mm, 1)
                if live(L_XT):
                    i = graph(base, u, L_XT)
                    pe.wait_ge(normed, i + 1)
                    if old(base, u, L_XT, 1):
                        pe.wait_ge(xT_low, i)
                    if live(L_OT + 1) and old(base, u, L_OT + 1, 0):
                        pe.wait_ge(oT_low, graph(base, u, L_OT + 1) + 1)
                    if live(L_GT + 1) and old(base, u, L_GT + 1, 0):
                        pe.wait_ge(gT_done, graph(base, u, L_GT + 1) + 1)
                    for kb in range(KB):
                        mm = pe.transpose(ps_t[:, kb * P:(kb + 1) * P], xn[:, kb * P:(kb + 1) * P],
                                          ident[:])
                    mm.then_inc(xT_mm, 1)
                if live(L_PV):
                    i = graph(base, u, L_PV)
                    pe.wait_ge(v_done, i + 1)
                    if old(base, u, L_PV, 1):
                        pe.wait_ge(o_done, i)
                    if live(L_TOP + 1):
                        pe.wait_ge(logits_done, graph(base, u, L_TOP + 1) + 1)
                    if live(L_RANK + 1) and (u - L_RANK - 1) % 2 == 1:
                        pe.wait_ge(placed, 2 * pair_of(base, u, L_RANK + 1) + 2)
                    pe.wait_ge(pT_done, i + 1)
                    for h in range(HEADS):
                        mm = pe.matmul(o_ps[:, h, :], probsT[:, h, :], v1[:, (u - L_PV) % 4, h, :],
                                       start=True, stop=True)
                    mm.then_inc(pv_mm, 1)
                if live(L_OT):
                    i, buf = graph(base, u, L_OT), (u - L_OT) % 2
                    pe.wait_ge(o_done, i + 1)
                    if old(base, u, L_OT, 1):
                        pe.wait_ge(oT_low, i)
                    if live(L_XT):
                        pe.wait_ge(xT_low, graph(base, u, L_XT) + 1)
                    if live(L_GT + 1) and old(base, u, L_GT + 1, 0):
                        pe.wait_ge(gT_done, graph(base, u, L_GT + 1) + 1)
                    for kb in range(KB):
                        mm = pe.transpose(ps_t[:, kb * P:(kb + 1) * P], o[:, buf, kb * P:(kb + 1) * P], ident[:])
                    mm.then_inc(oT_mm, 1)
                if live(L_V):
                    i, par, cols = graph(base, u, L_V), (u - L_V) // 2 % 2, (u - L_V) % 2 * P
                    pe.wait_ge(xT_low, i + 1)
                    if old(base, u, L_V, 1):
                        pe.wait_ge(v_done, i)
                    if live(L_X1 + 1) and old(base, u, L_X1 + 1, 0):
                        pe.wait_ge(x1_done, graph(base, u, L_X1 + 1) + 1)
                    for n, (kb, (a, b)) in enumerate((kb, ab) for kb in range(KB) for ab in PASSES):
                        mm = pe.matmul(ps_vo[:, 0, :], xT[a][:, par, kb, cols:cols + P], wall[:, b, 2, kb, :],
                                       start=n == 0, stop=n == 3 * KB - 1)
                    mm.then_inc(v_mm, 1)
                if live(L_PT):
                    i, buf = graph(base, u, L_PT), (u - L_PT) % 2
                    pe.wait_ge(exp_done, i + 1)
                    if old(base, u, L_PT, 1):
                        pe.wait_ge(pT_done, i)
                    for h in range(HEADS):
                        mm = pe.transpose(ps_pT[:, h // RG, h % RG * P:(h % RG + 1) * P], scores[:, buf, h, :], ident[:])
                    mm.then_inc(pT_mm, 1)
                if live(L_QK):
                    i, which, par = graph(base, u, L_QK), (u - L_QK) % 2, (u - L_QK) // 2 % 2
                    pe.wait_ge(xT_low, i + (2 if which == 0 else 1))
                    if old(base, u, L_QK, 1):
                        pe.wait_ge(qk_low, i)
                    for blk in range(KB):
                        for n, (kb, (a, b)) in enumerate((kb, ab) for kb in range(KB) for ab in PASSES):
                            mm = pe.matmul(ps_qk[:, blk, :], wall[:, a, which, kb, blk * P:(blk + 1) * P],
                                           xT[b][:, par, kb, :], start=n == 0, stop=n == 3 * KB - 1)
                    mm.then_inc(qk_mm, 1)
                if live(L_TOP):
                    i, buf = graph(base, u, L_TOP), (u - L_TOP) % 2
                    pe.wait_ge(gT_done, i + 1)
                    if old(base, u, L_TOP, 1):
                        pe.wait_ge(logits_done, i)
                    if live(L_PV):
                        pe.wait_ge(o_done, graph(base, u, L_PV) + 1)
                    else:
                        pe.wait_ge(placed, graph(base, u, L_RANK) // 2 * 2)
                    for kb in range(KB):
                        mm = pe.matmul(gate_ps, gT[:, buf, kb, :], wg[:, kb, :], start=kb == 0, stop=kb == KB - 1)
                    mm.then_inc(gate_mm, 1)
                if live(L_RANK) and (u - L_RANK) % 2 == 1:
                    pair, pp = pair_of(base, u, L_RANK), (u - L_RANK) // 2 % 2
                    pe.wait_ge(either_done, pair + 1)
                    if not live(L_TOP):
                        pe.wait_ge(logits_done, GRAPHS)
                        pe.wait_ge(placed, 2 * pair)
                    pe.matmul(rank_ps[:, 0, :], before[:], either[:, pp, 0, :], start=True, stop=True)
                    pe.matmul(rank_ps[:, 1, :], before[:], either[:, pp, 1, :], start=True, stop=False)
                    pe.matmul(rank_ps[:, 1, :], ones[:], either[:, pp, 0, :], start=False, stop=True)
                    pe.matmul(total_ps, ones[:], either[:, pp, 0, :], start=True, stop=False)
                    pe.matmul(total_ps, ones[:], either[:, pp, 1, :], start=False, stop=True).then_inc(rank_mm, 1)
                if live(L_X1):
                    i, buf = graph(base, u, L_X1), (u - L_X1) % 2
                    pe.wait_ge(oT_low, i + 1)
                    if old(base, u, L_X1, 1):
                        pe.wait_ge(x1_done, i)
                    if live(L_V):
                        pe.wait_ge(v_done, graph(base, u, L_V) + 1)
                    for n, (kb, (a, b)) in enumerate((kb, ab) for kb in range(KB) for ab in PASSES):
                        mm = pe.matmul(ps_vo[:, 1, :], oT[a][:, buf, kb, :], wall[:, b, 3, kb, :],
                                       start=n == 0, stop=n == 3 * KB - 1)
                    mm.then_inc(proj_mm, 1)
                if live(L_GT):
                    i = graph(base, u, L_GT)
                    pe.wait_ge(normed2, i + 1)
                    if live(L_OT):
                        pe.wait_ge(oT_low, graph(base, u, L_OT) + 1)
                    if old(base, u, L_GT, 1):
                        pe.wait_ge(gT_done, i)
                    for kb in range(KB):
                        mm = pe.transpose(ps_t[:, kb * P:(kb + 1) * P],
                                          xn2[:, (u - L_GT) % 8, kb * P:(kb + 1) * P], ident[:])
                    mm.then_inc(gT_mm, 1)

            pe.wait_ge(const_ready, 1)
            pe.wait_ge(consts_pool, 2 + EXPERTS)
            run(pe, step)

        @block.scalar
        def _(act):
            act.wait_ge(const_loaded, 16 * CONSTS)
            act.activation(bqk[:, 0, :], bqk[:, 0, :], ACT.Copy, scale=SCALE).then_inc(const_high, 1)
            act.wait_ge(const_high, 1)

            def step(base, u, live):
                if live(L_XT):
                    i, par, cols = graph(base, u, L_XT), (u - L_XT) // 2 % 2, (u - L_XT) % 2 * P
                    if old(base, u, L_XT, 4):
                        act.wait_ge(v_mm, i - 3)
                        act.wait_ge(qk_mm, i - 2 - (u - L_XT) % 2)
                    act.wait_ge(xT_mm, i + 1)
                    act.activation(xT[HIGH][:, par, :, cols:cols + P],
                                   ps_t[:].rearrange("p (k n) -> p k n", k=KB), ACT.Copy).then_inc(xT_high, 1)
                if live(L_OT):
                    i, buf = graph(base, u, L_OT), (u - L_OT) % 2
                    if old(base, u, L_OT, 2):
                        act.wait_ge(proj_mm, i - 1)
                    act.wait_ge(oT_mm, i + 1)
                    act.activation(oT[HIGH][:, buf], ps_t[:].rearrange("p (k n) -> p k n", k=KB),
                                   ACT.Copy).then_inc(oT_high, 1)
                if live(L_S):
                    i, buf = graph(base, u, L_S), (u - L_S) % 2
                    act.wait_ge(max_done, i + 1)
                    for h in range(RG):
                        act.activation(scores[:, buf, h, :], scores[:, buf, h, :], ACT.Exp,
                                       scale=-1.0, bias=neg_max[:, buf, h:h + 1])
                if live(L_PT):
                    i = graph(base, u, L_PT)
                    if old(base, u, L_PT, 1):
                        act.wait_ge(pv_mm, i)
                    act.wait_ge(pT_mm, i + 1)
                    act.activation(probsT[:], ps_pT[:].rearrange("p b (r n) -> p (b r) n", r=RG),
                                   ACT.Copy).then_inc(pT_done, 1)
                if live(L_S):
                    i, buf = graph(base, u, L_S), (u - L_S) % 2
                    for h in range(RG, HEADS):
                        e = act.activation(scores[:, buf, h, :], scores[:, buf, h, :], ACT.Exp,
                                           scale=-1.0, bias=neg_max[:, buf, h:h + 1])
                    e.then_inc(exp_done, 1)
                if live(L_QK):
                    i, which, par = graph(base, u, L_QK), (u - L_QK) % 2, (u - L_QK) // 2 % 2
                    if which == 0 and old(base, u, L_QK, 4):
                        act.wait_ge(s_mm, (i - 2) * HH)
                    if which == 1 and old(base, u, L_QK, 2):
                        act.wait_ge(k_spread[0], 16 * RG * (turns(base, u, L_QK, 2) - 1))
                        act.wait_ge(k_spread[1], 16 * RG * (turns(base, u, L_QK, 2) - 1))
                    act.wait_ge(qk_mm, i + 1)
                    for blk in range(KB):
                        act.activation(q[:, HIGH, par, blk, :] if which == 0 else k_all[:, HIGH, blk, :],
                                       ps_qk[:, blk, :], ACT.Identity,
                                       bias=bqk[:, which, blk:blk + 1]).then_inc(qk_high, 1)
                if live(L_GT):
                    i, buf = graph(base, u, L_GT), (u - L_GT) % 2
                    if old(base, u, L_GT, 2):
                        act.wait_ge(gate_mm, i - 1)
                    act.wait_ge(gT_mm, i + 1)
                    act.activation(gT[:, buf], ps_t[:].rearrange("p (k n) -> p k n", k=KB),
                                   ACT.Copy).then_inc(gT_done, 1)

            run(act, step)

        @block.vector
        def _(dve):
            dve.wait_ge(const_loaded, 16 * CONSTS)
            dve.wait_ge(const_high, 1)
            dve.tensor_scalar(mask[:], mask[:], -1.0, 1.0, ALU.mult, ALU.add).then_inc(const_low, 1)
            dve.wait_ge(const_low, 1)
            dve.tensor_scalar(mask[:], mask[:], MASKED, None, ALU.mult).then_inc(const_low, 1)
            dve.memset(v1[:], 1.0).then_inc(const_low, 1)
            dve.memset(k_heads[:].bitcast(F32), 0.0).then_inc(const_low, 1)
            dve.memset(counts[:], 0.0).then_inc(const_low, 1)
            dve.wait_ge(const_low, 5)
            dve.wait_ge(consts_pool, 2 + EXPERTS)
            dve.tensor_scalar(count_rows[:], expert_id[:], float(CAP), None, ALU.mult).then_inc(const_ready, 1)
            dve.wait_ge(const_ready, 1)

            def step(base, u, live):
                if live(L_XT):
                    i, par, cols = graph(base, u, L_XT), (u - L_XT) // 2 % 2, (u - L_XT) % 2 * P
                    dve.wait_ge(xT_high, i + 1)
                    dve.tensor_tensor(xT[LOW][:, par, :, cols:cols + P],
                                      ps_t[:].rearrange("p (k n) -> p k n", k=KB),
                                      xT[HIGH][:, par, :, cols:cols + P], ALU.subtract).then_inc(xT_low, 1)
                if live(L_S):
                    i, buf = graph(base, u, L_S), (u - L_S) % 2
                    if old(base, u, L_S, 2):
                        hold(dve, pT_mm, i - 1)
                    for h in range(HEADS):
                        hh, r = h // RG, h % RG
                        if r == 0:
                            hold(dve, s_mm, i * HH + hh + 1)
                        m = dve.tensor_tensor_reduce(
                            scores[:, buf, h, :], ps_s[:, hh, r * P:(r + 1) * P], mask[:], -1.0, 3.0e38,
                            ALU.add, ALU.min, neg_max[:, buf, h:h + 1])
                    m.then_inc(max_done, 1)
                if live(L_PV):
                    i, buf = graph(base, u, L_PV), (u - L_PV) % 2
                    dve.wait_ge(pv_mm, i + 1)
                    dve.reciprocal(denom[:, buf, :], o_ps[:, :, HEAD_DIM]).then_inc(denom_done, 1)
                    if old(base, u, L_PV, 2):
                        dve.wait_ge(oT_mm, i - 1)
                    dve.wait_ge(denom_done, i + 1)
                    dve.tensor_tensor(o[:, buf, :].rearrange("p (h c) -> p h c", c=HEAD_DIM),
                                      o_ps[:, :, 0:HEAD_DIM],
                                      denom[:, buf, :].unsqueeze(2).broadcast_to([P, HEADS, HEAD_DIM]),
                                      ALU.mult).then_inc(o_done, 1)
                if live(L_OT):
                    i, buf = graph(base, u, L_OT), (u - L_OT) % 2
                    dve.wait_ge(oT_high, i + 1)
                    dve.tensor_tensor(oT[LOW][:, buf], ps_t[:].rearrange("p (k n) -> p k n", k=KB),
                                      oT[HIGH][:, buf], ALU.subtract).then_inc(oT_low, 1)
                if live(L_V):
                    i, buf = graph(base, u, L_V), (u - L_V) % 4
                    if old(base, u, L_V, 4):
                        dve.wait_ge(pv_mm, i - 3)
                    dve.wait_ge(v_mm, i + 1)
                    dve.tensor_tensor(v1[:, buf, :, 0:HEAD_DIM],
                                      ps_vo[:, 0, :].rearrange("p (h c) -> p h c", c=HEAD_DIM),
                                      bv_all[:].rearrange("p (h c) -> p h c", c=HEAD_DIM),
                                      ALU.add).then_inc(v_done, 1)
                if live(L_NORM):
                    i, k = graph(base, u, L_NORM), (u - L_NORM) % 4
                    hold(dve, newton_done, newton_run(base, u, L_NORM, L_NEWTON))
                    if old(base, u, L_NORM, 1):
                        hold(dve, xT_mm, i)
                    dve.tensor_scalar(xn[:], xin[:, (u - L_NORM) % 8, :], moments[:, 0, k, 0:1],
                                      rstd[:, 0, k:k + 1], ALU.subtract, ALU.mult).then_inc(normed, 1)
                if live(L_NORM2):
                    i, k = graph(base, u, L_NORM2), (u - L_NORM2) % 8
                    m = (k + 2) % 4
                    hold(dve, newton_done, newton_run(base, u, L_NORM2, L_NEWTON2))
                    if old(base, u, L_NORM2, 8):
                        hold(dve, scattered[k // 2], 64 * (turns(base, u, L_NORM2, 8) - 1))
                    dve.tensor_scalar(xn2[:, k, :], x1[:, k, :], moments[:, 1, m, 0:1],
                                      rstd[:, 1, m:m + 1], ALU.subtract, ALU.mult).then_inc(normed2, 1)
                if live(L_STATS2):
                    i, k = graph(base, u, L_STATS2), (u - L_STATS2) % 8
                    dve.wait_ge(x1_done, i + 1)
                    dve.bn_stats(stats2[:, k % 4, :], x1[:, k, :]).then_inc(stats2_done, 1)
                if live(L_STATS):
                    i, k = graph(base, u, L_STATS), (u - L_STATS) % 8
                    dve.wait_ge(x_loaded[k], 16 * turns(base, u, L_STATS, 8))
                    dve.bn_stats(stats[:, k % 4, :], xin[:, k, :]).then_inc(stats_done, 1)
                if live(L_BEST):
                    i, k = graph(base, u, L_BEST), (u - L_BEST) % 4
                    hold(dve, logits_done, i + 1)
                    dve.max(top8[:, k, :], logits[:, k, :]).then_inc(chain_dve, 1)
                if live(L_STATS2):
                    i, k = graph(base, u, L_STATS2), (u - L_STATS2) % 4
                    hold(dve, stats2_done, i + 1)
                    dve.bn_aggr(moments[:, 1, (k + 2) % 4, :], stats2[:, k, :]).then_inc(moments2_done, 1)
                if live(L_BEST):
                    i, k = graph(base, u, L_BEST), (u - L_BEST) % 4
                    hold(dve, chain_dve, i + 1)
                    dve.max_index(top8_at[:, k, :], top8[:, k, :], logits[:, k, :]).then_inc(top_done, 1)
                    dve.tensor_copy(top_scores[:, :, bass.ds(i, 1)], top8[:, k, 0:TOP_K].unsqueeze(2))
                if live(L_STATS):
                    i, k = graph(base, u, L_STATS), (u - L_STATS) % 4
                    hold(dve, stats_done, i + 1)
                    dve.bn_aggr(moments[:, 0, k, :], stats[:, k, :]).then_inc(moments_done, 1)
                if live(L_BEST) and (u - L_BEST) % 2 == 1:
                    i, pair = graph(base, u, L_BEST), pair_of(base, u, L_BEST)
                    pp, k = (u - L_BEST) // 2 % 2, (u - L_BEST) % 4 - 1
                    dve.wait_ge(top_done, i + 1)
                    dve.tensor_copy(top_at[:, pp], top8_at[:, k:k + 2, 0:TOP_K]).then_inc(chosen_done, 1)
                    dve.wait_ge(chosen_done, 3 * pair + 1)
                    for c in range(TOP_K):
                        dve.tensor_tensor(
                            chosen[:, pp, c], expert_id[:].unsqueeze(1).broadcast_to([P, 2, EXPERTS]),
                            top_at[:, pp, :, c].unsqueeze(2).broadcast_to([P, 2, EXPERTS]),
                            ALU.is_equal).then_inc(chosen_done, 1)
                    dve.wait_ge(chosen_done, 3 * pair + 3)
                    dve.tensor_tensor(either[:, pp], chosen[:, pp, 0], chosen[:, pp, 1],
                                      ALU.add).then_inc(either_done, 1)
                if live(L_TOP):
                    i, k = graph(base, u, L_TOP), (u - L_TOP) % 4
                    if live(L_RANK) and (u - L_RANK) % 2 == 1:
                        dve.wait_ge(rank_mm, pair_of(base, u, L_RANK) + 1)
                    dve.wait_ge(gate_mm, i + 1)
                    dve.tensor_tensor(logits[:, k, :], gate_ps, bg_all[:],
                                      ALU.add).then_inc(logits_done, 1)
                if live(L_X1):
                    i, k = graph(base, u, L_X1), (u - L_X1) % 8
                    if old(base, u, L_X1, 8):
                        dve.wait_ge(x1_stored[k], 16 * turns(base, u, L_X1, 8) - 16)
                    dve.wait_ge(xres_biased, i + 1)
                    dve.wait_ge(proj_mm, i + 1)
                    dve.tensor_tensor(x1[:, k, :], ps_vo[:, 1, :], xres[:, k % 2, :], ALU.add).then_inc(x1_done, 1)
                if live(L_QK):
                    i, which, par = graph(base, u, L_QK), (u - L_QK) % 2, (u - L_QK) // 2 % 2
                    dve.wait_ge(qk_high, KB * i + KB)
                    for blk in range(KB):
                        high, low = ((q[:, HIGH, par, blk, :], q[:, LOW, par, blk, :]) if which == 0 else
                                     (k_all[:, HIGH, blk, :], k_all[:, LOW, blk, :]))
                        rest = dve.scalar_tensor_tensor(out=low, in0=ps_qk[:, blk, :],
                                                        scalar=bqk[:, which, blk:blk + 1], in1=high,
                                                        op0=ALU.add, op1=ALU.subtract)
                    rest.then_inc(qk_low, 1)
                if live(L_SLOT) and (u - L_SLOT) % 2 == 1:
                    i, pair = graph(base, u, L_SLOT), pair_of(base, u, L_SLOT)
                    pp, k = (u - L_SLOT) // 2 % 2, (u - L_SLOT) // 2 % 4
                    if old(base, u, L_SLOT, 8):
                        dve.wait_ge(scattered[k], 16 * 4 * (turns(base, u - 1, L_SLOT, 8) - 1))
                    dve.wait_ge(rank_mm, pair + 1)
                    dve.tensor_tensor(place[:, pp], rank_ps,
                                      count_rows[:].unsqueeze(1).broadcast_to([P, 2, EXPERTS]),
                                      ALU.add).then_inc(placed, 1)
                    dve.tensor_tensor(counts[:], total_ps, counts[:], ALU.add)
                    dve.wait_ge(placed, 2 * pair + 1)
                    dve.tensor_tensor(count_rows[:], total_ps, count_rows[:], ALU.add).then_inc(placed, 1)
                    for c in range(TOP_K):
                        dve.tensor_tensor(picked[:, pp, c], chosen[:, pp, c], place[:, pp],
                                          ALU.mult).then_inc(chain_slot, 1)
                    dve.wait_ge(chain_slot, 3 * pair + 2)
                    dve.tensor_reduce(slot_f[:, pp], picked[:, pp], AX.X, ALU.add).then_inc(chain_slot, 1)
                    dve.wait_ge(chain_slot, 3 * pair + 3)
                    dve.tensor_copy(slot_i[:, k], slot_f[:, pp]).then_inc(slot_done, 1)
                    dve.tensor_copy(slots[:, :, bass.ds(graph(base, u, L_SLOT + 1), 2)], slot_f[:, pp])

            run(dve, step)

        @block.gpsimd
        def _(pool):
            pool.memset(before[:], 1.0).then_inc(chain_pool, 1)
            pool.wait_ge(chain_pool, 1)
            pool.affine_select(out=before[:], in_=before[:], compare_op=ALU.is_gt, fill=0.0, base=0,
                               pattern=[[1, P]], channel_multiplier=-1).then_inc(consts_pool, 1)
            pool.memset(ones[:], 1.0).then_inc(consts_pool, 1)
            for e in range(EXPERTS):
                pool.memset(expert_id[:, e:e + 1], float(e)).then_inc(consts_pool, 1)
            pool.wait_ge(const_loaded, 16 * CONSTS)

            ROUND = 14

            def rsqrt(run_before, var, root, shifted, square):
                n = [0]

                def then(instruction):
                    n[0] += 1
                    if n[0] == ROUND:
                        instruction.then_inc(newton_done, 1)
                    else:
                        instruction.then_inc(newton_step, 1)
                        hold(pool, newton_step, run_before * (ROUND - 1) + n[0])

                then(pool.tensor_scalar(shifted, var, EPS, None, ALU.add))
                then(pool.tensor_scalar(root.bitcast(I32), shifted.bitcast(I32), -0.5, RSQRT_MAGIC,
                                        ALU.mult, ALU.add))
                for _ in range(3):
                    then(pool.tensor_tensor(square, root, root, ALU.mult))
                    then(pool.tensor_tensor(square, square, shifted, ALU.mult))
                    then(pool.tensor_scalar(square, square, -0.5, 1.5, ALU.mult, ALU.add))
                    then(pool.tensor_tensor(root, square, root, ALU.mult))
                assert n[0] == ROUND

            def step(base, u, live):
                if (live(L_NEWTON) or live(L_NEWTON2)) and u % 2 == 0:
                    norms = slice(0 if live(L_NEWTON) else 1, 2 if live(L_NEWTON2) else 1)
                    if live(L_NEWTON):
                        hold(pool, moments_done, graph(base, u, L_NEWTON) + 2)
                    if live(L_NEWTON2):
                        hold(pool, moments2_done, graph(base, u, L_NEWTON2) + 2)
                    k = (u - L_NEWTON) % 4
                    rsqrt(pair_of(base, u, L_NEWTON), moments[:, norms, k:k + 2, 1], rstd[:, norms, k:k + 2],
                          newton[:, 0, norms, :], newton[:, 1, norms, :])
                if live(L_X1):
                    k = (u - L_X1) % 2
                    pool.wait_ge(xres_loaded[k], 16 * turns(base, u, L_X1, 2))
                    pool.tensor_tensor(xres[:, k, :], xres[:, k, :], bo_all[:], ALU.add).then_inc(xres_biased, 1)
                if live(L_SLOT) and (u - L_SLOT) % 2 == 1:
                    i, pair = graph(base, u, L_SLOT), pair_of(base, u, L_SLOT)
                    k = (u - L_SLOT) // 2 % 4
                    hold(pool, slot_done, pair + 1)
                    for g in range(2):
                        for c in range(TOP_K):
                            pool.indirect_dma_start(
                                rows_dram, bass.IndirectOffsetOnAxis(slot_i[:, k, c, g:g + 1], axis=0),
                                xn2[:, (u - L_SLOT - 1 + g) % 8, :], None).then_inc(scattered[k], 16)

            run(pool, step)
            for k in range(4):
                pool.wait_ge(scattered[k], 64 * (GRAPHS // 8))


def experts(nc, b1, b2, w1, w2, ident, counts, count_rows, slots, outputs_at, rows_dram, expert_dram, EXPERTS, D, HID, CAP,
            TILES, FEWEST_TILES):
    KB, HB = D // P, HID // P
    UNROLL = 8
    L_XT, L_F1, L_HT, L_F2, L_STORE = 3, 4, 5, 6, 7
    GROUP, BITS = UNROLL, 3
    GROUPS = TILES // GROUP + 2
    ENTRIES = GROUPS * GROUP
    assert EXPERTS <= 2 ** BITS and GROUP * BITS <= 24 and L_F2 <= GROUP
    LAST_ROW = EXPERTS * CAP + (TILES - FEWEST_TILES - 1) * P
    HEAD_STEPS = -(-L_STORE // UNROLL) * UNROLL
    assert TILES % UNROLL == 0
    with ExitStack() as ctx:
        def sb(name, shape, dt=F32):
            return ctx.enter_context(nc.sbuf_tensor(name, shape, dt))

        def pb(name, shape):
            return ctx.enter_context(nc.psum_tensor(name, shape, F32))

        def sem(name):
            return ctx.enter_context(nc.semaphore(name))

        b1_all = sb("b1_all", [P, EXPERTS, HID])
        b2_all = sb("b2_all", [P, EXPERTS, D])
        zeros = sb("zeros", [P, D])
        tile_i = sb("tile_i", [1, ENTRIES], I32)
        tile_f = sb("tile_f", [1, ENTRIES])
        past = sb("past", [1, ENTRIES])
        tile_expert_f = sb("tile_expert_f", [1, ENTRIES])
        tile_first = sb("tile_first", [1, ENTRIES])
        tile_row_f = sb("tile_row_f", [1, ENTRIES])
        place_value = sb("place_value", [1, GROUPS, GROUP])
        packed_f = sb("packed_f", [1, GROUPS])
        tile_experts = sb("tile_experts", [1, GROUPS], I32)
        tile_row = sb("tile_row", [1, ENTRIES], I32)
        count_i = sb("count_i", [P, EXPERTS], I32)
        tiles_of = sb("tiles_of", [P, EXPERTS])
        jump = sb("jump", [P, EXPERTS])
        closer = sb("closer", list(slots.shape))
        moved_slots = sb("moved_slots", list(slots.shape))
        tiles_upto = sb("tiles_upto", [1, EXPERTS])
        pad_row = sb("pad_row", [1, EXPERTS], I32)
        rows = sb("rows", [P, 4, D])
        xT = [sb(f"rowsT{h}", [P, 2, KB, P], F32R) for h in (HIGH, LOW)]
        biased = sb("biased", [P, 2, HID])
        hidden = sb("hidden", [P, 2, HID])
        hT = [sb(f"hT{h}", [P, 2, HB, P], F32R) for h in (HIGH, LOW)]
        y = sb("y", [P, 4, D])
        ps_xT = pb("ps_xT", [P, 2, 512])
        ps_h = pb("ps_h", [P, 2, 512])
        ps_hT = pb("ps_hT", [P, 2, 512])
        ps_y = pb("ps_y", [P, 2, 512])

        bias_loaded, padded = sem("bias_loaded"), sem("padded")
        rows_loaded = [sem(f"rows_loaded{k}") for k in range(4)]
        y_stored = [sem(f"y_stored{k}") for k in range(4)]
        (tile_iota, zeros_done, moved, table_step, table_done, xT_mm, xT_high, xT_low, h_mm, h_biased, gelu_done,
         hT_mm, hT_high, hT_low, y_mm, y_done) = (sem("e_" + n) for n in (
             "tile_iota zeros_done moved table_step table_done xT_mm xT_high xT_low h_mm h_biased gelu_done "
             "hT_mm hT_high hT_low y_mm y_done").split())

        def run(eng, step):
            for t in range(HEAD_STEPS):
                step(t // UNROLL, t % UNROLL, lambda lag: t >= lag)
            with eng.Fori(HEAD_STEPS // UNROLL, TILES // UNROLL) as base:
                for u in range(UNROLL):
                    step(base, u, lambda lag: True)
            for t in range(TILES, TILES + L_STORE + 1):
                step(t // UNROLL, t % UNROLL, lambda lag: t - lag < TILES)

        def tile(base, u, lag):
            return base * UNROLL + (u - lag)

        def turns(base, u, lag, ring):
            return base * (UNROLL // ring) + ((u - lag) // ring + 1)

        def old(base, u, lag, back):
            return not isinstance(base, int) or tile(base, u, lag) >= back

        block = ctx.enter_context(nc.Block())

        @block.gpsimd
        def _(pool):
            pool.iota(tile_i[:], pattern=[[1, ENTRIES]], base=-GROUP, channel_multiplier=0).then_inc(tile_iota, 1)
            pool.memset(zeros[:], 0.0).then_inc(zeros_done, 1)
            pool.wait_ge(table_done, 1)
            for e in range(1, EXPERTS):
                if e > 1:
                    pool.wait_ge(moved, 2 * e - 2)
                pool.tensor_scalar(closer[:], slots[:], float(e * CAP), jump[:, e - 1:e], ALU.is_ge,
                                   ALU.mult).then_inc(moved, 1)
                pool.wait_ge(moved, 2 * e - 1)
                pool.tensor_tensor(moved_slots[:], (slots if e == 1 else moved_slots)[:], closer[:],
                                   ALU.add).then_inc(moved, 1)
            pool.wait_ge(moved, 2 * EXPERTS - 2)
            pool.tensor_copy(outputs_at[:], moved_slots[:]).then_inc(moved, 1)

        @block.sync
        def _(sp):
            sp.wait_ge(zeros_done, 1)
            for n in range(TILES - FEWEST_TILES):
                at = EXPERTS * CAP + n * P
                sp.dma_start(rows_dram[at:at + P, :], zeros[:]).then_inc(padded, 16)
            sp.wait_ge(table_done, 1)
            for e in range(EXPERTS):
                at = sp.value_load(pad_row[0:1, e:e + 1], min_val=e * CAP, max_val=(e + 1) * CAP - P)
                sp.dma_start(rows_dram[bass.ds(at, P), :], zeros[:]).then_inc(padded, 16)
            sp.wait_ge(padded, 16 * (TILES - FEWEST_TILES + EXPERTS))

            def step(base, u, live):
                if u == 0:
                    starts[:] = nc.values_load_multi_w_load_instructions(
                        tile_row[0:1, bass.ds(base * UNROLL + GROUP, UNROLL)], engines=[mybir.EngineType.SP],
                        min_val=0, max_val=LAST_ROW)[1]
                if live(L_STORE):
                    j, k = tile(base, u, L_STORE), (u - L_STORE) % 4
                    sp.wait_ge(y_done, j + 1)
                    sp.dma_start(expert_dram[bass.ds(j * P, P), :], y[:, k, :]).then_inc(y_stored[k], 16)
                if live(0):
                    j, k = tile(base, u, 0), u % 4
                    if old(base, u, 0, 4):
                        sp.wait_ge(xT_mm, j - 3)
                    sp.dma_start(rows[:, k, :], rows_dram[bass.ds(starts[u], P), :]).then_inc(rows_loaded[k], 16)

            starts = []
            run(sp, step)
            for k in range(4):
                sp.wait_ge(y_stored[k], 16 * (TILES // 4))

        def load_experts(engine, base):
            packed = nc.values_load_multi_w_load_instructions(
                tile_experts[0:1, bass.ds(base, 2)], engines=[engine], min_val=0,
                max_val=2 ** (GROUP * BITS) - 1)[1]
            return [number // 2 ** (BITS * n) % 2 ** BITS for number in packed for n in range(GROUP)]

        @block.tensor
        def _(pe):
            def step(base, u, live):
                if u == 0:
                    experts_of[:] = load_experts(mybir.EngineType.PE, base)
                if live(L_F1):
                    j, buf = tile(base, u, L_F1), (u - L_F1) % 2
                    e = experts_of[GROUP + u - L_F1]
                    pe.wait_ge(xT_low, j + 1)
                    if old(base, u, L_F1, 2):
                        pe.wait_ge(h_biased, j - 1)
                    for n, (kb, (a, b)) in enumerate((kb, ab) for kb in range(KB) for ab in PASSES):
                        mm = pe.matmul(ps_h[:, buf, 0:HID], xT[a][:, buf, kb, :],
                                       w1[:, b, bass.ds(e, 1), kb * HID:(kb + 1) * HID],
                                       start=n == 0, stop=n == 3 * KB - 1)
                    mm.then_inc(h_mm, 1)
                if live(L_XT):
                    j, buf, k = tile(base, u, L_XT), (u - L_XT) % 2, (u - L_XT) % 4
                    pe.wait_ge(rows_loaded[k], 16 * turns(base, u, L_XT, 4))
                    if old(base, u, L_XT, 2):
                        pe.wait_ge(xT_low, j - 1)
                    for kb in range(KB):
                        mm = pe.transpose(ps_xT[:, buf, kb * P:(kb + 1) * P], rows[:, k, kb * P:(kb + 1) * P],
                                          ident[:])
                    mm.then_inc(xT_mm, 1)
                if live(L_HT):
                    j, buf = tile(base, u, L_HT), (u - L_HT) % 2
                    pe.wait_ge(gelu_done, j + 1)
                    if old(base, u, L_HT, 2):
                        pe.wait_ge(hT_low, j - 1)
                    for hb in range(HB):
                        mm = pe.transpose(ps_hT[:, buf, hb * P:(hb + 1) * P], hidden[:, buf, hb * P:(hb + 1) * P],
                                          ident[:])
                    mm.then_inc(hT_mm, 1)
                if live(L_F2):
                    j, buf = tile(base, u, L_F2), (u - L_F2) % 2
                    e = experts_of[GROUP + u - L_F2]
                    pe.wait_ge(hT_low, j + 1)
                    if old(base, u, L_F2, 2):
                        pe.wait_ge(y_done, j - 1)
                    for n, (hb, (a, b)) in enumerate((hb, ab) for hb in range(HB) for ab in PASSES):
                        mm = pe.matmul(ps_y[:, buf, 0:D], hT[a][:, buf, hb, :],
                                       w2[:, b, bass.ds(e, 1), hb * D:(hb + 1) * D],
                                       start=n == 0, stop=n == 3 * HB - 1)
                    mm.then_inc(y_mm, 1)

            experts_of = []
            pe.wait_ge(table_done, 1)
            run(pe, step)

        @block.scalar
        def _(act):
            def step(base, u, live):
                if live(L_XT):
                    j, buf = tile(base, u, L_XT), (u - L_XT) % 2
                    if old(base, u, L_XT, 2):
                        act.wait_ge(h_mm, j - 1)
                    act.wait_ge(xT_mm, j + 1)
                    act.activation(xT[HIGH][:, buf], ps_xT[:, buf, 0:KB * P].rearrange("p (k n) -> p k n", k=KB),
                                   ACT.Copy).then_inc(xT_high, 1)
                if live(L_HT):
                    j, buf = tile(base, u, L_HT), (u - L_HT) % 2
                    if old(base, u, L_HT, 2):
                        act.wait_ge(y_mm, j - 1)
                    act.wait_ge(hT_mm, j + 1)
                    act.activation(hT[HIGH][:, buf], ps_hT[:, buf, 0:HID].rearrange("p (k n) -> p k n", k=HB),
                                   ACT.Copy).then_inc(hT_high, 1)
                if live(L_F1):
                    j, buf = tile(base, u, L_F1), (u - L_F1) % 2
                    if old(base, u, L_F1, 2):
                        act.wait_ge(hT_mm, j - 1)
                    act.wait_ge(h_biased, j + 1)
                    act.activation(hidden[:, buf, :], biased[:, buf, :], ACT.Gelu).then_inc(gelu_done, 1)

            act.dma_start(b1_all[:], b1.partition_broadcast(P)).then_inc(bias_loaded, 16)
            act.dma_start(b2_all[:], b2.partition_broadcast(P)).then_inc(bias_loaded, 16)
            run(act, step)

        @block.vector
        def _(dve):
            n = [0]

            def then(instruction):
                instruction.then_inc(table_step, 1)
                n[0] += 1
                dve.wait_ge(table_step, n[0])

            for g in range(GROUP):
                then(dve.memset(place_value[:, :, g:g + 1], float(2 ** (BITS * g))))
            dve.wait_ge(tile_iota, 1)
            then(dve.tensor_copy(tile_f[:], tile_i[:]))
            then(dve.tensor_copy(pad_row[:], count_rows[0:1, :]))
            then(dve.tensor_scalar(tiles_of[:], counts[:], float(P - 1), None, ALU.add))
            then(dve.tensor_copy(count_i[:], tiles_of[:]))
            then(dve.tensor_scalar(count_i[:], count_i[:], 7, None, ALU.logical_shift_right))
            then(dve.tensor_copy(tiles_of[:], count_i[:]))
            then(dve.tensor_scalar(jump[:], tiles_of[:], float(P), -float(CAP), ALU.mult, ALU.add))
            then(dve.tensor_copy(tiles_upto[:], tiles_of[0:1, :]))
            for e in range(1, EXPERTS):
                then(dve.tensor_tensor(tiles_upto[:, e:e + 1], tiles_upto[:, e - 1:e], tiles_of[0:1, e:e + 1], ALU.add))
            then(dve.memset(tile_expert_f[:], 0.0))
            then(dve.memset(tile_first[:], 0.0))
            for e in range(EXPERTS):
                then(dve.tensor_scalar(past[:], tile_f[:], tiles_upto[:, e:e + 1], None, ALU.is_ge))
                then(dve.tensor_tensor(tile_expert_f[:], tile_expert_f[:], past[:], ALU.add))
                then(dve.scalar_tensor_tensor(out=tile_first[:], in0=past[:], scalar=tiles_of[0:1, e:e + 1],
                                              in1=tile_first[:], op0=ALU.mult, op1=ALU.add))
            then(dve.tensor_tensor(tile_f[:], tile_f[:], tile_first[:], ALU.subtract))
            then(dve.tensor_scalar(tile_f[:], tile_f[:], float(P), None, ALU.mult))
            then(dve.scalar_tensor_tensor(out=tile_row_f[:], in0=tile_expert_f[:], scalar=float(CAP),
                                          in1=tile_f[:], op0=ALU.mult, op1=ALU.add))
            then(dve.tensor_scalar(tile_row_f[:], tile_row_f[:], 0.0, float(LAST_ROW), ALU.max, ALU.min))
            then(dve.tensor_copy(tile_row[:], tile_row_f[:]))
            then(dve.tensor_scalar(tile_expert_f[:], tile_expert_f[:], float(EXPERTS - 1), None, ALU.min))
            then(dve.tensor_tensor(place_value[:], place_value[:], tile_expert_f[:].rearrange("o (g n) -> o g n", n=GROUP),
                                   ALU.mult))
            then(dve.tensor_reduce(packed_f[:], place_value[:], AX.X, ALU.add))
            dve.tensor_copy(tile_experts[:], packed_f[:]).then_inc(table_done, 1)
            dve.wait_ge(table_done, 1)
            dve.wait_ge(bias_loaded, 32)

            def step(base, u, live):
                if u == 0:
                    experts_of[:] = load_experts(mybir.EngineType.DVE, base)
                if live(L_F1):
                    j, buf = tile(base, u, L_F1), (u - L_F1) % 2
                    e = experts_of[GROUP + u - L_F1]
                    if old(base, u, L_F1, 2):
                        dve.wait_ge(gelu_done, j - 1)
                    dve.wait_ge(h_mm, j + 1)
                    dve.tensor_tensor(biased[:, buf, :].unsqueeze(1), ps_h[:, buf, 0:HID].unsqueeze(1),
                                      b1_all[:, bass.ds(e, 1), :], ALU.add).then_inc(h_biased, 1)
                if live(L_XT):
                    j, buf = tile(base, u, L_XT), (u - L_XT) % 2
                    dve.wait_ge(xT_high, j + 1)
                    dve.tensor_tensor(xT[LOW][:, buf], ps_xT[:, buf, 0:KB * P].rearrange("p (k n) -> p k n", k=KB),
                                      xT[HIGH][:, buf], ALU.subtract).then_inc(xT_low, 1)
                if live(L_HT):
                    j, buf = tile(base, u, L_HT), (u - L_HT) % 2
                    dve.wait_ge(hT_high, j + 1)
                    dve.tensor_tensor(hT[LOW][:, buf], ps_hT[:, buf, 0:HID].rearrange("p (k n) -> p k n", k=HB),
                                      hT[HIGH][:, buf], ALU.subtract).then_inc(hT_low, 1)
                if live(L_F2):
                    j, buf, k = tile(base, u, L_F2), (u - L_F2) % 2, (u - L_F2) % 4
                    e = experts_of[GROUP + u - L_F2]
                    if old(base, u, L_F2, 4):
                        dve.wait_ge(y_stored[k], 16 * (turns(base, u, L_F2, 4) - 1))
                    dve.wait_ge(y_mm, j + 1)
                    dve.tensor_tensor(y[:, k, :].unsqueeze(1), ps_y[:, buf, 0:D].unsqueeze(1),
                                      b2_all[:, bass.ds(e, 1), :], ALU.add).then_inc(y_done, 1)

            experts_of = []
            run(dve, step)


def combine(nc, outputs_at, top_scores, x1_dram, expert_dram, out_rows, GRAPHS, D):
    UNROLL = 4
    with ExitStack() as ctx:
        def sb(name, shape, dt=F32):
            return ctx.enter_context(nc.sbuf_tensor(name, shape, dt))

        def sem(name):
            return ctx.enter_context(nc.semaphore(name))

        gates = sb("gates", [P, TOP_K, GRAPHS])
        gate_sum = sb("gate_sum", [P, GRAPHS])
        index = sb("index", [P, 4, TOP_K], I32)
        x1 = sb("c_x1", [P, 4, D])
        y = sb("c_y", [P, 4, TOP_K, D])
        part = sb("part", [P, 4, D])
        total = sb("total", [P, 4, D])
        x1_loaded = [sem(f"c_x1_loaded{k}") for k in range(4)]
        y_gathered = [sem(f"c_y_gathered{k}") for k in range(4)]
        out_stored = [sem(f"out_stored{k}") for k in range(4)]
        gate_step, gate_exp, gates_done, index_done, part_done, total_done, held = (sem("c_" + n) for n in (
            "gate_step gate_exp gates_done index_done part_done total_done held").split())

        block = ctx.enter_context(nc.Block())

        @block.sync
        def _(sp):
            def load(i, k, again):
                if again:
                    sp.wait_ge(part_done, i - 3)
                sp.dma_start(x1[:, k, :], x1_dram[bass.ds(i * P, P), :]).then_inc(x1_loaded[k], 16)

            def store(i, k):
                sp.wait_ge(total_done, i + 1)
                sp.dma_start(out_rows[bass.ds(i * P, P), :], total[:, k, :]).then_inc(out_stored[k], 16)

            for i in range(4):
                load(i, i, False)
            with sp.Fori(1, GRAPHS // UNROLL) as base:
                for u in range(UNROLL):
                    store(base * UNROLL + (u - UNROLL), u)
                    load(base * UNROLL + u, u, True)
            for i in range(GRAPHS - 4, GRAPHS):
                store(i, i % 4)
            for k in range(4):
                sp.wait_ge(out_stored[k], 16 * (GRAPHS // 4))

        @block.gpsimd
        def _(pool):
            def gather(base, u, again):
                i = base * UNROLL + u
                if again:
                    pool.wait_ge(total_done, i - 3)
                    pool.sem_inc(held, 1)
                pool.tensor_copy(index[:, u, :].unsqueeze(2), outputs_at[:, :, bass.ds(i, 1)]).then_inc(index_done, 1)
                pool.wait_ge(index_done, i + 1)
                pool.sem_inc(held, 1)
                for c in range(TOP_K):
                    pool.indirect_dma_start(y[:, u, c, :], None, expert_dram,
                                            bass.IndirectOffsetOnAxis(index[:, u, c:c + 1], axis=0)).then_inc(
                                                y_gathered[u], 16)

            for u in range(4):
                gather(0, u, False)
            with pool.Fori(1, GRAPHS // UNROLL) as base:
                for u in range(UNROLL):
                    gather(base, u, True)

        @block.scalar
        def _(act):
            act.wait_ge(gate_step, 1)
            act.activation(gates[:, 1, :], gate_sum[:], ACT.Exp).then_inc(gate_exp, 1)

        @block.vector
        def _(dve):
            dve.tensor_tensor(gate_sum[:], top_scores[:, 1, :], top_scores[:, 0, :], ALU.subtract).then_inc(gate_step, 1)
            dve.wait_ge(gate_exp, 1)
            dve.tensor_scalar(gate_sum[:], gates[:, 1, :], 1.0, None, ALU.add).then_inc(gate_step, 1)
            dve.wait_ge(gate_step, 2)
            dve.reciprocal(gates[:, 0, :], gate_sum[:]).then_inc(gate_step, 1)
            dve.wait_ge(gate_step, 3)
            dve.tensor_tensor(gates[:, 1, :], gates[:, 1, :], gates[:, 0, :], ALU.mult).then_inc(gates_done, 1)
            dve.wait_ge(gates_done, 1)

            def add(base, u, again):
                i = base * UNROLL + u
                n = base
                if again:
                    dve.wait_ge(out_stored[u], n * 16)
                dve.wait_ge(x1_loaded[u], n * 16 + 16)
                dve.wait_ge(y_gathered[u], n * 32 + 32)
                dve.scalar_tensor_tensor(out=part[:, u, :], in0=y[:, u, 0, :], scalar=gates[:, 0, bass.ds(i, 1)],
                                         in1=x1[:, u, :], op0=ALU.mult, op1=ALU.add).then_inc(part_done, 1)
                dve.wait_ge(part_done, i + 1)
                dve.scalar_tensor_tensor(out=total[:, u, :], in0=y[:, u, 1, :], scalar=gates[:, 1, bass.ds(i, 1)],
                                         in1=part[:, u, :], op0=ALU.mult, op1=ALU.add).then_inc(total_done, 1)

            for u in range(4):
                add(0, u, False)
            with dve.Fori(1, GRAPHS // UNROLL) as base:
                for u in range(UNROLL):
                    add(base, u, True)


_INS = ["x", "adj", "L0_gnn_Wq", "L0_gnn_bq", "L0_gnn_Wk", "L0_gnn_bk", "L0_gnn_Wv", "L0_gnn_bv", "L0_gnn_Wo",
        "L0_gnn_bo", "L0_ffn_Wg", "L0_ffn_bg", "L0_ffn_W1", "L0_ffn_b1", "L0_ffn_W2", "L0_ffn_b2"]


def kernel(**inputs):
    import numpy as _np
    import concourse.bacc as _bacc
    from concourse.bass_utils import run_bass_kernel_spmd as _run

    nc = _bacc.Bacc("TRN2", target_bir_lowering=False, num_devices=1)
    arrays, args = {}, []
    for name in _INS:
        a = _np.ascontiguousarray(inputs[name])
        arrays[f"in_{name}"] = a
        args.append(nc.dram_tensor(f"in_{name}", a.shape, mybir.dt.from_np(a.dtype), kind="ExternalInput").ap())
    graphs, n, d = inputs["x"].shape
    n_experts = inputs["L0_ffn_W1"].shape[0]
    table = n_experts * (graphs * n + P) + n_experts * P
    args.append(nc.dram_tensor("out_x", (graphs, n, d), F32, kind="ExternalOutput").ap())
    args.append(nc.dram_tensor("x1_dram", (graphs * n, d), F32, kind="Internal").ap())
    args.append(nc.dram_tensor("rows_dram", (table, d), F32, kind="Internal").ap())
    tiles = graphs * n * TOP_K // P + n_experts
    args.append(nc.dram_tensor("expert_dram", (tiles * P, d), F32, kind="Internal").ap())
    build(nc, *args)
    r = _run(nc, [arrays], core_ids=[0])
    return r.results[0]["out_x"]
```

```python
from contextlib import ExitStack

import concourse.bass as bass
from concourse import mybir

F32 = mybir.dt.float32
F32R = mybir.dt.float32r
BF16 = mybir.dt.bfloat16
I32 = mybir.dt.int32
U32 = mybir.dt.uint32
ALU = mybir.AluOpType
ACT = mybir.ActivationFunctionType
AX = mybir.AxisListType

P = 128
HEADS = 8
HEAD_DIM = 32
TOP_K = 2
EPS = 1e-5
MASKED = -1000000000.0
RSQRT_MAGIC = float(0x5F3759DF)
PASSES = ((0, 0), (1, 0), (0, 1))
HIGH, LOW = 0, 1


def first_graphs(graphs):
    return graphs * 11 // 16


def tile_counts(graphs, experts):
    full = graphs * TOP_K
    first = first_graphs(graphs) * TOP_K
    return first + experts, first + experts + (full - first) + 2 * experts


def build(nc, x, adj, Wq, bq, Wk, bk, Wv, bv, Wo, bo, Wg, bg, W1, b1, W2, b2, out, x1_dram, rows_dram,
          expert_dram0, expert_dram1):
    GRAPHS, N, D = x.shape
    EXPERTS, _, HID = W1.shape
    TOKENS = GRAPHS * N
    KB = D // P
    HB = HID // P
    RG = P // HEAD_DIM
    HH = HEADS // RG
    CAP = TOKENS + P
    FIRST_TILES, TILES = tile_counts(GRAPHS, EXPERTS)
    assert N == P and KB == 2 and HH == 2

    x_rows = x.rearrange("g n d -> (g n) d")
    out_rows = out.rearrange("g n d -> (g n) d")

    ctx = ExitStack()
    with ctx:
        def keep(name, shape, dt):
            return ctx.enter_context(nc.sbuf_tensor(name, shape, dt))

        w1 = keep("w1", [P, 2, EXPERTS, KB * HID], F32R)
        w2 = keep("w2", [P, 2, EXPERTS, HB * D], F32R)
        ident = keep("ident", [P, P], F32)
        slots = keep("slots", [P, TOP_K, GRAPHS], F32)
        outputs_at = keep("outputs_at", [P, TOP_K, GRAPHS], I32)
        top_scores = keep("top_scores", [P, TOP_K, GRAPHS], F32)
        counts = keep("counts", [P, EXPERTS], F32)
        count_rows = keep("count_rows", [P, EXPERTS], F32)
        half_counts = keep("half_counts", [P, 2, EXPERTS], F32)

        wall = keep("attn_w", [P, 2, 4, KB, D], F32R)

        setup(nc, Wq, Wk, Wv, Wo, wall, ident, D)
        attention(nc, x_rows, adj, wall, W1, W2, w1, w2, bq, bk, bv, bo, Wg, bg, ident, slots, top_scores,
                  counts, count_rows, half_counts, x1_dram, rows_dram, GRAPHS, D, EXPERTS, CAP)
        with ExitStack() as ends_ctx:
            sums = Sums(nc, ends_ctx, top_scores, outputs_at, x1_dram, out_rows, D, GRAPHS)
            experts(nc, b1, b2, w1, w2, ident, count_rows, half_counts, slots, outputs_at, rows_dram,
                    (expert_dram0, expert_dram1), sums, GRAPHS, EXPERTS, D, HID, CAP, FIRST_TILES, TILES)
            last_sums(nc, sums, expert_dram1, GRAPHS)


def setup(nc, Wq, Wk, Wv, Wo, wall, ident, D):
    KB = D // P
    with ExitStack() as ctx:
        raw = ctx.enter_context(nc.sbuf_tensor("raw", [P, 4, KB * D], F32))
        loaded = [ctx.enter_context(nc.semaphore(f"w_loaded{k}")) for k in range(4)]
        q_scaled, split_high, ident_zero, ident_done = (
            ctx.enter_context(nc.semaphore(n)) for n in ("q_scaled", "w_split_high", "ident_zero", "ident_done"))
        block = ctx.enter_context(nc.Block())
        SCALE = float(HEAD_DIM) ** -0.5

        @block.sync
        def _(sp):
            for k, w in enumerate((Wq, Wk, Wv, Wo)):
                sp.dma_start(raw[:, k, :].rearrange("p (k d) -> p k d", k=KB),
                             w.rearrange("(k p) d -> p k d", p=P)).then_inc(loaded[k], 16)

        @block.scalar
        def _(act):
            act.wait_ge(loaded[0], 16)
            act.activation(raw[:, 0, :], raw[:, 0, :], ACT.Copy, scale=SCALE).then_inc(q_scaled, 1)
            act.wait_ge(q_scaled, 1)
            for k in range(4):
                act.wait_ge(loaded[k], 16)
                act.activation(wall[:, HIGH, k], raw[:, k, :].rearrange("p (k d) -> p k d", k=KB),
                               ACT.Copy).then_inc(split_high, 1)

        @block.vector
        def _(dve):
            for k in range(4):
                dve.wait_ge(split_high, k + 1)
                dve.tensor_tensor(wall[:, LOW, k], raw[:, k, :].rearrange("p (k d) -> p k d", k=KB),
                                  wall[:, HIGH, k], ALU.subtract)

        @block.gpsimd
        def _(pool):
            pool.memset(ident[:], 0.0).then_inc(ident_zero, 1)
            pool.wait_ge(ident_zero, 1)
            pool.affine_select(out=ident[:], in_=ident[:], compare_op=ALU.not_equal, fill=1.0, base=0,
                               pattern=[[-1, P]], channel_multiplier=1).then_inc(ident_done, 1)


def attention(nc, x_rows, adj, wall, W1, W2, w1, w2, bq, bk, bv, bo, Wg, bg, ident, slots, top_scores,
              counts, count_rows, half_counts, x1_dram, rows_dram, GRAPHS, D, EXPERTS, CAP):
    KB, RG, HH = D // P, P // HEAD_DIM, HEADS * HEAD_DIM // P
    VW = HEAD_DIM + 1
    SCALE = float(HEAD_DIM) ** -0.5
    UNROLL = 8
    CONSTS = 1 + 1 + 2 * KB + 3
    L_STATS, L_NEWTON, L_NORM, L_XT, L_QK, L_V = 4, 6, 7, 8, 10, 11
    L_SPREAD, L_S, L_PT, L_PV, L_OT, L_RES, L_X1 = 12, 13, 14, 15, 16, 16, 17
    L_STATS2, L_NEWTON2, L_NORM2, L_GT, L_TOP, L_BEST, L_RANK, L_SLOT = 18, 20, 21, 22, 23, 24, 25, 25
    L_LAST = L_SLOT + 1
    HEAD_STEPS = -(-L_LAST // UNROLL) * UNROLL
    assert GRAPHS % UNROLL == 0

    with ExitStack() as ctx:
        def sb(name, shape, dt=F32):
            return ctx.enter_context(nc.sbuf_tensor(name, shape, dt))

        def pb(name, shape):
            return ctx.enter_context(nc.psum_tensor(name, shape, F32))

        def sem(name):
            return ctx.enter_context(nc.semaphore(name))

        wg = sb("wg", [P, KB, EXPERTS])
        bqk = sb("bqk", [P, 2, KB])
        bv_all = sb("bv_all", [P, D])
        bo_all = sb("bo_all", [P, D])
        bg_all = sb("bg_all", [P, EXPERTS])
        mask = sb("mask", [P, P])
        before = sb("before", [P, P], BF16)
        ones = sb("ones", [P, P], BF16)
        expert_id = sb("expert_id", [P, EXPERTS])
        xin = sb("xin", [P, 8, D])
        stats = sb("stats", [P, 4, 6])
        moments = sb("moments", [P, 2, 4, 2])
        rstd = sb("rstd", [P, 2, 4])
        shift = sb("shift", [P, 2, 4])
        newton = sb("newton", [P, 3, 2, 2])
        xn = sb("xn", [P, D])
        xT = [sb(f"xT{h}", [P, 2, KB, 2 * P], F32R) for h in (HIGH, LOW)]
        q = sb("q", [P, 2, 2, KB, 2 * P], F32R)
        k_all = sb("k_all", [P, 2, KB, 2 * P], F32R)
        k_heads = sb("k_heads", [P, 2, 2, KB, RG, P], F32R)
        v1 = sb("v1", [P, 4, HEADS, VW])
        scores = sb("scores", [P, 2, HEADS, P])
        neg_max = sb("neg_max", [P, 2, HEADS])
        probsT = sb("probsT", [P, HEADS, P])
        denom = sb("denom", [P, 2, HEADS])
        o = sb("o", [P, 2, D])
        oT = [sb(f"oT{h}", [P, 2, KB, P], F32R) for h in (HIGH, LOW)]
        xres = sb("xres", [P, 2, D])
        x1 = sb("x1", [P, 8, D])
        stats2 = sb("stats2", [P, 4, 6])
        xn2 = sb("xn2", [P, 8, D])
        gT = sb("gT", [P, 2, KB, P])
        logits = sb("logits", [P, 4, EXPERTS])
        top8 = sb("top8", [P, 4, 8])
        top8_at = sb("top8_at", [P, 4, 8], U32)
        top_at = sb("top_at", [P, 2, 2, TOP_K])
        chosen = sb("chosen", [P, 2, TOP_K, 2, EXPERTS])
        either = sb("either", [P, 2, 2, EXPERTS], BF16)
        place = sb("place", [P, 2, 2, EXPERTS])
        picked = sb("picked", [P, 2, TOP_K, 2, EXPERTS])
        slot_f = sb("slot_f", [P, 2, TOP_K, 2])
        slot_i = sb("slot_i", [P, 4, TOP_K, 2], I32)

        ps_s = pb("ps_s", [P, HH, RG * P])
        ps_pT = pb("ps_pT", [P, HH, RG * P])
        ps_qk = pb("ps_qk", [P, KB, 2 * P])
        ps_vo = pb("ps_vo", [P, 2, D])
        ps_t = pb("ps_t", [P, 512])[:, 0:KB * P]
        ps_o = pb("ps_o", [P, 512])
        o_ps = ps_o[:, 0:HEADS * VW].rearrange("p (h c) -> p h c", c=VW)
        gate_ps = ps_o[:, 272:272 + EXPERTS]
        rank_ps = ps_o[:, 304:304 + 2 * EXPERTS].rearrange("p (g e) -> p g e", e=EXPERTS)
        total_ps = ps_o[:, 336:336 + EXPERTS]

        x_loaded = [sem(f"x_loaded{k}") for k in range(8)]
        k_spread = [sem(f"k_spread{k}") for k in range(2)]
        xres_loaded = [sem(f"xres_loaded{k}") for k in range(2)]
        x1_stored = [sem(f"x1_stored{k}") for k in range(8)]
        scattered = [sem(f"scattered{k}") for k in range(4)]
        const_loaded, counted = sem("const_loaded"), sem("counted")
        (const_high, const_low, const_ready, consts_pool, chain_pool, chain_dve, held, stats_done, moments_done, normed,
         xT_mm, xT_high, xT_low, qk_mm, qk_high, qk_low, v_mm, v_done, s_mm, max_done, exp_done,
         pT_mm, pT_done, pv_mm, denom_done, o_done, oT_mm, oT_high, oT_low, proj_mm, xres_biased,
         x1_done, stats2_done, moments2_done, normed2, gT_mm, gT_done, gate_mm, logits_done, top_done,
         chosen_done, either_done, rank_mm, placed, chain_slot, slot_done, newton_step, newton_done) = (sem(n) for n in (
             "const_high const_low const_ready consts_pool chain_pool chain_dve held stats_done moments_done normed "
             "xT_mm xT_high xT_low qk_mm qk_high qk_low v_mm v_done s_mm max_done exp_done "
             "pT_mm pT_done pv_mm denom_done o_done oT_mm oT_high oT_low proj_mm xres_biased "
             "x1_done stats2_done moments2_done normed2 gT_mm gT_done gate_mm logits_done top_done "
             "chosen_done either_done rank_mm placed chain_slot slot_done newton_step newton_done").split())

        def hold(eng, semaphore, count):
            eng.wait_ge(semaphore, count)
            eng.sem_inc(held, 1)

        def run(eng, step):
            for t in range(HEAD_STEPS):
                step(t // UNROLL, t % UNROLL, lambda lag: t >= lag)
            with eng.Fori(HEAD_STEPS // UNROLL, GRAPHS // UNROLL) as base:
                for u in range(UNROLL):
                    step(base, u, lambda lag: True)
            for t in range(GRAPHS, GRAPHS + L_LAST):
                step(t // UNROLL, t % UNROLL, lambda lag: t - lag < GRAPHS)

        def graph(base, u, lag):
            return base * UNROLL + (u - lag)

        def turns(base, u, lag, ring):
            return base * (UNROLL // ring) + ((u - lag) // ring + 1)

        def pair_of(base, u, lag):
            return base * (UNROLL // 2) + (u - lag) // 2

        def newton_run(base, u, lag, newton_lag):
            first = (u - lag) // 2 * 2 + newton_lag
            return base * (UNROLL // 2) + ((first - L_NEWTON) // 2 + 1)

        def old(base, u, lag, back):
            return not isinstance(base, int) or graph(base, u, lag) >= back

        PIECE = W1.shape[2] * KB
        assert PIECE == W2.shape[1] // P * D and 2 * PIECE <= 8 * D and 2 * EXPERTS <= L_X1
        pieces = [(W1[e].rearrange("(k p) h -> p k h", p=P), w1, KB, e) for e in range(EXPERTS)]
        pieces += [(W2[e].rearrange("(k p) d -> p k d", p=P), w2, PIECE // D, e) for e in range(EXPERTS)]
        raw = [ring[:].rearrange("p k d -> p (k d)")[:, n * PIECE:(n + 1) * PIECE] for ring in (x1, xn2) for n in range(2)]
        piece_loaded = [sem(f"piece_loaded{k}") for k in range(len(raw))]
        piece_high, piece_low = sem("piece_high"), sem("piece_low")

        def piece(base, u):
            n = base * UNROLL + u if isinstance(base, int) else len(pieces)
            return (n, *pieces[n]) if n < len(pieces) else None

        block = ctx.enter_context(nc.Block())

        @block.sync
        def _(sp):
            sp.dma_start(mask[:], adj).then_inc(const_loaded, 16)
            sp.dma_start(wg[:], Wg.rearrange("(k p) e -> p k e", p=P)).then_inc(const_loaded, 16)
            for k, b in enumerate((bq, bk)):
                for blk in range(KB):
                    sp.dma_start(bqk[:, k, blk:blk + 1], b[blk * P:(blk + 1) * P].unsqueeze(1)).then_inc(
                        const_loaded, 16)
            for dst, b in ((bv_all, bv), (bo_all, bo), (bg_all, bg)):
                sp.dma_start(dst[:], b.partition_broadcast(P)).then_inc(const_loaded, 16)

            AHEAD = len(raw) - 1

            def load_piece(n):
                if n >= len(raw):
                    sp.wait_ge(piece_low, n - len(raw) + 1)
                sp.dma_start(raw[n % len(raw)].rearrange("p (k h) -> p k h", k=pieces[n][2]), pieces[n][0]).then_inc(
                    piece_loaded[n % len(raw)], 16)

            for n in range(AHEAD):
                load_piece(n)

            def step(base, u, live):
                if live(0):
                    i, k = graph(base, u, 0), u % 8
                    if old(base, u, 0, 8):
                        sp.wait_ge(normed, i - 7)
                    sp.dma_start(xin[:, k, :], x_rows[bass.ds(i * P, P), :]).then_inc(x_loaded[k], 16)
                if piece(base, u + AHEAD):
                    load_piece(base * UNROLL + u + AHEAD)
                if live(L_RES):
                    i, k = graph(base, u, L_RES), (u - L_RES) % 2
                    if old(base, u, L_RES, 2):
                        sp.wait_ge(x1_done, i - 1)
                    sp.dma_start(xres[:, k, :], x_rows[bass.ds(i * P, P), :]).then_inc(xres_loaded[k], 16)
                if live(L_SPREAD):
                    i, buf, cols = graph(base, u, L_SPREAD), (u - L_SPREAD) % 2, (u - L_SPREAD) % 2 * P
                    hold(sp, qk_low, i + (2 if buf == 0 else 1))
                    if old(base, u, L_SPREAD, 2):
                        hold(sp, s_mm, (i - 1) * HH)
                    for r in range(RG):
                        rows = slice(r * HEAD_DIM, (r + 1) * HEAD_DIM)
                        sp.dma_start(k_heads[rows, buf, :, :, r, :].bitcast(F32),
                                     k_all[rows, :, :, cols:cols + P].bitcast(F32)).then_inc(
                            k_spread[buf], 16)
                if live(L_X1 + 1):
                    i, k = graph(base, u, L_X1 + 1), (u - L_X1 - 1) % 8
                    sp.wait_ge(x1_done, i + 1)
                    sp.dma_start(x1_dram[bass.ds(i * P, P), :], x1[:, k, :]).then_inc(x1_stored[k], 16)

            run(sp, step)
            for k in range(8):
                sp.wait_ge(x1_stored[k], 16 * (GRAPHS // 8))

        @block.tensor
        def _(pe):
            def step(base, u, live):
                if live(L_S):
                    i, par, cols = graph(base, u, L_S), (u - L_S) // 2 % 2, (u - L_S) % 2 * P
                    pe.wait_ge(k_spread[(u - L_S) % 2], 16 * RG * turns(base, u, L_S, 2))
                    if old(base, u, L_S, 1):
                        pe.wait_ge(max_done, i)
                    for hh in range(HH):
                        for n, (a, b) in enumerate(PASSES):
                            mm = pe.matmul(ps_s[:, hh, :], q[:, a, par, hh, cols:cols + P],
                                           k_heads[:, (u - L_S) % 2, b, hh], start=n == 0, stop=n == len(PASSES) - 1)
                        mm.then_inc(s_mm, 1)
                if live(L_XT):
                    i = graph(base, u, L_XT)
                    pe.wait_ge(normed, i + 1)
                    if old(base, u, L_XT, 1):
                        pe.wait_ge(xT_low, i)
                    if live(L_OT + 1) and old(base, u, L_OT + 1, 0):
                        pe.wait_ge(oT_low, graph(base, u, L_OT + 1) + 1)
                    if live(L_GT + 1) and old(base, u, L_GT + 1, 0):
                        pe.wait_ge(gT_done, graph(base, u, L_GT + 1) + 1)
                    for kb in range(KB):
                        mm = pe.transpose(ps_t[:, kb * P:(kb + 1) * P], xn[:, kb * P:(kb + 1) * P],
                                          ident[:])
                    mm.then_inc(xT_mm, 1)
                if live(L_PV):
                    i = graph(base, u, L_PV)
                    pe.wait_ge(v_done, i + 1)
                    if old(base, u, L_PV, 1):
                        pe.wait_ge(o_done, i)
                    if live(L_TOP + 1):
                        pe.wait_ge(logits_done, graph(base, u, L_TOP + 1) + 1)
                    if live(L_RANK + 1) and (u - L_RANK - 1) % 2 == 1:
                        pe.wait_ge(placed, 2 * pair_of(base, u, L_RANK + 1) + 2)
                    pe.wait_ge(pT_done, i + 1)
                    for h in range(HEADS):
                        mm = pe.matmul(o_ps[:, h, :], probsT[:, h, :], v1[:, (u - L_PV) % 4, h, :],
                                       start=True, stop=True)
                    mm.then_inc(pv_mm, 1)
                if live(L_OT):
                    i, buf = graph(base, u, L_OT), (u - L_OT) % 2
                    pe.wait_ge(o_done, i + 1)
                    if old(base, u, L_OT, 1):
                        pe.wait_ge(oT_low, i)
                    if live(L_XT):
                        pe.wait_ge(xT_low, graph(base, u, L_XT) + 1)
                    if live(L_GT + 1) and old(base, u, L_GT + 1, 0):
                        pe.wait_ge(gT_done, graph(base, u, L_GT + 1) + 1)
                    for kb in range(KB):
                        mm = pe.transpose(ps_t[:, kb * P:(kb + 1) * P], o[:, buf, kb * P:(kb + 1) * P], ident[:])
                    mm.then_inc(oT_mm, 1)
                if live(L_V):
                    i, par, cols = graph(base, u, L_V), (u - L_V) // 2 % 2, (u - L_V) % 2 * P
                    pe.wait_ge(xT_low, i + 1)
                    if old(base, u, L_V, 1):
                        pe.wait_ge(v_done, i)
                    if live(L_X1 + 1) and old(base, u, L_X1 + 1, 0):
                        pe.wait_ge(x1_done, graph(base, u, L_X1 + 1) + 1)
                    for n, (kb, (a, b)) in enumerate((kb, ab) for kb in range(KB) for ab in PASSES):
                        mm = pe.matmul(ps_vo[:, 0, :], xT[a][:, par, kb, cols:cols + P], wall[:, b, 2, kb, :],
                                       start=n == 0, stop=n == 3 * KB - 1)
                    mm.then_inc(v_mm, 1)
                if live(L_PT):
                    i, buf = graph(base, u, L_PT), (u - L_PT) % 2
                    pe.wait_ge(exp_done, i + 1)
                    if old(base, u, L_PT, 1):
                        pe.wait_ge(pT_done, i)
                    for h in range(HEADS):
                        mm = pe.transpose(ps_pT[:, h // RG, h % RG * P:(h % RG + 1) * P], scores[:, buf, h, :], ident[:])
                    mm.then_inc(pT_mm, 1)
                if live(L_QK):
                    i, which, par = graph(base, u, L_QK), (u - L_QK) % 2, (u - L_QK) // 2 % 2
                    pe.wait_ge(xT_low, i + (2 if which == 0 else 1))
                    if old(base, u, L_QK, 1):
                        pe.wait_ge(qk_low, i)
                    for blk in range(KB):
                        for n, (kb, (a, b)) in enumerate((kb, ab) for kb in range(KB) for ab in PASSES):
                            mm = pe.matmul(ps_qk[:, blk, :], wall[:, a, which, kb, blk * P:(blk + 1) * P],
                                           xT[b][:, par, kb, :], start=n == 0, stop=n == 3 * KB - 1)
                    mm.then_inc(qk_mm, 1)
                if live(L_TOP):
                    i, buf = graph(base, u, L_TOP), (u - L_TOP) % 2
                    pe.wait_ge(gT_done, i + 1)
                    if old(base, u, L_TOP, 1):
                        pe.wait_ge(logits_done, i)
                    if live(L_PV):
                        pe.wait_ge(o_done, graph(base, u, L_PV) + 1)
                    else:
                        pe.wait_ge(placed, graph(base, u, L_RANK) // 2 * 2)
                    for kb in range(KB):
                        mm = pe.matmul(gate_ps, gT[:, buf, kb, :], wg[:, kb, :], start=kb == 0, stop=kb == KB - 1)
                    mm.then_inc(gate_mm, 1)
                if live(L_RANK) and (u - L_RANK) % 2 == 1:
                    pair, pp = pair_of(base, u, L_RANK), (u - L_RANK) // 2 % 2
                    pe.wait_ge(either_done, pair + 1)
                    if not live(L_TOP):
                        pe.wait_ge(logits_done, GRAPHS)
                        pe.wait_ge(placed, 2 * pair)
                    pe.matmul(rank_ps[:, 0, :], before[:], either[:, pp, 0, :], start=True, stop=True)
                    pe.matmul(rank_ps[:, 1, :], before[:], either[:, pp, 1, :], start=True, stop=False)
                    pe.matmul(rank_ps[:, 1, :], ones[:], either[:, pp, 0, :], start=False, stop=True)
                    pe.matmul(total_ps, ones[:], either[:, pp, 0, :], start=True, stop=False)
                    pe.matmul(total_ps, ones[:], either[:, pp, 1, :], start=False, stop=True).then_inc(rank_mm, 1)
                if live(L_X1):
                    i, buf = graph(base, u, L_X1), (u - L_X1) % 2
                    pe.wait_ge(oT_low, i + 1)
                    if old(base, u, L_X1, 1):
                        pe.wait_ge(x1_done, i)
                    if live(L_V):
                        pe.wait_ge(v_done, graph(base, u, L_V) + 1)
                    for n, (kb, (a, b)) in enumerate((kb, ab) for kb in range(KB) for ab in PASSES):
                        mm = pe.matmul(ps_vo[:, 1, :], oT[a][:, buf, kb, :], wall[:, b, 3, kb, :],
                                       start=n == 0, stop=n == 3 * KB - 1)
                    mm.then_inc(proj_mm, 1)
                if live(L_GT):
                    i = graph(base, u, L_GT)
                    pe.wait_ge(normed2, i + 1)
                    if live(L_OT):
                        pe.wait_ge(oT_low, graph(base, u, L_OT) + 1)
                    if old(base, u, L_GT, 1):
                        pe.wait_ge(gT_done, i)
                    for kb in range(KB):
                        mm = pe.transpose(ps_t[:, kb * P:(kb + 1) * P],
                                          xn2[:, (u - L_GT) % 8, kb * P:(kb + 1) * P], ident[:])
                    mm.then_inc(gT_mm, 1)

            pe.wait_ge(const_ready, 1)
            pe.wait_ge(consts_pool, 2 + EXPERTS)
            run(pe, step)

        @block.scalar
        def _(act):
            act.wait_ge(const_loaded, 16 * CONSTS)
            act.activation(bqk[:, 0, :], bqk[:, 0, :], ACT.Copy, scale=SCALE).then_inc(const_high, 1)
            act.wait_ge(const_high, 1)

            def step(base, u, live):
                if piece(base, u):
                    n, _, split, _, e = piece(base, u)
                    act.wait_ge(piece_loaded[n % len(raw)], 16 * (n // len(raw) + 1))
                    act.activation(split[:, HIGH, e, :], raw[n % len(raw)], ACT.Copy).then_inc(piece_high, 1)
                if live(L_XT):
                    i, par, cols = graph(base, u, L_XT), (u - L_XT) // 2 % 2, (u - L_XT) % 2 * P
                    if old(base, u, L_XT, 4):
                        act.wait_ge(v_mm, i - 3)
                        act.wait_ge(qk_mm, i - 2 - (u - L_XT) % 2)
                    act.wait_ge(xT_mm, i + 1)
                    act.activation(xT[HIGH][:, par, :, cols:cols + P],
                                   ps_t[:].rearrange("p (k n) -> p k n", k=KB), ACT.Copy).then_inc(xT_high, 1)
                if live(L_NORM):
                    i, k = graph(base, u, L_NORM), (u - L_NORM) % 4
                    hold(act, newton_done, newton_run(base, u, L_NORM, L_NEWTON))
                    if old(base, u, L_NORM, 1):
                        hold(act, xT_mm, i)
                    act.activation(xn[:], xin[:, (u - L_NORM) % 8, :], ACT.Identity, scale=rstd[:, 0, k:k + 1],
                                   bias=shift[:, 0, k:k + 1]).then_inc(normed, 1)
                if live(L_NORM2):
                    i, k = graph(base, u, L_NORM2), (u - L_NORM2) % 8
                    m = (k + 2) % 4
                    hold(act, newton_done, newton_run(base, u, L_NORM2, L_NEWTON2))
                    if old(base, u, L_NORM2, 8):
                        hold(act, scattered[k // 2], 64 * (turns(base, u, L_NORM2, 8) - 1))
                    act.activation(xn2[:, k, :], x1[:, k, :], ACT.Identity, scale=rstd[:, 1, m:m + 1],
                                   bias=shift[:, 1, m:m + 1]).then_inc(normed2, 1)
                if live(L_OT):
                    i, buf = graph(base, u, L_OT), (u - L_OT) % 2
                    if old(base, u, L_OT, 2):
                        act.wait_ge(proj_mm, i - 1)
                    act.wait_ge(oT_mm, i + 1)
                    act.activation(oT[HIGH][:, buf], ps_t[:].rearrange("p (k n) -> p k n", k=KB),
                                   ACT.Copy).then_inc(oT_high, 1)
                if live(L_S):
                    i, buf = graph(base, u, L_S), (u - L_S) % 2
                    act.wait_ge(max_done, i + 1)
                    for h in range(RG):
                        act.activation(scores[:, buf, h, :], scores[:, buf, h, :], ACT.Exp,
                                       scale=-1.0, bias=neg_max[:, buf, h:h + 1])
                if live(L_PT):
                    i = graph(base, u, L_PT)
                    if old(base, u, L_PT, 1):
                        act.wait_ge(pv_mm, i)
                    act.wait_ge(pT_mm, i + 1)
                    act.activation(probsT[:], ps_pT[:].rearrange("p b (r n) -> p (b r) n", r=RG),
                                   ACT.Copy).then_inc(pT_done, 1)
                if live(L_S):
                    i, buf = graph(base, u, L_S), (u - L_S) % 2
                    for h in range(RG, HEADS):
                        e = act.activation(scores[:, buf, h, :], scores[:, buf, h, :], ACT.Exp,
                                           scale=-1.0, bias=neg_max[:, buf, h:h + 1])
                    e.then_inc(exp_done, 1)
                if live(L_QK):
                    i, which, par = graph(base, u, L_QK), (u - L_QK) % 2, (u - L_QK) // 2 % 2
                    if which == 0 and old(base, u, L_QK, 4):
                        act.wait_ge(s_mm, (i - 2) * HH)
                    if which == 1 and old(base, u, L_QK, 2):
                        act.wait_ge(k_spread[0], 16 * RG * (turns(base, u, L_QK, 2) - 1))
                        act.wait_ge(k_spread[1], 16 * RG * (turns(base, u, L_QK, 2) - 1))
                    act.wait_ge(qk_mm, i + 1)
                    for blk in range(KB):
                        act.activation(q[:, HIGH, par, blk, :] if which == 0 else k_all[:, HIGH, blk, :],
                                       ps_qk[:, blk, :], ACT.Identity,
                                       bias=bqk[:, which, blk:blk + 1]).then_inc(qk_high, 1)
                if live(L_GT):
                    i, buf = graph(base, u, L_GT), (u - L_GT) % 2
                    if old(base, u, L_GT, 2):
                        act.wait_ge(gate_mm, i - 1)
                    act.wait_ge(gT_mm, i + 1)
                    act.activation(gT[:, buf], ps_t[:].rearrange("p (k n) -> p k n", k=KB),
                                   ACT.Copy).then_inc(gT_done, 1)

            run(act, step)

        @block.vector
        def _(dve):
            dve.wait_ge(const_loaded, 16 * CONSTS)
            dve.wait_ge(const_high, 1)
            dve.tensor_scalar(mask[:], mask[:], -1.0, 1.0, ALU.mult, ALU.add).then_inc(const_low, 1)
            dve.wait_ge(const_low, 1)
            dve.tensor_scalar(mask[:], mask[:], MASKED, None, ALU.mult).then_inc(const_low, 1)
            dve.memset(v1[:], 1.0).then_inc(const_low, 1)
            dve.memset(k_heads[:].bitcast(F32), 0.0).then_inc(const_low, 1)
            dve.memset(counts[:], 0.0).then_inc(const_low, 1)
            dve.wait_ge(const_low, 5)
            dve.wait_ge(consts_pool, 2 + EXPERTS)
            dve.tensor_scalar(count_rows[:], expert_id[:], float(CAP), None, ALU.mult).then_inc(const_ready, 1)
            dve.wait_ge(const_ready, 1)

            def step(base, u, live):
                if piece(base, u):
                    n, _, split, _, e = piece(base, u)
                    dve.wait_ge(piece_high, n + 1)
                    dve.tensor_tensor(split[:, LOW, e, :], raw[n % len(raw)], split[:, HIGH, e, :],
                                      ALU.subtract).then_inc(piece_low, 1)
                if live(L_XT):
                    i, par, cols = graph(base, u, L_XT), (u - L_XT) // 2 % 2, (u - L_XT) % 2 * P
                    dve.wait_ge(xT_high, i + 1)
                    dve.tensor_tensor(xT[LOW][:, par, :, cols:cols + P],
                                      ps_t[:].rearrange("p (k n) -> p k n", k=KB),
                                      xT[HIGH][:, par, :, cols:cols + P], ALU.subtract).then_inc(xT_low, 1)
                if live(L_S):
                    i, buf = graph(base, u, L_S), (u - L_S) % 2
                    if old(base, u, L_S, 2):
                        hold(dve, pT_mm, i - 1)
                    for h in range(HEADS):
                        hh, r = h // RG, h % RG
                        if r == 0:
                            hold(dve, s_mm, i * HH + hh + 1)
                        m = dve.tensor_tensor_reduce(
                            scores[:, buf, h, :], ps_s[:, hh, r * P:(r + 1) * P], mask[:], -1.0, 3.0e38,
                            ALU.add, ALU.min, neg_max[:, buf, h:h + 1])
                    m.then_inc(max_done, 1)
                if live(L_PV):
                    i, buf = graph(base, u, L_PV), (u - L_PV) % 2
                    dve.wait_ge(pv_mm, i + 1)
                    dve.reciprocal(denom[:, buf, :], o_ps[:, :, HEAD_DIM]).then_inc(denom_done, 1)
                    if old(base, u, L_PV, 2):
                        dve.wait_ge(oT_mm, i - 1)
                    dve.wait_ge(denom_done, i + 1)
                    dve.tensor_tensor(o[:, buf, :].rearrange("p (h c) -> p h c", c=HEAD_DIM),
                                      o_ps[:, :, 0:HEAD_DIM],
                                      denom[:, buf, :].unsqueeze(2).broadcast_to([P, HEADS, HEAD_DIM]),
                                      ALU.mult).then_inc(o_done, 1)
                if live(L_OT):
                    i, buf = graph(base, u, L_OT), (u - L_OT) % 2
                    dve.wait_ge(oT_high, i + 1)
                    dve.tensor_tensor(oT[LOW][:, buf], ps_t[:].rearrange("p (k n) -> p k n", k=KB),
                                      oT[HIGH][:, buf], ALU.subtract).then_inc(oT_low, 1)
                if live(L_V):
                    i, buf = graph(base, u, L_V), (u - L_V) % 4
                    if old(base, u, L_V, 4):
                        dve.wait_ge(pv_mm, i - 3)
                    dve.wait_ge(v_mm, i + 1)
                    dve.tensor_tensor(v1[:, buf, :, 0:HEAD_DIM],
                                      ps_vo[:, 0, :].rearrange("p (h c) -> p h c", c=HEAD_DIM),
                                      bv_all[:].rearrange("p (h c) -> p h c", c=HEAD_DIM),
                                      ALU.add).then_inc(v_done, 1)
                if live(L_STATS2):
                    i, k = graph(base, u, L_STATS2), (u - L_STATS2) % 8
                    dve.wait_ge(x1_done, i + 1)
                    dve.bn_stats(stats2[:, k % 4, :], x1[:, k, :]).then_inc(stats2_done, 1)
                if live(L_STATS):
                    i, k = graph(base, u, L_STATS), (u - L_STATS) % 8
                    dve.wait_ge(x_loaded[k], 16 * turns(base, u, L_STATS, 8))
                    dve.bn_stats(stats[:, k % 4, :], xin[:, k, :]).then_inc(stats_done, 1)
                if live(L_BEST):
                    i, k = graph(base, u, L_BEST), (u - L_BEST) % 4
                    hold(dve, logits_done, i + 1)
                    dve.max(top8[:, k, :], logits[:, k, :]).then_inc(chain_dve, 1)
                if live(L_STATS2):
                    i, k = graph(base, u, L_STATS2), (u - L_STATS2) % 4
                    hold(dve, stats2_done, i + 1)
                    if old(base, u, L_STATS2, 4):
                        hold(dve, newton_done, newton_run(base, u, L_STATS2 + 4, L_NEWTON2))
                    dve.bn_aggr(moments[:, 1, (k + 2) % 4, :], stats2[:, k, :]).then_inc(moments2_done, 1)
                if live(L_BEST):
                    i, k = graph(base, u, L_BEST), (u - L_BEST) % 4
                    hold(dve, chain_dve, i + 1)
                    dve.max_index(top8_at[:, k, :], top8[:, k, :], logits[:, k, :]).then_inc(top_done, 1)
                    dve.tensor_copy(top_scores[:, :, bass.ds(i, 1)], top8[:, k, 0:TOP_K].unsqueeze(2))
                if live(L_STATS):
                    i, k = graph(base, u, L_STATS), (u - L_STATS) % 4
                    hold(dve, stats_done, i + 1)
                    if old(base, u, L_STATS, 4):
                        hold(dve, newton_done, newton_run(base, u, L_STATS + 4, L_NEWTON))
                    dve.bn_aggr(moments[:, 0, k, :], stats[:, k, :]).then_inc(moments_done, 1)
                if live(L_BEST) and (u - L_BEST) % 2 == 1:
                    i, pair = graph(base, u, L_BEST), pair_of(base, u, L_BEST)
                    pp, k = (u - L_BEST) // 2 % 2, (u - L_BEST) % 4 - 1
                    dve.wait_ge(top_done, i + 1)
                    dve.tensor_copy(top_at[:, pp], top8_at[:, k:k + 2, 0:TOP_K]).then_inc(chosen_done, 1)
                    dve.wait_ge(chosen_done, 3 * pair + 1)
                    for c in range(TOP_K):
                        dve.tensor_tensor(
                            chosen[:, pp, c], expert_id[:].unsqueeze(1).broadcast_to([P, 2, EXPERTS]),
                            top_at[:, pp, :, c].unsqueeze(2).broadcast_to([P, 2, EXPERTS]),
                            ALU.is_equal).then_inc(chosen_done, 1)
                    dve.wait_ge(chosen_done, 3 * pair + 3)
                    dve.tensor_tensor(either[:, pp], chosen[:, pp, 0], chosen[:, pp, 1],
                                      ALU.add).then_inc(either_done, 1)
                if live(L_TOP):
                    i, k = graph(base, u, L_TOP), (u - L_TOP) % 4
                    if live(L_RANK) and (u - L_RANK) % 2 == 1:
                        dve.wait_ge(rank_mm, pair_of(base, u, L_RANK) + 1)
                    dve.wait_ge(gate_mm, i + 1)
                    dve.tensor_tensor(logits[:, k, :], gate_ps, bg_all[:],
                                      ALU.add).then_inc(logits_done, 1)
                if live(L_SLOT) and (u - L_SLOT) % 2 == 1:
                    pair, pp = pair_of(base, u, L_SLOT), (u - L_SLOT) // 2 % 2
                    dve.wait_ge(rank_mm, pair + 1)
                    dve.tensor_tensor(place[:, pp], rank_ps,
                                      count_rows[:].unsqueeze(1).broadcast_to([P, 2, EXPERTS]),
                                      ALU.add).then_inc(placed, 1)
                    dve.tensor_tensor(counts[:], total_ps, counts[:], ALU.add).then_inc(counted, 1)
                    dve.wait_ge(placed, 2 * pair + 1)
                    dve.tensor_tensor(count_rows[:], total_ps, count_rows[:], ALU.add).then_inc(placed, 1)
                if live(L_X1):
                    i, k = graph(base, u, L_X1), (u - L_X1) % 8
                    if old(base, u, L_X1, 8):
                        dve.wait_ge(x1_stored[k], 16 * turns(base, u, L_X1, 8) - 16)
                    dve.wait_ge(xres_biased, i + 1)
                    dve.wait_ge(proj_mm, i + 1)
                    dve.tensor_tensor(x1[:, k, :], ps_vo[:, 1, :], xres[:, k % 2, :], ALU.add).then_inc(x1_done, 1)
                if live(L_QK):
                    i, which, par = graph(base, u, L_QK), (u - L_QK) % 2, (u - L_QK) // 2 % 2
                    dve.wait_ge(qk_high, KB * i + KB)
                    for blk in range(KB):
                        high, low = ((q[:, HIGH, par, blk, :], q[:, LOW, par, blk, :]) if which == 0 else
                                     (k_all[:, HIGH, blk, :], k_all[:, LOW, blk, :]))
                        rest = dve.scalar_tensor_tensor(out=low, in0=ps_qk[:, blk, :],
                                                        scalar=bqk[:, which, blk:blk + 1], in1=high,
                                                        op0=ALU.add, op1=ALU.subtract)
                    rest.then_inc(qk_low, 1)
                if live(L_SLOT) and (u - L_SLOT) % 2 == 1:
                    i, pair = graph(base, u, L_SLOT), pair_of(base, u, L_SLOT)
                    pp, k = (u - L_SLOT) // 2 % 2, (u - L_SLOT) // 2 % 4
                    if old(base, u, L_SLOT, 8):
                        dve.wait_ge(scattered[k], 16 * 4 * (turns(base, u - 1, L_SLOT, 8) - 1))
                    dve.wait_ge(counted, pair + 1)
                    dve.tensor_copy(half_counts[:, bass.ds(pair // (first_graphs(GRAPHS) // 2), 1), :], counts[:].unsqueeze(1))
                    for c in range(TOP_K):
                        dve.tensor_tensor(picked[:, pp, c], chosen[:, pp, c], place[:, pp],
                                          ALU.mult).then_inc(chain_slot, 1)
                    dve.wait_ge(chain_slot, 3 * pair + 2)
                    dve.tensor_reduce(slot_f[:, pp], picked[:, pp], AX.X, ALU.add).then_inc(chain_slot, 1)
                    dve.wait_ge(chain_slot, 3 * pair + 3)
                    dve.tensor_copy(slot_i[:, k], slot_f[:, pp]).then_inc(slot_done, 1)
                    dve.tensor_copy(slots[:, :, bass.ds(graph(base, u, L_SLOT + 1), 2)], slot_f[:, pp])

            run(dve, step)

        @block.gpsimd
        def _(pool):
            pool.memset(before[:], 1.0).then_inc(chain_pool, 1)
            pool.wait_ge(chain_pool, 1)
            pool.affine_select(out=before[:], in_=before[:], compare_op=ALU.is_gt, fill=0.0, base=0,
                               pattern=[[1, P]], channel_multiplier=-1).then_inc(consts_pool, 1)
            pool.memset(ones[:], 1.0).then_inc(consts_pool, 1)
            for e in range(EXPERTS):
                pool.memset(expert_id[:, e:e + 1], float(e)).then_inc(consts_pool, 1)
            pool.wait_ge(const_loaded, 16 * CONSTS)

            ROUND = 16

            def rsqrt(run_before, mean, var, root, shift, shifted, square, negated):
                n = [0]

                def then(instruction):
                    n[0] += 1
                    if n[0] == ROUND:
                        instruction.then_inc(newton_done, 1)
                    else:
                        instruction.then_inc(newton_step, 1)
                        hold(pool, newton_step, run_before * (ROUND - 1) + n[0])

                then(pool.tensor_scalar(shifted, var, EPS, None, ALU.add))
                then(pool.tensor_scalar(root.bitcast(I32), shifted.bitcast(I32), -0.5, RSQRT_MAGIC,
                                        ALU.mult, ALU.add))
                for _ in range(3):
                    then(pool.tensor_tensor(square, root, root, ALU.mult))
                    then(pool.tensor_tensor(square, square, shifted, ALU.mult))
                    then(pool.tensor_scalar(square, square, -0.5, 1.5, ALU.mult, ALU.add))
                    then(pool.tensor_tensor(root, square, root, ALU.mult))
                then(pool.tensor_scalar(negated, mean, -1.0, None, ALU.mult))
                then(pool.tensor_tensor(shift, negated, root, ALU.mult))
                assert n[0] == ROUND

            def step(base, u, live):
                if (live(L_NEWTON) or live(L_NEWTON2)) and u % 2 == 0:
                    norms = slice(0 if live(L_NEWTON) else 1, 2 if live(L_NEWTON2) else 1)
                    if live(L_NEWTON):
                        if old(base, u, L_NEWTON, 4):
                            hold(pool, normed, graph(base, u, L_NEWTON) - 2)
                        hold(pool, moments_done, graph(base, u, L_NEWTON) + 2)
                    if live(L_NEWTON2):
                        if old(base, u, L_NEWTON2, 4):
                            hold(pool, normed2, graph(base, u, L_NEWTON2) - 2)
                        hold(pool, moments2_done, graph(base, u, L_NEWTON2) + 2)
                    k = (u - L_NEWTON) % 4
                    rsqrt(pair_of(base, u, L_NEWTON), moments[:, norms, k:k + 2, 0], moments[:, norms, k:k + 2, 1],
                          rstd[:, norms, k:k + 2], shift[:, norms, k:k + 2], newton[:, 0, norms, :],
                          newton[:, 1, norms, :], newton[:, 2, norms, :])
                if live(L_X1):
                    k = (u - L_X1) % 2
                    pool.wait_ge(xres_loaded[k], 16 * turns(base, u, L_X1, 2))
                    pool.tensor_tensor(xres[:, k, :], xres[:, k, :], bo_all[:], ALU.add).then_inc(xres_biased, 1)
                if live(L_SLOT) and (u - L_SLOT) % 2 == 1:
                    i, pair = graph(base, u, L_SLOT), pair_of(base, u, L_SLOT)
                    k = (u - L_SLOT) // 2 % 4
                    hold(pool, slot_done, pair + 1)
                    for g in range(2):
                        for c in range(TOP_K):
                            pool.indirect_dma_start(
                                rows_dram, bass.IndirectOffsetOnAxis(slot_i[:, k, c, g:g + 1], axis=0),
                                xn2[:, (u - L_SLOT - 1 + g) % 8, :], None).then_inc(scattered[k], 16)

            run(pool, step)
            for k in range(4):
                pool.wait_ge(scattered[k], 64 * (GRAPHS // 8))


def experts(nc, b1, b2, w1, w2, ident, count_rows, half_counts, slots, outputs_at, rows_dram, expert_drams, sums,
            GRAPHS, EXPERTS, D, HID, CAP, FIRST_TILES, TILES):
    KB, HB = D // P, HID // P
    UNROLL = 8
    L_XT, L_F1, L_HT, L_F2, L_STORE = 3, 4, 5, 6, 7
    GROUP, BITS = UNROLL, 3
    GROUPS = TILES // GROUP + 2
    ENTRIES = GROUPS * GROUP
    assert EXPERTS <= 2 ** BITS and GROUP * BITS <= 24 and L_F2 <= GROUP
    SPARE = 2 * EXPERTS
    LAST_ROW = EXPERTS * CAP + (SPARE - 1) * P
    FIRST = FIRST_TILES + GROUP
    HEAD_STEPS = -(-L_STORE // UNROLL) * UNROLL
    assert TILES % UNROLL == 0 and FIRST_TILES % UNROLL == 0
    with ExitStack() as ctx:
        def sb(name, shape, dt=F32):
            return ctx.enter_context(nc.sbuf_tensor(name, shape, dt))

        def pb(name, shape):
            return ctx.enter_context(nc.psum_tensor(name, shape, F32))

        def sem(name):
            return ctx.enter_context(nc.semaphore(name))

        b1_all = sb("b1_all", [P, EXPERTS, HID])
        b2_all = sb("b2_all", [P, EXPERTS, D])
        zeros = sb("zeros", [P, D])
        tile_i = sb("tile_i", [1, ENTRIES], I32)
        tile_f = sb("tile_f", [1, ENTRIES])
        past = sb("past", [1, ENTRIES])
        tile_expert_f = sb("tile_expert_f", [1, ENTRIES])
        tile_row_f = sb("tile_row_f", [1, ENTRIES])
        place_value = sb("place_value", [1, GROUPS, GROUP])
        packed_f = sb("packed_f", [1, GROUPS])
        tile_experts = sb("tile_experts", [1, GROUPS], I32)
        tile_row = sb("tile_row", [1, ENTRIES], I32)
        padded_counts = sb("padded_counts", [P, 3, EXPERTS])
        count_i = sb("count_i", [P, 3, EXPERTS], I32)
        tiles_end = sb("tiles_end", [P, 2, EXPERTS])
        tiles_start = sb("tiles_start", [P, EXPERTS + 1])
        tiles_of = sb("tiles_of", [P, 2, EXPERTS])
        gap = sb("gap", [P, 2, EXPERTS])
        skipped = sb("skipped", [P, 1])
        closer = sb("closer", list(slots.shape))
        moved_slots = sb("moved_slots", list(slots.shape))
        tiles_upto = sb("tiles_upto", [1, 2, EXPERTS])
        pad_row = sb("pad_row", [1, EXPERTS], I32)
        rows = sb("rows", [P, 4, D])
        xT = [sb(f"rowsT{h}", [P, 2, KB, P], F32R) for h in (HIGH, LOW)]
        biased = sb("biased", [P, 2, HID])
        hidden = sb("hidden", [P, 2, HID])
        hT = [sb(f"hT{h}", [P, 2, HB, P], F32R) for h in (HIGH, LOW)]
        y = sb("y", [P, 4, D])
        ps_xT = pb("ps_xT", [P, 2, 512])
        ps_h = pb("ps_h", [P, 2, 512])
        ps_hT = pb("ps_hT", [P, 2, 512])
        ps_y = pb("ps_y", [P, 2, 512])

        bias_loaded, padded, pad_done, gap_done = sem("bias_loaded"), sem("padded"), sem("pad_done"), sem("gap_done")
        rows_loaded = [sem(f"rows_loaded{k}") for k in range(4)]
        y_stored = [sem(f"y_stored{k}") for k in range(4)]
        (tile_iota, zeros_done, moved, table_step, table_done, xT_mm, xT_high, xT_low, h_mm, h_biased, gelu_done,
         hT_mm, hT_high, hT_low, y_mm, y_done) = (sem("e_" + n) for n in (
             "tile_iota zeros_done moved table_step table_done xT_mm xT_high xT_low h_mm h_biased gelu_done "
             "hT_mm hT_high hT_low y_mm y_done").split())

        STORES_SECOND = FIRST_TILES // UNROLL
        SUMS_FROM = STORES_SECOND + 1
        SUMS_TO = SUMS_FROM + first_graphs(GRAPHS) // UNROLL
        TURNS = TILES // UNROLL
        assert L_STORE < UNROLL and SUMS_TO <= TURNS

        def run(eng, step):
            always = lambda lag: True

            def alone(turn):
                for u in range(UNROLL):
                    t = turn * UNROLL + u
                    step(turn, u, lambda lag: lag <= t < lag + TILES, int(t - L_STORE >= FIRST_TILES))

            def turns_from(first, end, half):
                with eng.Fori(first, end) as base:
                    for u in range(UNROLL):
                        step(base, u, always, half, first == SUMS_FROM + 1)

            alone(0)
            turns_from(1, STORES_SECOND, 0)
            alone(STORES_SECOND)
            for u in range(UNROLL):
                step(SUMS_FROM, u, always, 1, True)
            turns_from(SUMS_FROM + 1, SUMS_TO, 1)
            for turn in range(SUMS_TO, TURNS + 1):
                alone(turn)

        def sum_turn(base, u):
            turn = base - SUMS_FROM
            return turn * UNROLL + u, turn * (UNROLL // sums.RING) + u // sums.RING, u % sums.RING

        def tile(base, u, lag):
            return base * UNROLL + (u - lag)

        def turns(base, u, lag, ring):
            return base * (UNROLL // ring) + ((u - lag) // ring + 1)

        def old(base, u, lag, back):
            return not isinstance(base, int) or tile(base, u, lag) >= back

        block = ctx.enter_context(nc.Block())

        @block.gpsimd
        def _(pool):
            pool.iota(tile_i[:], pattern=[[1, ENTRIES]], base=-GROUP, channel_multiplier=0).then_inc(tile_iota, 1)
            pool.memset(zeros[:], 0.0).then_inc(zeros_done, 1)
            pool.wait_ge(gap_done, 1)
            H = first_graphs(GRAPHS)
            halves = (slice(0, H), slice(H, GRAPHS))
            pool.tensor_scalar(moved_slots[:, :, halves[0]], slots[:, :, halves[0]], 0.0, None, ALU.add).then_inc(moved, 1)
            pool.tensor_scalar(moved_slots[:, :, halves[1]], slots[:, :, halves[1]], skipped[:, 0:1], None,
                               ALU.subtract).then_inc(moved, 1)
            for e in range(1, EXPERTS):
                if e > 1:
                    pool.wait_ge(moved, 4 * e - 2)
                for half, graphs in enumerate(halves):
                    pool.tensor_scalar(closer[:, :, graphs], slots[:, :, graphs], float(e * CAP),
                                       gap[:, half, e - 1:e], ALU.is_ge, ALU.mult).then_inc(moved, 1)
                pool.wait_ge(moved, 4 * e)
                for half, graphs in enumerate(halves):
                    pool.tensor_tensor(moved_slots[:, :, graphs], moved_slots[:, :, graphs], closer[:, :, graphs],
                                       ALU.subtract).then_inc(moved, 1)
            pool.wait_ge(moved, 4 * EXPERTS - 2)
            pool.tensor_copy(outputs_at[:], moved_slots[:]).then_inc(moved, 1)
            pool.wait_ge(moved, 4 * EXPERTS - 1)
            for k in range(4):
                pool.wait_ge(y_stored[k], 16 * (FIRST_TILES // 4))

            for i in range(2 * sums.RING):
                sums.gather(pool, i, i, expert_drams[0], i >= sums.RING)
            with pool.Fori(1, H // (2 * sums.RING)) as turn:
                for k in range(2 * sums.RING):
                    sums.gather(pool, turn * (2 * sums.RING) + k, k, expert_drams[0], True)

        @block.sync
        def _(sp):
            sp.wait_ge(zeros_done, 1)
            for n in range(SPARE):
                at = EXPERTS * CAP + n * P
                sp.dma_start(rows_dram[at:at + P, :], zeros[:]).then_inc(padded, 16)
            sp.wait_ge(pad_done, 1)
            fill = nc.values_load_multi_w_load_instructions(
                pad_row[0:1, :], engines=[mybir.EngineType.SP], min_val=0, max_val=EXPERTS * CAP - P)[1]
            for e in range(EXPERTS):
                sp.dma_start(rows_dram[bass.ds(fill[e], P), :], zeros[:]).then_inc(padded, 16)
            sp.wait_ge(table_done, 1)
            sp.wait_ge(padded, 16 * (SPARE + EXPERTS))

            def step(base, u, live, half, summing=False):
                if u == 0:
                    starts[:] = nc.values_load_multi_w_load_instructions(
                        tile_row[0:1, bass.ds(base * UNROLL + GROUP, UNROLL)], engines=[mybir.EngineType.SP],
                        min_val=0, max_val=LAST_ROW)[1]
                if live(L_STORE):
                    j, k = tile(base, u, L_STORE), (u - L_STORE) % 4
                    sp.wait_ge(y_done, j + 1)
                    sp.dma_start(expert_drams[half][bass.ds((j - half * FIRST_TILES) * P, P), :],
                                 y[:, k, :]).then_inc(y_stored[k], 16)
                if live(0):
                    j, k = tile(base, u, 0), u % 4
                    if old(base, u, 0, 4):
                        sp.wait_ge(xT_mm, j - 3)
                    sp.dma_start(rows[:, k, :], rows_dram[bass.ds(starts[u], P), :]).then_inc(rows_loaded[k], 16)
                if summing:
                    g, turn, k = sum_turn(base, u)
                    if isinstance(base, int) and g == 0:
                        for first in range(sums.AHEAD):
                            sums.load(sp, first, first, False)
                    sums.move(sp, g, k, isinstance(base, int))

            starts = []
            run(sp, step)
            for k in range(4):
                sp.wait_ge(y_stored[k], 16 * (TILES // 4))

        def load_experts(engine, base):
            packed = nc.values_load_multi_w_load_instructions(
                tile_experts[0:1, bass.ds(base, 2)], engines=[engine], min_val=0,
                max_val=2 ** (GROUP * BITS) - 1)[1]
            return [number // 2 ** (BITS * n) % 2 ** BITS for number in packed for n in range(GROUP)]

        @block.tensor
        def _(pe):
            def step(base, u, live, half, summing=False):
                if u == 0:
                    experts_of[:] = load_experts(mybir.EngineType.PE, base)
                if live(L_F1):
                    j, buf = tile(base, u, L_F1), (u - L_F1) % 2
                    e = experts_of[GROUP + u - L_F1]
                    pe.wait_ge(xT_low, j + 1)
                    if old(base, u, L_F1, 2):
                        pe.wait_ge(h_biased, j - 1)
                    for n, (kb, (a, b)) in enumerate((kb, ab) for kb in range(KB) for ab in PASSES):
                        mm = pe.matmul(ps_h[:, buf, 0:HID], xT[a][:, buf, kb, :],
                                       w1[:, b, bass.ds(e, 1), kb * HID:(kb + 1) * HID],
                                       start=n == 0, stop=n == 3 * KB - 1)
                    mm.then_inc(h_mm, 1)
                if live(L_XT):
                    j, buf, k = tile(base, u, L_XT), (u - L_XT) % 2, (u - L_XT) % 4
                    pe.wait_ge(rows_loaded[k], 16 * turns(base, u, L_XT, 4))
                    if old(base, u, L_XT, 2):
                        pe.wait_ge(xT_low, j - 1)
                    for kb in range(KB):
                        mm = pe.transpose(ps_xT[:, buf, kb * P:(kb + 1) * P], rows[:, k, kb * P:(kb + 1) * P],
                                          ident[:])
                    mm.then_inc(xT_mm, 1)
                if live(L_HT):
                    j, buf = tile(base, u, L_HT), (u - L_HT) % 2
                    pe.wait_ge(gelu_done, j + 1)
                    if old(base, u, L_HT, 2):
                        pe.wait_ge(hT_low, j - 1)
                    for hb in range(HB):
                        mm = pe.transpose(ps_hT[:, buf, hb * P:(hb + 1) * P], hidden[:, buf, hb * P:(hb + 1) * P],
                                          ident[:])
                    mm.then_inc(hT_mm, 1)
                if live(L_F2):
                    j, buf = tile(base, u, L_F2), (u - L_F2) % 2
                    e = experts_of[GROUP + u - L_F2]
                    pe.wait_ge(hT_low, j + 1)
                    if old(base, u, L_F2, 2):
                        pe.wait_ge(y_done, j - 1)
                    for n, (hb, (a, b)) in enumerate((hb, ab) for hb in range(HB) for ab in PASSES):
                        mm = pe.matmul(ps_y[:, buf, 0:D], hT[a][:, buf, hb, :],
                                       w2[:, b, bass.ds(e, 1), hb * D:(hb + 1) * D],
                                       start=n == 0, stop=n == 3 * HB - 1)
                    mm.then_inc(y_mm, 1)

            experts_of = []
            pe.wait_ge(table_done, 1)
            run(pe, step)

        @block.scalar
        def _(act):
            def step(base, u, live, half, summing=False):
                if live(L_XT):
                    j, buf = tile(base, u, L_XT), (u - L_XT) % 2
                    if old(base, u, L_XT, 2):
                        act.wait_ge(h_mm, j - 1)
                    act.wait_ge(xT_mm, j + 1)
                    act.activation(xT[HIGH][:, buf], ps_xT[:, buf, 0:KB * P].rearrange("p (k n) -> p k n", k=KB),
                                   ACT.Copy).then_inc(xT_high, 1)
                if live(L_HT):
                    j, buf = tile(base, u, L_HT), (u - L_HT) % 2
                    if old(base, u, L_HT, 2):
                        act.wait_ge(y_mm, j - 1)
                    act.wait_ge(hT_mm, j + 1)
                    act.activation(hT[HIGH][:, buf], ps_hT[:, buf, 0:HID].rearrange("p (k n) -> p k n", k=HB),
                                   ACT.Copy).then_inc(hT_high, 1)
                if live(L_F1):
                    j, buf = tile(base, u, L_F1), (u - L_F1) % 2
                    if old(base, u, L_F1, 2):
                        act.wait_ge(hT_mm, j - 1)
                    act.wait_ge(h_biased, j + 1)
                    act.activation(hidden[:, buf, :], biased[:, buf, :], ACT.Gelu).then_inc(gelu_done, 1)

            act.dma_start(b1_all[:], b1.partition_broadcast(P)).then_inc(bias_loaded, 16)
            act.dma_start(b2_all[:], b2.partition_broadcast(P)).then_inc(bias_loaded, 16)
            sums.exp_of_gates(act)
            run(act, step)

        @block.vector
        def _(dve):
            n = [0]

            def then(*instructions):
                for instruction in instructions:
                    instruction.then_inc(table_step, 1)
                n[0] += len(instructions)
                dve.wait_ge(table_step, n[0])

            then(dve.tensor_copy(pad_row[:], count_rows[0:1, :]),
                 dve.tensor_scalar(padded_counts[:, 0:2, :], half_counts[:], float(P - 1), None, ALU.add),
                 dve.tensor_copy(padded_counts[:, 2, :], half_counts[:, 0, :]),
                 dve.memset(tiles_start[:], 0.0),
                 dve.memset(tile_expert_f[:], 0.0),
                 *[dve.memset(place_value[:, :, g:g + 1], float(2 ** (BITS * g))) for g in range(GROUP)])
            dve.sem_inc(pad_done, 1)
            then(dve.tensor_copy(count_i[:], padded_counts[:]))
            then(dve.tensor_scalar(count_i[:], count_i[:], 7, None, ALU.logical_shift_right))
            then(dve.tensor_copy(tiles_end[:], count_i[:, 0:2, :]),
                 dve.tensor_copy(tiles_start[:, 0:EXPERTS], count_i[:, 2, :]))
            then(dve.tensor_copy(tiles_of[:, 0, :], tiles_end[:, 0, :]),
                 dve.tensor_tensor(tiles_of[:, 1, :], tiles_end[:, 1, :], tiles_start[:, 0:EXPERTS], ALU.subtract),
                 dve.tensor_copy(gap[:, 0, :], tiles_end[:, 0, :]),
                 dve.tensor_tensor(gap[:, 1, :], tiles_end[:, 1, :], tiles_start[:, 1:EXPERTS + 1], ALU.subtract),
                 dve.tensor_scalar(skipped[:], tiles_start[:, 0:1], float(P), None, ALU.mult))
            then(dve.tensor_scalar(gap[:], gap[:], -float(P), float(CAP), ALU.mult, ALU.add),
                 dve.tensor_copy(tiles_upto[:, 0, 0:1], tiles_of[0:1, 0, 0:1]),
                 dve.tensor_scalar(tiles_upto[:, 1, 0:1], tiles_of[0:1, 1, 0:1], float(FIRST_TILES), None, ALU.add))
            dve.sem_inc(gap_done, 1)
            for e in range(1, EXPERTS):
                then(dve.tensor_tensor(tiles_upto[:, :, e:e + 1], tiles_upto[:, :, e - 1:e], tiles_of[0:1, :, e:e + 1],
                                       ALU.add))
            dve.wait_ge(tile_iota, 1)
            then(dve.tensor_copy(tile_f[:], tile_i[:]))
            parts = (slice(0, FIRST), slice(FIRST, ENTRIES))
            then(dve.tensor_scalar(tile_row_f[:, parts[0]], tile_f[:, parts[0]], float(P), None, ALU.mult),
                 dve.tensor_scalar(tile_row_f[:, parts[1]], tile_f[:, parts[1]], -float(FIRST_TILES), float(P),
                                   ALU.add, ALU.mult))
            then(dve.tensor_scalar(tile_row_f[:, parts[1]], tile_row_f[:, parts[1]], skipped[0:1, 0:1], None, ALU.add))
            for e in range(EXPERTS):
                then(*[dve.tensor_scalar(past[:, part], tile_f[:, part], tiles_upto[:, half, e:e + 1],
                                         gap[0:1, half, e:e + 1], ALU.is_ge, ALU.mult)
                       for half, part in enumerate(parts)],
                     *[dve.scalar_tensor_tensor(out=tile_expert_f[:, part], in0=tile_f[:, part],
                                                scalar=tiles_upto[:, half, e:e + 1], in1=tile_expert_f[:, part],
                                                op0=ALU.is_ge, op1=ALU.add)
                       for half, part in enumerate(parts)])
                then(dve.tensor_tensor(tile_row_f[:], tile_row_f[:], past[:], ALU.add))
            then(dve.tensor_scalar(tile_row_f[:], tile_row_f[:], 0.0, float(LAST_ROW), ALU.max, ALU.min),
                 dve.tensor_scalar(tile_expert_f[:], tile_expert_f[:], float(EXPERTS - 1), None, ALU.min))
            then(dve.tensor_copy(tile_row[:], tile_row_f[:]),
                 dve.tensor_tensor(place_value[:], place_value[:],
                                   tile_expert_f[:].rearrange("o (g n) -> o g n", n=GROUP), ALU.mult))
            then(dve.tensor_reduce(packed_f[:], place_value[:], AX.X, ALU.add))
            dve.tensor_copy(tile_experts[:], packed_f[:]).then_inc(table_done, 1)
            sums.make_gates(dve)
            dve.wait_ge(table_done, 1)
            dve.wait_ge(bias_loaded, 32)

            def step(base, u, live, half, summing=False):
                if u == 0:
                    experts_of[:] = load_experts(mybir.EngineType.DVE, base)
                if live(L_F1):
                    j, buf = tile(base, u, L_F1), (u - L_F1) % 2
                    e = experts_of[GROUP + u - L_F1]
                    if old(base, u, L_F1, 2):
                        dve.wait_ge(gelu_done, j - 1)
                    dve.wait_ge(h_mm, j + 1)
                    dve.tensor_tensor(biased[:, buf, :].unsqueeze(1), ps_h[:, buf, 0:HID].unsqueeze(1),
                                      b1_all[:, bass.ds(e, 1), :], ALU.add).then_inc(h_biased, 1)
                if live(L_XT):
                    j, buf = tile(base, u, L_XT), (u - L_XT) % 2
                    dve.wait_ge(xT_high, j + 1)
                    dve.tensor_tensor(xT[LOW][:, buf], ps_xT[:, buf, 0:KB * P].rearrange("p (k n) -> p k n", k=KB),
                                      xT[HIGH][:, buf], ALU.subtract).then_inc(xT_low, 1)
                if live(L_HT):
                    j, buf = tile(base, u, L_HT), (u - L_HT) % 2
                    dve.wait_ge(hT_high, j + 1)
                    dve.tensor_tensor(hT[LOW][:, buf], ps_hT[:, buf, 0:HID].rearrange("p (k n) -> p k n", k=HB),
                                      hT[HIGH][:, buf], ALU.subtract).then_inc(hT_low, 1)
                if summing:
                    g, turn, slot = sum_turn(base, u)
                    sums.add_first(dve, g, turn, slot, not isinstance(base, int) or u >= sums.RING)
                if live(L_F2):
                    j, buf, k = tile(base, u, L_F2), (u - L_F2) % 2, (u - L_F2) % 4
                    e = experts_of[GROUP + u - L_F2]
                    if old(base, u, L_F2, 4):
                        dve.wait_ge(y_stored[k], 16 * (turns(base, u, L_F2, 4) - 1))
                    dve.wait_ge(y_mm, j + 1)
                    dve.tensor_tensor(y[:, k, :].unsqueeze(1), ps_y[:, buf, 0:D].unsqueeze(1),
                                      b2_all[:, bass.ds(e, 1), :], ALU.add).then_inc(y_done, 1)
                if summing:
                    sums.add_second(dve, g, slot)

            experts_of = []
            run(dve, step)


class Sums:

    RING = 4
    AHEAD = RING - 1

    def __init__(self, nc, ctx, top_scores, outputs_at, x1_dram, out_rows, D, GRAPHS):
        def sb(name, shape, dt=F32):
            return ctx.enter_context(nc.sbuf_tensor(name, shape, dt))

        def sem(name):
            return ctx.enter_context(nc.semaphore(name))

        self.top_scores, self.outputs_at, self.x1_dram, self.out_rows = top_scores, outputs_at, x1_dram, out_rows
        ring = self.RING
        self.gates = sb("gates", [P, TOP_K, GRAPHS])
        self.gate_sum = sb("gate_sum", [P, GRAPHS])
        self.index = sb("index", [P, 2, ring, TOP_K], I32)
        self.x1 = sb("c_x1", [P, ring, D])
        self.y = sb("c_y", [P, ring, TOP_K, D])
        self.part = sb("part", [P, ring, D])
        self.total = sb("total", [P, ring, D])
        self.x1_loaded = [sem(f"c_x1_loaded{k}") for k in range(ring)]
        self.y_gathered = [sem(f"c_y_gathered{k}") for k in range(ring)]
        self.out_stored = [sem(f"out_stored{k}") for k in range(ring)]
        (self.gate_step, self.gate_exp, self.gates_done, self.index_done, self.part_done, self.total_done,
         self.held) = (sem("c_" + n) for n in (
             "gate_step gate_exp gates_done index_done part_done total_done held").split())

    def load(self, sp, i, k, again):
        if again:
            sp.wait_ge(self.part_done, i - (self.RING - 1))
        sp.dma_start(self.x1[:, k, :], self.x1_dram[bass.ds(i * P, P), :]).then_inc(self.x1_loaded[k], 16)

    def store(self, sp, i, k):
        sp.wait_ge(self.total_done, i + 1)
        sp.dma_start(self.out_rows[bass.ds(i * P, P), :], self.total[:, k, :]).then_inc(self.out_stored[k], 16)

    def move(self, sp, i, k, begins=False):
        if not (begins and i == 0):
            self.store(sp, i - 1, (k - 1) % self.RING)
        self.load(sp, i + self.AHEAD, (k + self.AHEAD) % self.RING, not (begins and i == 0))

    def gather(self, pool, i, n, expert_dram, again):
        ring, half, k = self.RING, n // self.RING, n % self.RING
        if again:
            pool.wait_ge(self.total_done, i - (ring - 1))
            pool.sem_inc(self.held, 1)
        if k == 0:
            pool.tensor_copy(self.index[:, half], self.outputs_at[:, :, bass.ds(i, ring)].rearrange(
                "p c g -> p g c")).then_inc(self.index_done, 1)
            pool.wait_ge(self.index_done, i // ring + 1)
            pool.sem_inc(self.held, 1)
        for c in range(TOP_K):
            pool.indirect_dma_start(self.y[:, k, c, :], None, expert_dram,
                                    bass.IndirectOffsetOnAxis(self.index[:, half, k, c:c + 1], axis=0)).then_inc(
                                        self.y_gathered[k], 16)

    def exp_of_gates(self, act):
        act.wait_ge(self.gate_step, 1)
        act.activation(self.gates[:, 1, :], self.gate_sum[:], ACT.Exp).then_inc(self.gate_exp, 1)

    def make_gates(self, dve):
        gates, gate_sum, top_scores = self.gates, self.gate_sum, self.top_scores
        dve.tensor_tensor(gate_sum[:], top_scores[:, 1, :], top_scores[:, 0, :], ALU.subtract).then_inc(self.gate_step, 1)
        dve.wait_ge(self.gate_exp, 1)
        dve.tensor_scalar(gate_sum[:], gates[:, 1, :], 1.0, None, ALU.add).then_inc(self.gate_step, 1)
        dve.wait_ge(self.gate_step, 2)
        dve.reciprocal(gates[:, 0, :], gate_sum[:]).then_inc(self.gate_step, 1)
        dve.wait_ge(self.gate_step, 3)
        dve.tensor_tensor(gates[:, 1, :], gates[:, 1, :], gates[:, 0, :], ALU.mult).then_inc(self.gates_done, 1)
        dve.wait_ge(self.gates_done, 1)

    def add(self, dve, i, turn, k, again):
        self.add_first(dve, i, turn, k, again)
        self.add_second(dve, i, k)

    def add_first(self, dve, i, turn, k, again):
        if again:
            dve.wait_ge(self.out_stored[k], turn * 16)
        dve.wait_ge(self.x1_loaded[k], turn * 16 + 16)
        dve.wait_ge(self.y_gathered[k], turn * 32 + 32)
        dve.scalar_tensor_tensor(out=self.part[:, k, :], in0=self.y[:, k, 0, :], scalar=self.gates[:, 0, bass.ds(i, 1)],
                                 in1=self.x1[:, k, :], op0=ALU.mult, op1=ALU.add).then_inc(self.part_done, 1)

    def add_second(self, dve, i, k):
        dve.wait_ge(self.part_done, i + 1)
        dve.scalar_tensor_tensor(out=self.total[:, k, :], in0=self.y[:, k, 1, :],
                                 scalar=self.gates[:, 1, bass.ds(i, 1)], in1=self.part[:, k, :], op0=ALU.mult,
                                 op1=ALU.add).then_inc(self.total_done, 1)


def last_sums(nc, sums, expert_dram, GRAPHS):
    RING = sums.RING
    FIRST, TURNS = first_graphs(GRAPHS) // RING, GRAPHS // RING
    with nc.Block() as block:
        @block.sync
        def _(sp):
            with sp.Fori(FIRST, TURNS - 1) as turn:
                for k in range(RING):
                    sums.move(sp, turn * RING + k, k)
            sums.move(sp, GRAPHS - RING, 0)
            for i in range(GRAPHS - RING, GRAPHS):
                sums.store(sp, i, i % RING)
            for k in range(RING):
                sp.wait_ge(sums.out_stored[k], 16 * TURNS)

        @block.gpsimd
        def _(pool):
            with pool.Fori(FIRST // 2, TURNS // 2) as turn:
                for k in range(2 * RING):
                    sums.gather(pool, turn * (2 * RING) + k, k, expert_dram, True)

        @block.vector
        def _(dve):
            with dve.Fori(FIRST, TURNS) as turn:
                for k in range(RING):
                    sums.add(dve, turn * RING + k, turn, k, True)


_INS = ["x", "adj", "L0_gnn_Wq", "L0_gnn_bq", "L0_gnn_Wk", "L0_gnn_bk", "L0_gnn_Wv", "L0_gnn_bv", "L0_gnn_Wo",
        "L0_gnn_bo", "L0_ffn_Wg", "L0_ffn_bg", "L0_ffn_W1", "L0_ffn_b1", "L0_ffn_W2", "L0_ffn_b2"]


def kernel(**inputs):
    import numpy as _np
    import concourse.bacc as _bacc
    from concourse.bass_utils import run_bass_kernel_spmd as _run

    nc = _bacc.Bacc("TRN2", target_bir_lowering=False, num_devices=1)
    arrays, args = {}, []
    for name in _INS:
        a = _np.ascontiguousarray(inputs[name])
        arrays[f"in_{name}"] = a
        args.append(nc.dram_tensor(f"in_{name}", a.shape, mybir.dt.from_np(a.dtype), kind="ExternalInput").ap())
    graphs, n, d = inputs["x"].shape
    n_experts = inputs["L0_ffn_W1"].shape[0]
    table = n_experts * (graphs * n + P) + 2 * n_experts * P
    args.append(nc.dram_tensor("out_x", (graphs, n, d), F32, kind="ExternalOutput").ap())
    args.append(nc.dram_tensor("x1_dram", (graphs * n, d), F32, kind="Internal").ap())
    args.append(nc.dram_tensor("rows_dram", (table, d), F32, kind="Internal").ap())
    first_tiles, tiles = tile_counts(graphs, n_experts)
    for half, count in enumerate((first_tiles, tiles - first_tiles)):
        args.append(nc.dram_tensor(f"expert_dram{half}", (count * P, d), F32, kind="Internal").ap())
    build(nc, *args)
    r = _run(nc, [arrays], core_ids=[0])
    return r.results[0]["out_x"]
```
